# Optimizing a Trainium2 kernel written in Bass

```python
import numpy as np
import jax
import jax.numpy as jnp

def _softmax(x, axis=-1):
    return jax.nn.softmax(x, axis=axis)

def _gelu(x):
    return jax.nn.gelu(x, approximate=True)

def _silu(x):
    return jax.nn.silu(x)

def _sigmoid(x):
    return jax.nn.sigmoid(x)

def _layernorm(x, axis=-1, eps=1e-05):
    m = jnp.mean(x, axis=axis, keepdims=True)
    v = jnp.var(x, axis=axis, keepdims=True)
    return (x - m) / jnp.sqrt(v + eps)

def _scatter_add(tgt, idx, src, axis=0):
    return tgt.at[idx].add(src)

def _segment_sum(src, seg, n):
    return jax.ops.segment_sum(src, seg, n)
kernel_name = 'mk_pixart_seq_d2_seqx_r2_0ed7fa'

def setup_inputs(seed: int=0):
    np.random.seed(seed)
    _w = jnp.asarray

    def _rec_inputs():
        import jax
        import jax.numpy as jnp
        _rk = jax.random.key(seed)
        x = -0.0002928 + 1 * jax.random.normal(jax.random.fold_in(_rk, 1), (8, 224, 512), jnp.float32)
        _lenS = 224 - jax.random.randint(jax.random.fold_in(_rk, 7), (8,), 0, max(1, 224 // 4) + 1, jnp.int32)
        _lenS2 = 750 - jax.random.randint(jax.random.fold_in(_rk, 8), (8,), 0, max(1, 750 // 4) + 1, jnp.int32)
        cond_1024 = 0.000887014 + 1.03683 * jax.random.normal(jax.random.fold_in(_rk, 11), (8, 512), jnp.float32)
        _ctx_1024P = jax.random.normal(jax.random.fold_in(_rk, 12), (8, 16, 512), jnp.float32)
        _ctx_1024c = jax.random.dirichlet(jax.random.fold_in(_rk, 512), 0.3 * jnp.ones((16,), jnp.float32), (8, 750))
        _ctx_1024t = jnp.einsum('bsk,bkd->bsd', _ctx_1024c, _ctx_1024P)
        _ctx_1024t = _ctx_1024t * jax.lax.rsqrt(jnp.mean(jnp.square(_ctx_1024t)) + 1e-12) * 0.953939
        ctx_1024 = 0.00086875 + 0.999764 * (_ctx_1024t + 0.3 * jax.random.normal(jax.random.fold_in(_rk, 612), (8, 750, 512), jnp.float32))
        return (x, cond_1024, ctx_1024)
    x, cond_1024, ctx_1024 = _rec_inputs()

    def _L0_xcond_setup():
        import jax, jax.numpy as jnp
        import numpy as np
        import math
        D_MODEL = 512
        N_HEADS = 16
        HEAD_DIM = D_MODEL // N_HEADS
        D_FF = 2048
        EPS = 1e-05
        ROPE_BASE = 10000.0

        def _rope(t):
            L, Dh = (t.shape[1], t.shape[-1])
            half = Dh // 2
            inv_freq = 1.0 / ROPE_BASE ** (jnp.arange(half, dtype=t.dtype) / half)
            ang = jnp.arange(L, dtype=t.dtype)[:, None] * inv_freq[None, :]
            cos = jnp.cos(ang)[None, :, None, :]
            sin = jnp.sin(ang)[None, :, None, :]
            t1, t2 = (t[..., :half], t[..., half:])
            return jnp.concatenate([t1 * cos - t2 * sin, t2 * cos + t1 * sin], axis=-1)

        def _adaln(x, emb, w, b):
            e = emb[:, 0, :]
            gb = e @ w.T + b
            gamma, beta = jnp.split(gb, 2, axis=-1)
            mu = x.mean(-1, keepdims=True)
            var = x.var(-1, keepdims=True)
            xn = (x - mu) * jax.lax.rsqrt(var + EPS)
            return xn * (1.0 + gamma[:, None, :]) + beta[:, None, :]

        def _attn(q, k, v):
            scale = 1.0 / math.sqrt(HEAD_DIM)
            scores = jnp.einsum('bqhd,bkhd->bhqk', q, k) * scale
            w = jax.nn.softmax(scores, axis=-1)
            out = jnp.einsum('bhqk,bkhd->bqhd', w, v)
            B, Lq = (out.shape[0], out.shape[1])
            return out.reshape(B, Lq, D_MODEL)
        key = jax.random.key(seed)
        ks = jax.random.split(key, 24)
        s = 0.02
        inp = {'x': jax.random.normal(ks[0], (2, 1024, D_MODEL), jnp.float32), 'noise_emb': jax.random.normal(ks[1], (2, 1, D_MODEL), jnp.float32), 'context': jax.random.normal(ks[2], (2, 512, D_MODEL), jnp.float32), 'ln1_w': jax.random.normal(ks[3], (2 * D_MODEL, D_MODEL), jnp.float32) * s, 'ln1_b': jax.random.normal(ks[4], (2 * D_MODEL,), jnp.float32) * s, 'ln2_w': jax.random.normal(ks[5], (2 * D_MODEL, D_MODEL), jnp.float32) * s, 'ln2_b': jax.random.normal(ks[6], (2 * D_MODEL,), jnp.float32) * s, 'ln3_w': jax.random.normal(ks[7], (2 * D_MODEL, D_MODEL), jnp.float32) * s, 'ln3_b': jax.random.normal(ks[8], (2 * D_MODEL,), jnp.float32) * s, 'qkv_w': jax.random.normal(ks[9], (3 * D_MODEL, D_MODEL), jnp.float32) * s, 'sa_out_w': jax.random.normal(ks[10], (D_MODEL, D_MODEL), jnp.float32) * s, 'q_w': jax.random.normal(ks[11], (D_MODEL, D_MODEL), jnp.float32) * s, 'k_w': jax.random.normal(ks[12], (D_MODEL, D_MODEL), jnp.float32) * s, 'v_w': jax.random.normal(ks[13], (D_MODEL, D_MODEL), jnp.float32) * s, 'ca_out_w': jax.random.normal(ks[14], (D_MODEL, D_MODEL), jnp.float32) * s, 'ffn_w1': jax.random.normal(ks[15], (D_FF, D_MODEL), jnp.float32) * s, 'ffn_b1': jax.random.normal(ks[16], (D_FF,), jnp.float32) * s, 'ffn_w2': jax.random.normal(ks[17], (D_MODEL, D_FF), jnp.float32) * s, 'ffn_b2': jax.random.normal(ks[18], (D_MODEL,), jnp.float32) * s}
        return inp
    _L0_xcond_all = _L0_xcond_setup()
    _L0_xcond_in = {k: v for k, v in _L0_xcond_all.items() if k in ('ln1_w', 'ln1_b', 'ln2_w', 'ln2_b', 'ln3_w', 'ln3_b', 'qkv_w', 'sa_out_w', 'q_w', 'k_w', 'v_w', 'ca_out_w', 'ffn_w1', 'ffn_b1', 'ffn_w2', 'ffn_b2')}
    del _L0_xcond_all

    def _L1_xcond_setup():
        import jax, jax.numpy as jnp
        import numpy as np
        LN_EPS = 1e-06

        def _ln(x):
            mu = jnp.mean(x, axis=-1, keepdims=True)
            var = jnp.var(x, axis=-1, keepdims=True)
            return (x - mu) * jax.lax.rsqrt(var + LN_EPS)
        key = jax.random.key(seed)
        H, NH = (512, 16)
        B, N, S = (4, 512, 77)
        MLP = int(H * 4.0)
        ks = jax.random.split(key, 20)
        s = 1.0 / np.sqrt(H)
        return {'x': jax.random.normal(ks[0], (B, N, H), jnp.float32), 'c': jax.random.normal(ks[1], (B, H), jnp.float32), 'context': jax.random.normal(ks[2], (B, S, H), jnp.float32), 'W_mod': jax.random.normal(ks[3], (H, 6 * H), jnp.float32) * s, 'b_mod': jnp.zeros((6 * H,), jnp.float32), 'W_qkv': jax.random.normal(ks[4], (H, 3 * H), jnp.float32) * s, 'b_qkv': jnp.zeros((3 * H,), jnp.float32), 'W_proj': jax.random.normal(ks[5], (H, H), jnp.float32) * s, 'b_proj': jnp.zeros((H,), jnp.float32), 'W_qc': jax.random.normal(ks[6], (H, H), jnp.float32) * s, 'b_qc': jnp.zeros((H,), jnp.float32), 'W_kvc': jax.random.normal(ks[7], (H, 2 * H), jnp.float32) * s, 'b_kvc': jnp.zeros((2 * H,), jnp.float32), 'W_cproj': jax.random.normal(ks[8], (H, H), jnp.float32) * s, 'b_cproj': jnp.zeros((H,), jnp.float32), 'W_mlp1': jax.random.normal(ks[9], (H, MLP), jnp.float32) * s, 'b_mlp1': jnp.zeros((MLP,), jnp.float32), 'W_mlp2': jax.random.normal(ks[10], (MLP, H), jnp.float32) * (1.0 / np.sqrt(MLP)), 'b_mlp2': jnp.zeros((H,), jnp.float32)}
    _L1_xcond_all = _L1_xcond_setup()
    _L1_xcond_in = {k: v for k, v in _L1_xcond_all.items() if k in ('W_mod', 'b_mod', 'W_qkv', 'b_qkv', 'W_proj', 'b_proj', 'W_qc', 'b_qc', 'W_kvc', 'b_kvc', 'W_cproj', 'b_cproj', 'W_mlp1', 'b_mlp1', 'W_mlp2', 'b_mlp2')}
    del _L1_xcond_all
    return {'x': x, 'cond_1024': cond_1024, 'ctx_1024': ctx_1024, 'L0_xcond_ln1_w': _L0_xcond_in['ln1_w'], 'L0_xcond_ln1_b': _L0_xcond_in['ln1_b'], 'L0_xcond_ln2_w': _L0_xcond_in['ln2_w'], 'L0_xcond_ln2_b': _L0_xcond_in['ln2_b'], 'L0_xcond_ln3_w': _L0_xcond_in['ln3_w'], 'L0_xcond_ln3_b': _L0_xcond_in['ln3_b'], 'L0_xcond_qkv_w': _L0_xcond_in['qkv_w'], 'L0_xcond_sa_out_w': _L0_xcond_in['sa_out_w'], 'L0_xcond_q_w': _L0_xcond_in['q_w'], 'L0_xcond_k_w': _L0_xcond_in['k_w'], 'L0_xcond_v_w': _L0_xcond_in['v_w'], 'L0_xcond_ca_out_w': _L0_xcond_in['ca_out_w'], 'L0_xcond_ffn_w1': _L0_xcond_in['ffn_w1'], 'L0_xcond_ffn_b1': _L0_xcond_in['ffn_b1'], 'L0_xcond_ffn_w2': _L0_xcond_in['ffn_w2'], 'L0_xcond_ffn_b2': _L0_xcond_in['ffn_b2'], 'L1_xcond_W_mod': _L1_xcond_in['W_mod'], 'L1_xcond_b_mod': _L1_xcond_in['b_mod'], 'L1_xcond_W_qkv': _L1_xcond_in['W_qkv'], 'L1_xcond_b_qkv': _L1_xcond_in['b_qkv'], 'L1_xcond_W_proj': _L1_xcond_in['W_proj'], 'L1_xcond_b_proj': _L1_xcond_in['b_proj'], 'L1_xcond_W_qc': _L1_xcond_in['W_qc'], 'L1_xcond_b_qc': _L1_xcond_in['b_qc'], 'L1_xcond_W_kvc': _L1_xcond_in['W_kvc'], 'L1_xcond_b_kvc': _L1_xcond_in['b_kvc'], 'L1_xcond_W_cproj': _L1_xcond_in['W_cproj'], 'L1_xcond_b_cproj': _L1_xcond_in['b_cproj'], 'L1_xcond_W_mlp1': _L1_xcond_in['W_mlp1'], 'L1_xcond_b_mlp1': _L1_xcond_in['b_mlp1'], 'L1_xcond_W_mlp2': _L1_xcond_in['W_mlp2'], 'L1_xcond_b_mlp2': _L1_xcond_in['b_mlp2']}

def reference(x, cond_1024, ctx_1024, L0_xcond_ln1_w, L0_xcond_ln1_b, L0_xcond_ln2_w, L0_xcond_ln2_b, L0_xcond_ln3_w, L0_xcond_ln3_b, L0_xcond_qkv_w, L0_xcond_sa_out_w, L0_xcond_q_w, L0_xcond_k_w, L0_xcond_v_w, L0_xcond_ca_out_w, L0_xcond_ffn_w1, L0_xcond_ffn_b1, L0_xcond_ffn_w2, L0_xcond_ffn_b2, L1_xcond_W_mod, L1_xcond_b_mod, L1_xcond_W_qkv, L1_xcond_b_qkv, L1_xcond_W_proj, L1_xcond_b_proj, L1_xcond_W_qc, L1_xcond_b_qc, L1_xcond_W_kvc, L1_xcond_b_kvc, L1_xcond_W_cproj, L1_xcond_b_cproj, L1_xcond_W_mlp1, L1_xcond_b_mlp1, L1_xcond_W_mlp2, L1_xcond_b_mlp2):
    import jax
    import jax.numpy as jnp

    def _L0_xcond_ref(x, noise_emb, context, ln1_w, ln1_b, ln2_w, ln2_b, ln3_w, ln3_b, qkv_w, sa_out_w, q_w, k_w, v_w, ca_out_w, ffn_w1, ffn_b1, ffn_w2, ffn_b2):
        import jax, jax.numpy as jnp
        import numpy as np
        import math
        D_MODEL = 512
        N_HEADS = 16
        HEAD_DIM = D_MODEL // N_HEADS
        D_FF = 2048
        EPS = 1e-05
        ROPE_BASE = 10000.0

        def _rope(t):
            L, Dh = (t.shape[1], t.shape[-1])
            half = Dh // 2
            inv_freq = 1.0 / ROPE_BASE ** (jnp.arange(half, dtype=t.dtype) / half)
            ang = jnp.arange(L, dtype=t.dtype)[:, None] * inv_freq[None, :]
            cos = jnp.cos(ang)[None, :, None, :]
            sin = jnp.sin(ang)[None, :, None, :]
            t1, t2 = (t[..., :half], t[..., half:])
            return jnp.concatenate([t1 * cos - t2 * sin, t2 * cos + t1 * sin], axis=-1)

        def _adaln(x, emb, w, b):
            e = emb[:, 0, :]
            gb = e @ w.T + b
            gamma, beta = jnp.split(gb, 2, axis=-1)
            mu = x.mean(-1, keepdims=True)
            var = x.var(-1, keepdims=True)
            xn = (x - mu) * jax.lax.rsqrt(var + EPS)
            return xn * (1.0 + gamma[:, None, :]) + beta[:, None, :]

        def _attn(q, k, v):
            scale = 1.0 / math.sqrt(HEAD_DIM)
            scores = jnp.einsum('bqhd,bkhd->bhqk', q, k) * scale
            w = jax.nn.softmax(scores, axis=-1)
            out = jnp.einsum('bhqk,bkhd->bqhd', w, v)
            B, Lq = (out.shape[0], out.shape[1])
            return out.reshape(B, Lq, D_MODEL)
        B, L, D = x.shape
        L_ctx = context.shape[1]
        res = x
        xn = _adaln(x, noise_emb, ln1_w, ln1_b)
        qkv = xn @ qkv_w.T
        q, k, v = jnp.split(qkv, 3, axis=-1)
        q = _rope(q.reshape(B, L, N_HEADS, HEAD_DIM))
        k = _rope(k.reshape(B, L, N_HEADS, HEAD_DIM))
        v = v.reshape(B, L, N_HEADS, HEAD_DIM)
        sa = _attn(q, k, v) @ sa_out_w.T
        x = res + sa
        res = x
        xn = _adaln(x, noise_emb, ln2_w, ln2_b)
        q = _rope((xn @ q_w.T).reshape(B, L, N_HEADS, HEAD_DIM))
        k = _rope((context @ k_w.T).reshape(B, L_ctx, N_HEADS, HEAD_DIM))
        v = (context @ v_w.T).reshape(B, L_ctx, N_HEADS, HEAD_DIM)
        ca = _attn(q, k, v) @ ca_out_w.T
        x = res + ca
        res = x
        xn = _adaln(x, noise_emb, ln3_w, ln3_b)
        h = jax.nn.gelu(xn @ ffn_w1.T + ffn_b1, approximate=False)
        x = res + (h @ ffn_w2.T + ffn_b2)
        return x

    def _L1_xcond_ref(x, c, context, W_mod, b_mod, W_qkv, b_qkv, W_proj, b_proj, W_qc, b_qc, W_kvc, b_kvc, W_cproj, b_cproj, W_mlp1, b_mlp1, W_mlp2, b_mlp2):
        import jax, jax.numpy as jnp
        import numpy as np
        LN_EPS = 1e-06

        def _ln(x):
            mu = jnp.mean(x, axis=-1, keepdims=True)
            var = jnp.var(x, axis=-1, keepdims=True)
            return (x - mu) * jax.lax.rsqrt(var + LN_EPS)
        B, N, H = x.shape
        NH = 16
        hd = H // NH
        scale = hd ** (-0.5)
        c_proj = jax.nn.silu(c) @ W_mod + b_mod
        shift_a, scale_a, gate_a, shift_m, scale_m, gate_m = jnp.split(c_proj, 6, axis=-1)

        def modulate(t, shift, sc):
            return t * (1 + sc[:, None]) + shift[:, None]
        x_norm = modulate(_ln(x), shift_a, scale_a)
        qkv = x_norm @ W_qkv + b_qkv
        q, k, v = jnp.split(qkv, 3, axis=-1)
        q = q.reshape(B, N, NH, hd).transpose(0, 2, 1, 3)
        k = k.reshape(B, N, NH, hd).transpose(0, 2, 1, 3)
        v = v.reshape(B, N, NH, hd).transpose(0, 2, 1, 3)
        attn_w = jax.nn.softmax(jnp.einsum('bhqd,bhkd->bhqk', q, k) * scale, axis=-1)
        attn_out = jnp.einsum('bhqk,bhkd->bhqd', attn_w, v)
        attn_out = attn_out.transpose(0, 2, 1, 3).reshape(B, N, H)
        attn_out = attn_out @ W_proj + b_proj
        x = x + gate_a[:, None] * attn_out
        S = context.shape[1]
        q_c = _ln(x) @ W_qc + b_qc
        kv_c = _ln(context) @ W_kvc + b_kvc
        k_c, v_c = jnp.split(kv_c, 2, axis=-1)
        q_c = q_c.reshape(B, N, NH, hd).transpose(0, 2, 1, 3)
        k_c = k_c.reshape(B, S, NH, hd).transpose(0, 2, 1, 3)
        v_c = v_c.reshape(B, S, NH, hd).transpose(0, 2, 1, 3)
        c_attn_w = jax.nn.softmax(jnp.einsum('bhqd,bhsd->bhqs', q_c, k_c) * scale, axis=-1)
        c_attn_out = jnp.einsum('bhqs,bhsd->bhqd', c_attn_w, v_c)
        c_attn_out = c_attn_out.transpose(0, 2, 1, 3).reshape(B, N, H)
        c_attn_out = c_attn_out @ W_cproj + b_cproj
        x = x + c_attn_out
        x_norm2 = modulate(_ln(x), shift_m, scale_m)
        h = jax.nn.gelu(x_norm2 @ W_mlp1 + b_mlp1)
        h = h @ W_mlp2 + b_mlp2
        x = x + gate_m[:, None] * h
        return x
    x = _L0_xcond_ref(x, cond_1024[:, None, :], ctx_1024, L0_xcond_ln1_w, L0_xcond_ln1_b, L0_xcond_ln2_w, L0_xcond_ln2_b, L0_xcond_ln3_w, L0_xcond_ln3_b, L0_xcond_qkv_w, L0_xcond_sa_out_w, L0_xcond_q_w, L0_xcond_k_w, L0_xcond_v_w, L0_xcond_ca_out_w, L0_xcond_ffn_w1, L0_xcond_ffn_b1, L0_xcond_ffn_w2, L0_xcond_ffn_b2)
    x = _L1_xcond_ref(x, cond_1024, ctx_1024, L1_xcond_W_mod, L1_xcond_b_mod, L1_xcond_W_qkv, L1_xcond_b_qkv, L1_xcond_W_proj, L1_xcond_b_proj, L1_xcond_W_qc, L1_xcond_b_qc, L1_xcond_W_kvc, L1_xcond_b_kvc, L1_xcond_W_cproj, L1_xcond_b_cproj, L1_xcond_W_mlp1, L1_xcond_b_mlp1, L1_xcond_W_mlp2, L1_xcond_b_mlp2)
    return x

_drawn_inputs = setup_inputs


def setup_inputs(seed=0):
    import zlib

    import numpy as np

    out = dict(_drawn_inputs(seed))
    spreads = {'L1_xcond_b_mod': (0.0, 0.1),
     'L1_xcond_b_qkv': (0.0, 0.1),
     'L1_xcond_b_proj': (0.0, 0.1),
     'L1_xcond_b_qc': (0.0, 0.549),
     'L1_xcond_b_kvc': (0.0, 0.1),
     'L1_xcond_b_cproj': (0.0, 0.1),
     'L1_xcond_b_mlp1': (0.0, 0.1),
     'L1_xcond_b_mlp2': (0.0, 0.1)}
    factors = {'L0_xcond_ln1_b': 8.0,
     'L0_xcond_ln2_w': 8.0,
     'L0_xcond_ln2_b': 8.0,
     'L0_xcond_ln3_b': 8.0,
     'L0_xcond_q_w': 7.449,
     'L0_xcond_k_w': 8.0,
     'L0_xcond_ffn_b1': 5.716,
     'L0_xcond_ffn_b2': 3.043}
    for name, (base, spread) in spreads.items():
        noise = np.random.default_rng([zlib.crc32(name.encode()), seed]).standard_normal(out[name].shape)
        drawn = base * np.exp(spread * noise) if base else spread * noise
        out[name] = jnp.asarray(drawn.astype(out[name].dtype))
    for name, factor in factors.items():
        out[name] = (out[name] * factor).astype(out[name].dtype)
    return out
```

```python
from contextlib import ExitStack

import numpy as np

import concourse.bass as bass
from concourse import mybir

F32 = mybir.dt.float32
F32R = mybir.dt.float32r
BF16 = mybir.dt.bfloat16
ALU = mybir.AluOpType
ACT = mybir.ActivationFunctionType
AX = mybir.AxisListType

B, N, D = 8, 224, 512
NC = 750
H, HD = 16, 32
FF = 2048
P = 128
KT = D // P
TT, TP = 2, 112
HG = P // HD
NG = H // HG
SCALE = HD ** -0.5
STACK = 3 * HD
STACKM = STACK + 2
CHUNK = 1024
SWAP = [(i + HD // 2) % HD for i in range(HD)]
CREDIT = 16


class Tally:

    def __init__(self, sem):
        self.sem, self.base, self.per = sem, CREDIT, 0

    def at(self, rnd, n):
        return rnd * self.per + (self.base + n)


class Signals:

    def __init__(self, nc, ctx):
        def new(name):
            self.all[name] = Tally(ctx.enter_context(nc.semaphore(name)))
            return self.all[name]

        self.all = {}
        self.const = new("const")
        self.c_in = new("c_in")
        self.c_silu = new("c_silu")
        self.m_raw0 = new("m_raw0")
        self.m_raw1 = new("m_raw1")
        self.tr_full = new("tr_full")
        self.tr_free = new("tr_free")
        self.mod_rows = new("mod_rows")
        self.gates_out = new("gates_out")
        self.w_raw0 = new("w_raw0")
        self.w_raw1 = new("w_raw1")
        self.w_hi = new("w_hi")
        self.w_lo = new("w_lo")
        self.x_in = new("x_in")
        self.res_in = new("res_in")
        self.ctx_in = new("ctx_in")
        self.gate_in = new("gate_in")
        self.k_in0 = new("k_in0")
        self.k_in1 = new("k_in1")
        self.q_in0 = new("q_in0")
        self.q_in1 = new("q_in1")
        self.x_out = new("x_out")
        self.two_waits = new("two_waits")
        self.stats = new("stats")
        self.ln_var = new("ln_var")
        self.rstd = new("rstd")
        self.xn_ready = new("xn_ready")
        self.cstats = new("cstats")
        self.cvar = new("cvar")
        self.crstd = new("crstd")
        self.cn_ready = new("cn_ready")
        self.wk_full = new("wk_full")
        self.wk_free = new("wk_free")
        self.xm_ready = new("xm_ready")
        self.xm_hi = new("xm_hi")
        self.xm_lo = new("xm_lo")
        self.cx_hi = new("cx_hi")
        self.f_cos = new("f_cos")
        self.f_sin = new("f_sin")
        self.f_flat = new("f_flat")
        self.f_hi = new("f_hi")
        self.f_lo = new("f_lo")
        self.max_full = new("max_full")
        self.max_free = new("max_free")
        self.m_rows = new("m_rows")
        self.m_top = new("m_top")
        self.m_ready = new("m_ready")
        self.shift_full = new("shift_full")
        self.shift_free = new("shift_free")
        self.s_full = new("s_full")
        self.s_free = new("s_free")
        self.av_done = new("av_done")
        self.e_sum = new("e_sum")
        self.sum_done = new("sum_done")
        self.a_rec = new("a_rec")
        self.a_flat = new("a_flat")
        self.a_hi = new("a_hi")
        self.a_lo = new("a_lo")
        self.up_full = new("up_full")
        self.g_flat = new("g_flat")
        self.g_hi = new("g_hi")
        self.g_lo = new("g_lo")
        self.down_done = new("down_done")
        self.y_full = new("y_full")
        self.y_mid = new("y_mid")
        self.y_gate = new("y_gate")
        self.y_ready = new("y_ready")

    def plan(self, **per):
        for tally in self.all.values():
            tally.per = 0
        for name, n in per.items():
            self.all[name].per = n

    def close(self, once, rounds):
        for name, tally in self.all.items():
            tally.base += tally.per * (1 if name in once else rounds)
            tally.per = 0


ONCE = ("w_raw0", "w_raw1", "w_hi", "w_lo", "c_in", "const")


def f32(ap):
    return ap.bitcast(F32)


def three_passes(pe, out, w_hi, w_lo, x_hi, x_lo, first, last):
    pe.matmul(out, w_hi, x_hi, start=first, stop=False)
    pe.matmul(out, w_hi, x_lo, start=False, stop=False)
    return pe.matmul(out, w_lo, x_hi, start=False, stop=last)



def weight_chunks(w, hi, lo):
    rows, cols = w.shape
    wv = w.rearrange("(k p) n -> p k n", p=P)
    step = next(c for c in (CHUNK, 768, 512) if cols % c == 0)
    return [(wv[:, k, c:c + step], hi[:, k, c:c + step], lo[:, k, c:c + step])
            for k in range(rows // P) for c in range(0, cols, step)]


def weights_sync(sp, s, chunks, stage):
    for i, (raw, _, _) in enumerate(chunks):
        if i >= 2:
            sp.wait_ge(s.w_lo.sem, s.w_lo.at(0, i - 1))
        sp.dma_start(stage[:, i % 2, 0:raw.shape[1]], raw).then_inc((s.w_raw0, s.w_raw1)[i % 2].sem, 16)


def weights_scalar(act, s, chunks, stage):
    for i, (raw, hi, _) in enumerate(chunks):
        act.wait_ge((s.w_raw0, s.w_raw1)[i % 2].sem, (s.w_raw0, s.w_raw1)[i % 2].at(0, 16 * (i // 2 + 1)))
        act.activation(hi, stage[:, i % 2, 0:raw.shape[1]], ACT.Copy).then_inc(s.w_hi.sem, 1)


def weights_vector(dve, s, chunks, stage):
    for i, (raw, hi, lo) in enumerate(chunks):
        dve.wait_ge(s.w_hi.sem, s.w_hi.at(0, i + 1))
        dve.tensor_tensor(lo, stage[:, i % 2, 0:raw.shape[1]], f32(hi), ALU.subtract).then_inc(s.w_lo.sem, 1)


def weights_plan(chunks):
    n = len(chunks)
    return dict(w_raw0=16 * ((n + 1) // 2), w_raw1=16 * (n // 2), w_hi=n, w_lo=n)



def modulation(nc, s, t, io):
    chunks = []
    for w in (io["ln1_w"], io["ln2_w"], io["ln3_w"], io["W_mod"]):
        wv = w.rearrange("(k p) n -> p k n", p=P)
        chunks += [wv[:, :, c:c + D] for c in range(0, w.shape[1], D)]
    NV = len(chunks)
    with ExitStack() as ctx:
        def sb(name, shape, dt=F32):
            return ctx.enter_context(nc.sbuf_tensor(name, shape, dt))
        raw = sb("mod_raw", [P, 2, KT, D])
        cond = sb("cond", [P, 2, KT, B])
        rows = sb("mod_rows_sb", [B, NV, D])
        bias = sb("mod_bias", [B, NV, D])
        ps_rows = ctx.enter_context(nc.psum_tensor("ps_rows", [B, 2, D], F32))
        ps_vec = ctx.enter_context(nc.psum_tensor("ps_vec", [P, NV, KT, B], F32))
        s.plan(m_raw0=16 * NV // 2, m_raw1=16 * NV // 2, c_in=32 + 16 * 4, tr_full=NV, tr_free=NV, mod_rows=1,
             const=CONSTS, c_silu=1, gates_out=32)
        block = ctx.enter_context(nc.Block())

        @block.sync
        def _(sp):
            sp.dma_start(cond[:, 0], io["condT"].rearrange("(k p) b -> p k b", p=P)).then_inc(s.c_in.sem, 16)
            sp.dma_start(cond[:, 1], io["condT"].rearrange("(k p) b -> p k b", p=P)).then_inc(s.c_in.sem, 16)
            at = 0
            for name in ("ln1_b", "ln2_b", "ln3_b", "b_mod"):
                n = io[name].shape[0] // D
                sp.dma_start(bias[:, at:at + n, :].rearrange("p a d -> p (a d)"),
                             io[name].partition_broadcast(B)).then_inc(s.c_in.sem, 16)
                at += n
            for i, w in enumerate(chunks):
                if i >= 2:
                    sp.wait_ge(s.tr_full.sem, s.tr_full.at(0, i - 1))
                sp.dma_start(raw[:, i % 2], w).then_inc((s.m_raw0, s.m_raw1)[i % 2].sem, 16)
            sp.wait_ge(s.tr_free.sem, s.tr_free.at(0, NV))
            for g, v in enumerate((8, 11)):
                sp.dma_start(io["gates"][g], rows[:, v, :]).then_inc(s.gates_out.sem, 8 * 2)
            sp.wait_ge(s.gates_out.sem, s.gates_out.at(0, 32))

        @block.scalar
        def _(act):
            act.wait_ge(s.c_in.sem, s.c_in.at(0, 96))
            act.activation(cond[:, 1], cond[:, 1], ACT.Silu).then_inc(s.c_silu.sem, 1)

        @block.tensor
        def _(pe):
            pe.wait_ge(s.c_in.sem, s.c_in.at(0, 96))
            pe.wait_ge(s.c_silu.sem, s.c_silu.at(0, 1))
            for i in range(NV):
                pe.wait_ge((s.m_raw0, s.m_raw1)[i % 2].sem, (s.m_raw0, s.m_raw1)[i % 2].at(0, 16 * (i // 2 + 1)))
                if i >= 2:
                    pe.wait_ge(s.tr_free.sem, s.tr_free.at(0, i - 1))
                for k in range(KT):
                    mm = pe.matmul(ps_rows[:, i % 2, :], cond[:, int(i >= 6), k, :], raw[:, i % 2, k, :],
                                   start=(k == 0), stop=(k == KT - 1))
                mm.then_inc(s.tr_full.sem, 1)
            pe.wait_ge(s.tr_free.sem, s.tr_free.at(0, NV))
            pe.wait_ge(s.const.sem, s.const.at(0, CONSTS))
            for v in range(NV):
                for k in range(KT):
                    mm = pe.transpose(ps_vec[:, v, k, :], rows[:, v, k * P:(k + 1) * P], t.ident[0:B, 0:B])
            mm.then_inc(s.mod_rows.sem, 1)

        @block.vector
        def _(dve):
            dve.wait_ge(s.c_in.sem, s.c_in.at(0, 96))
            for i in range(NV):
                dve.wait_ge(s.tr_full.sem, s.tr_full.at(0, i + 1))
                dve.tensor_tensor(rows[:, i, :], ps_rows[:, i % 2, :], bias[:, i, :], ALU.add).then_inc(s.tr_free.sem, 1)
            dve.wait_ge(s.mod_rows.sem, s.mod_rows.at(0, 1))
            for ln, sc, sh in ((0, 0, 1), (1, 2, 3), (2, 4, 5), (3, 7, 6), (5, 10, 9)):
                dve.tensor_scalar(t.mod[:, ln, 0], ps_vec[:, sc], 1.0, None, ALU.add)
                dve.tensor_copy(t.mod[:, ln, 1], ps_vec[:, sh])
            dve.memset(t.mod[:, 4, 0], 1.0)
            dve.memset(t.mod[:, 4, 1], 0.0)
            dve.drain()

        @block.gpsimd
        def _(pool):
            constants(pool, s, t)
    s.close((), 1)


CONSTS = 8


def constants(pool, s, t):
    pool.memset(t.ident[:], 0.0).then_inc(s.const.sem, 1)
    pool.wait_ge(s.const.sem, s.const.at(0, 1))
    pool.affine_select(out=t.ident[:], in_=t.ident[:], compare_op=ALU.not_equal, fill=1.0, base=0,
                       pattern=[[-1, P]], channel_multiplier=1).then_inc(s.const.sem, 1)
    pool.memset(t.ones[:], 1.0).then_inc(s.const.sem, 1)
    pool.memset(t.neghalf[:], -0.5).then_inc(s.const.sem, 1)
    pool.memset(t.eps[:, 0], 1e-5).then_inc(s.const.sem, 1)
    pool.memset(t.eps[:, 1], 1e-6).then_inc(s.const.sem, 1)
    pool.wait_ge(s.const.sem, s.const.at(0, 6))
    pool.tensor_copy(t.ident_bf[:], t.ident[:]).then_inc(s.const.sem, 1)
    pool.wait_ge(s.const.sem, s.const.at(0, 7))
    pool.memset(t.pad[:], 0.0).then_inc(s.const.sem, 1)



def ln_vector_stats(dve, s, rnd, x, st, mv, tiles, pad, stats, var):
    for i in range(tiles):
        dve.bn_stats(st[:, i, :], x[:, i, :]).then_inc(stats.sem, 1)
    dve.wait_ge(stats.sem, stats.at(rnd, tiles))
    dve.tensor_copy(pad[:, 0:1], pad[:, 1:2])
    for i in range(tiles):
        dve.bn_aggr(mv[:, i, :], st[:, i, :]).then_inc(var.sem, 1)


def ln_pool_rstd(pool, s, rnd, mv, rs, eps, nh, tiles, var, rstd):
    pool.wait_ge(var.sem, var.at(rnd, tiles))
    pool.wait_ge(rstd.sem, rstd.at(rnd, 0))
    pool.tensor_tensor(rs[:, 0, :], mv[:, :, 1], eps, ALU.add).then_inc(rstd.sem, 1)
    pool.wait_ge(rstd.sem, rstd.at(rnd, 1))
    pool.tensor_tensor(rs[:, 1, :], rs[:, 0, :], nh, ALU.pow).then_inc(rstd.sem, 1)


def ln_vector_apply(dve, s, rnd, x, mv, rs, tiles, rstd, ready):
    dve.wait_ge(rstd.sem, rstd.at(rnd, 2))
    for i in range(tiles):
        dve.tensor_scalar(x[:, i, :], x[:, i, :], mv[:, i, 0:1], rs[:, 1, i:i + 1],
                          ALU.subtract, ALU.mult).then_inc(ready.sem, 1)



class Attention:

    def __init__(self, cross, layer):
        self.cross, self.layer = cross, layer
        self.keys = NC if cross else N
        self.kp = 125 if cross else TP
        self.tiles = self.keys // self.kp
        self.pairs = self.tiles // 2
        self.kcols = [(0, 376), (376, 750)] if cross else [(0, N)]
        self.fu = len(self.kcols) + 1
        self.mu = HG * (4 if cross else 1)
        self.gs = 1 if cross else 2
        self.fills = NG // self.gs // 2
        self.rope = layer == 0
        order = [("ctx", i) for i in range(8 if cross else 0)] + [("x", i) for i in range(2)]
        groups = [0, 1] if cross else [0, 1, 2, 3]
        f = [("f", g, u) for g in groups for u in range(self.fu)]
        v = [("v", i) for i in range(self.tiles)]
        cut = self.gs * self.fu

        def fh(fs):
            out = list(fs[:1])
            for w, after in zip(fs, fs[1:] + [None]):
                out += ([after] if after else []) + [("h", *w[1:])]
            return out

        if cross:
            m = [("m", 0, u) for u in range(self.mu)]
            self.front = order + fh(f[:3]) + v[:3]
            for i in range(3):
                self.front += fh([f[3 + i]]) + [v[3 + i]]
            self.front += m[:8] + [("t", 0, 0)] + m[8:]
        else:
            self.front = order + fh(f[:cut]) + v + fh(f[cut:]) + [("m", 0, u) for u in range(self.mu)] + [("t", 0, 0)]
        self.steps = [self.step(g) for g in range(NG)]
        self.body = self.front + [e for st in self.steps for e in st] + [("y", i) for i in range(TT)]
        self.work = [e for e in self.body if e[0] in ("ctx", "x", "f", "v", "y")]
        self.index = {w: i for i, w in enumerate(self.work)}
        assert len(self.work) % 2 == 0
        self.fn = {w[1:]: i for i, w in enumerate(w for w in self.work if w[0] == "f")}

    def step(self, g):
        more = g + 1 < NG
        m = [("m", g + 1, u) for u in range(self.mu)] if more else []
        s = [[("s", g, c, j) for j in range(HG)] for c in range(self.pairs)]
        e = [("e", g, c) for c in range(self.pairs)]
        v = [("a", g, c) for c in range(self.pairs)]
        o = [("o", g), ("d", g)]
        if not self.cross:
            out = s[0][:2] + [("t", g, 1)] + m[:1] + s[0][2:3] + m[1:2] + s[0][3:] + m[2:3] + e + m[3:] + v
            return out + ([("t", g + 1, 0)] if more else []) + o
        deep = g + 2 < NG
        f = [("f", g + 2, u) for u in range(3)] if deep else [None] * 3
        h = [("h", g + 2, u) for u in range(3)] if deep else [None] * 3
        out = s[0][:2] + [("t", g, 1)] + s[0][2:] + [f[0]] + s[1] + [e[0], v[0], f[1]] + s[2] + [e[1], v[1]]
        out += m[:2] + [h[0]] + m[2:4] + [e[2], v[2], h[1], f[2]] + m[4:7] + [o[0]] + m[7:8]
        if more:
            out += [("t", g + 1, 0)]
        out += m[8:10] + [o[1], h[2]] + m[10:]
        return [x for x in out if x]

    def events(self):
        return self.body


def attention_phase(nc, s, t, io, cross, layer, x_src, x_dst):
    a = Attention(cross, layer)
    ln = 3 * layer + int(cross)
    biased = layer == 1
    pre = "c" if cross else "s"
    with ExitStack() as ctx:
        def sb(name, shape, dt=F32):
            return ctx.enter_context(nc.sbuf_tensor(f"{pre}{layer}_{name}", shape, dt))

        def psum(name, shape):
            return ctx.enter_context(nc.psum_tensor(f"{pre}{layer}_ps_{name}", shape, F32))

        names = dict(k="wk", q="wq", v="wv", o="wo")
        W = {}
        if cross:
            srcs = {n: io[f"{'c' if cross else 's'}{layer}_{n}"] for n in ("wk", "wv", "wq", "wo")}
            for n in srcs:
                W[n] = (sb(n + "_hi", [P, KT, D], F32R), sb(n + "_lo", [P, KT, D], F32R))
            chunks = [c for n in ("wk", "wv", "wq", "wo") for c in weight_chunks(srcs[n], *W[n])]
        else:
            wq = (sb("qkv_hi", [P, KT, 3 * D], F32R), sb("qkv_lo", [P, KT, 3 * D], F32R))
            W["wq"], W["wk"], W["wv"] = [tuple(h[:, :, i * D:(i + 1) * D] for h in wq) for i in range(3)]
            W["wo"] = (sb("wo_hi", [P, KT, D], F32R), sb("wo_lo", [P, KT, D], F32R))
            chunks = weight_chunks(io[f"s{layer}_qkv"], *wq) + weight_chunks(io[f"s{layer}_wo"], *W["wo"])
        craw_all = sb("craw", [P, 6, D]) if cross else None
        stage = craw_all[:, 0:4].rearrange("p (s a) n -> p s (a n)", s=2) if cross else sb("stage", [P, 2, CHUNK])

        xa = sb("xa", [TP, TT, D])
        res = sb("res", [TP, TT, D])
        stt, mv, rs = sb("st", [P, 8, 6]), sb("mv", [P, 8, 2]), sb("rs", [P, 2, 8])
        xm = sb("xm", [P, 2, N])
        xh, xl = sb("xh", [P, KT, N], F32R), sb("xl", [P, KT, N], F32R)
        if cross:
            craw = craw_all[0:125]
            cst, cmv, crs = sb("cst", [125, 6, 6]), sb("cmv", [125, 6, 2]), sb("crs", [125, 2, 6])
            ch, cl = sb("ch", [P, KT, NC], F32R), sb("cl", [P, KT, NC], F32R)
            ksrc = sb("ksrc", [P, 2, NC], F32R)
            qsrc = sb("qsrc", [P, 2, N], F32R)
            kst = sb("kst", [P, 2, HG, NC], F32R)
            qst = sb("qst", [P, 2, HG, N], F32R)
        else:
            src = sb("src", [P, 2, 4, 2, N], F32R)
            st2 = sb("st2", [P, 2, 2, HG, 2, N], F32R)
        kvh, kvl = (ch, cl) if cross else (xh, xl)
        wid = 376 if cross else N
        fa, fs = sb("fa", [P, 2, wid]), sb("fs", [P, 2, wid]) if a.rope else None
        if a.rope:
            cos, sin = sb("cos", [P, a.keys]), sb("sin", [P, a.keys])
        vt = sb("vt", [a.kp, a.tiles, D])
        mx, mhl = sb("mx", [TP, HG, TT]), sb("mhl", [TP, HG, TT, 2], BF16)
        mx2 = sb("mx2", [TP, HG, TT, 2]) if cross else None
        pt = sb("pt", [a.kp, 2, HG, 2, N])
        es = sb("es", [a.kp, HG, N])
        rec, af = sb("rec", [P, N]), sb("af", [P, N])
        ah, al = sb("ah", [P, NG, N], F32R), sb("al", [P, NG, N], F32R)
        if biased:
            ym = sb("ym", [TP, D])
            bq, bk = sb("bq", [P, KT]), sb("bk", [P, KT])
            bv, bo = sb("bv", [P, D]), sb("bo", [P, D])
            gate = sb("gate", [TP, D]) if not cross else None

        wk = psum("wk", [P, 2, 512])
        ps_max = psum("max", [P, 2, 512])
        ps_s = psum("s", [P, 2, 512])
        ps_o = psum("o", [P, 512])
        ps_shift = psum("shift", [P, 512])

        def kstack(g, j, rows, c0, c1):
            if cross:
                return kst[0:rows, g % 2, j, c0:c1]
            return st2[0:rows, g // 2, 0, j, g % 2, c0:c1]

        def qstack(g, j, rows, c0, c1):
            if cross:
                return qst[0:rows, g % 2, j, c0:c1]
            return st2[0:rows, g // 2, 1, j, g % 2, c0:c1]

        def e_count(cs):
            g, c = divmod(cs, a.pairs)
            per = 2 * a.pairs - 1
            return g * per + (2 * c - 1 if c > 0 else 0)

        def sum_pair(eng, b, g, c):
            cs = g * a.pairs + c
            eng.wait_ge(s.s_free.sem, s.s_free.at(b, (cs + 1) * HG))
            tile = [pt[:, cs % 2, :, k, :] for k in range(2)]
            if c == 0:
                eng.wait_ge(s.sum_done.sem, s.sum_done.at(b, g))
                eng.tensor_tensor(es[:], tile[0], tile[1], ALU.add).then_inc(s.e_sum.sem, 1)
            else:
                for k in range(2):
                    eng.wait_ge(s.e_sum.sem, s.e_sum.at(b, e_count(cs) + k))
                    eng.tensor_tensor(es[:], es[:], tile[k], ALU.add).then_inc(s.e_sum.sem, 1)

        def f_width(u):
            return a.kcols[u][1] - a.kcols[u][0] if u < len(a.kcols) else N

        def f_dst(g, u, half):
            isq = u == a.fu - 1
            if not cross:
                return src[:, g // 2, 2 * isq + half, g % 2, :]
            return qsrc[:, half, :] if isq else ksrc[:, half, a.kcols[u][0]:a.kcols[u][1]]

        slots = 2
        dmas = 12
        nchunks = len(chunks)
        nf = NG * a.fu
        gated = biased and not cross
        cn = biased and cross
        s.plan(**weights_plan(chunks), x_in=16, res_in=16, ctx_in=16 * cross, gate_in=16 * gated,
             k_in0=16 * dmas * a.fills, k_in1=16 * dmas * a.fills, q_in0=16 * dmas * a.fills * cross, q_in1=16 * dmas * a.fills * cross, x_out=16,
             wk_full=len(a.work), wk_free=len(a.work), max_full=NG * a.mu, max_free=NG * a.mu,
             s_full=NG * HG * a.pairs, s_free=NG * HG * a.pairs, shift_full=NG * 2, shift_free=NG * 2,
             av_done=NG * a.pairs, sum_done=NG, stats=TT, ln_var=TT, rstd=2, xn_ready=TT,
             cstats=6 * cn, cvar=6 * cn, crstd=2 * cn, cn_ready=6 * cn,
             xm_ready=KT // 2, xm_hi=KT, xm_lo=KT, cx_hi=8 * cross,
             f_cos=nf * a.rope, f_sin=nf * a.rope, f_flat=nf * a.rope, f_hi=nf, f_lo=nf,
             m_top=2 * NG, m_ready=2 * NG, m_rows=2 * NG * cross, e_sum=NG * (2 * a.pairs - 1),
             a_rec=NG, a_flat=NG, a_hi=NG, a_lo=NG, y_mid=TT * biased, y_gate=TT * gated,
             c_in=16 * 6, const=2)
        block = ctx.enter_context(nc.Block())
        xv = x_src.rearrange("b (t p) d -> b p t d", p=TP)
        yv = x_dst.rearrange("b (t p) d -> b p t d", p=TP)

        @block.sync
        def _(sp):
            n = 0
            if a.rope:
                sp.dma_start(cos[:], io["cos"][:, 0:a.keys]).then_inc(s.c_in.sem, 16)
                sp.dma_start(sin[:], io["sin"][:, 0:a.keys]).then_inc(s.c_in.sem, 16)
                n += 2
            if biased:
                for dst, name in ((bq, "bq"), (bk, "bk")):
                    sp.dma_start(dst[:], io[f"{pre}_{name}"]).then_inc(s.c_in.sem, 16)
                for dst, name in ((bv, "bv"), (bo, "bo")):
                    sp.dma_start(dst[:], io[f"{pre}_{name}"].partition_broadcast(P)).then_inc(s.c_in.sem, 16)
                n += 4
            while n < 6:
                sp.dma_start(stt[:, 0, 0:2], io["cos"][:, 0:2]).then_inc(s.c_in.sem, 16)
                n += 1
                sp.wait_ge(s.c_in.sem, s.c_in.at(0, 16 * n))
            weights_sync(sp, s, chunks, stage)
            sp.wait_ge(s.w_lo.sem, s.w_lo.at(0, nchunks))
            with sp.Fori(0, B) as b:
                sp.wait_ge(s.wk_full.sem, s.wk_full.at(b, a.index[("x", 1)] + 1 - len(a.work)))
                sp.dma_start(xa[:], xv[b]).then_inc(s.x_in.sem, 16)
                if cross:
                    sp.wait_ge(s.wk_full.sem, s.wk_full.at(b, a.index[("ctx", 7)] + 1 - len(a.work)))
                    sp.dma_start(craw[:], io["ctx"][b].rearrange("(t p) d -> p t d", p=125)).then_inc(s.ctx_in.sem, 16)
                if gated:
                    sp.wait_ge(s.y_gate.sem, s.y_gate.at(b, 0))
                    sp.dma_start(gate[:], io["gates"][0, b].partition_broadcast(TP)).then_inc(s.gate_in.sem, 16)
                sp.wait_ge(s.x_out.sem, s.x_out.at(b, 0))
                sp.dma_start(res[:], xv[b]).then_inc(s.res_in.sem, 16)
                order = [0, 1, 2, 3] if cross else [0, 1]
                for i in order:
                    if cross:
                        done = s.s_full.at(b, (i - 1) * HG * a.pairs)
                        sp.wait_ge(s.f_lo.sem, s.f_lo.at(b, a.fn[(i, 1)] + 1))
                        sp.sem_inc(s.two_waits.sem, 1)
                        sp.wait_ge(s.s_full.sem, done)
                        sem = (s.k_in0, s.k_in1)[i % 2].sem
                        for j in range(HG):
                            r = slice(HD * j, HD * (j + 1))
                            for row, kh in ((0, 0), (1, 0), (2, 1)):
                                to = slice(HD * row, HD * (row + 1))
                                sp.dma_start(f32(kst[to, i % 2, j, :]), f32(ksrc[r, kh, :])).then_inc(sem, 16)
                        sp.wait_ge(s.f_lo.sem, s.f_lo.at(b, a.fn[(i, 2)] + 1))
                        sem = (s.q_in0, s.q_in1)[i % 2].sem
                        for j in range(HG):
                            r = slice(HD * j, HD * (j + 1))
                            for row, qh in ((0, 0), (1, 1), (2, 0)):
                                to = slice(HD * row, HD * (row + 1))
                                sp.dma_start(f32(qst[to, i % 2, j, :]), f32(qsrc[r, qh, :])).then_inc(sem, 16)
                    else:
                        sp.wait_ge(s.f_lo.sem, s.f_lo.at(b, a.fn[(2 * i + 1, 1)] + 1))
                        sp.sem_inc(s.two_waits.sem, 1)
                        sp.wait_ge(s.s_full.sem, s.s_full.at(b, (2 * i - 2) * HG * a.pairs))
                        sem = (s.k_in0, s.k_in1)[i].sem
                        for j in range(HG):
                            r = slice(HD * j, HD * (j + 1))
                            for row, kind in ((0, slice(0, 4, 2)), (1, slice(0, 4, 3)), (2, slice(1, 3, 1))):
                                to = slice(HD * row, HD * (row + 1))
                                sp.dma_start(f32(st2[to, i, :, j].rearrange("p a g n -> p a (g n)")),
                                             f32(src[r, i, kind].rearrange("p a g n -> p a (g n)"))).then_inc(sem, 16)
                sp.wait_ge(s.wk_free.sem, s.wk_free.at(b, len(a.work)))
                sp.dma_start(yv[b], res[:]).then_inc(s.x_out.sem, 16)
            sp.wait_ge(s.x_out.sem, s.x_out.at(B, 0))

        @block.tensor
        def _(pe):
            pe.wait_ge(s.w_lo.sem, s.w_lo.at(0, nchunks))
            pe.wait_ge(s.const.sem, s.const.at(0, 2))

            def batch(b):
                def bank(w):
                    i = a.index[w]
                    pe.wait_ge(s.wk_free.sem, s.wk_free.at(b, i - 1))
                    return wk[:, i % 2, :]

                def scores(g, c, j):
                    i = (g * a.pairs + c) * HG + j
                    if c == 0 and j in (0, 2):
                        pe.wait_ge(s.shift_free.sem, s.shift_free.at(b, 2 * g + j // 2 + 1))
                    pe.wait_ge(s.s_free.sem, s.s_free.at(b, i - 1))
                    for k in range(2):
                        kt = 2 * c + k
                        mm = pe.matmul(ps_s[0:a.kp, i % 2, k * N:(k + 1) * N],
                                       kstack(g, j, STACKM, kt * a.kp, (kt + 1) * a.kp),
                                       qstack(g, j, STACKM, 0, N), start=True, stop=True)
                    mm.then_inc(s.s_full.sem, 1)

                def values(g, c):
                    i = g * a.pairs + c
                    if c == 0:
                        pe.wait_ge(s.a_flat.sem, s.a_flat.at(b, g))
                    pe.wait_ge(s.s_free.sem, s.s_free.at(b, (i + 1) * HG))
                    for k in range(2):
                        for j in range(HG):
                            kt = 2 * c + k
                            h = g * HG + j
                            mm = pe.matmul(ps_o[HD * j:HD * (j + 1), 0:N], vt[:, kt, HD * h:HD * (h + 1)],
                                           pt[:, i % 2, j, k, :], start=(kt == 0), stop=(kt == a.tiles - 1))
                    mm.then_inc(s.av_done.sem, 1)

                def sums(g):
                    pe.wait_ge(s.e_sum.sem, s.e_sum.at(b, (g + 1) * (2 * a.pairs - 1)))
                    for j in range(HG):
                        mm = pe.matmul(ps_o[HD * j:HD * (j + 1), N:2 * N], t.ones[0:a.kp, 0:HD], es[:, j, :],
                                       start=True, stop=True)
                    mm.then_inc(s.sum_done.sem, 1)

                def maxima(g, u):
                    i = g * a.mu + u
                    slot, fill = (g % 2, g // 2 + 1) if cross else (g // 2, 1)
                    if u == 0:
                        pe.wait_ge((s.k_in0, s.k_in1)[slot].sem, (s.k_in0, s.k_in1)[slot].at(b, 16 * dmas * fill))
                        if cross:
                            pe.wait_ge((s.q_in0, s.q_in1)[slot].sem, (s.q_in0, s.q_in1)[slot].at(b, 16 * dmas * fill))
                    pe.wait_ge(s.max_free.sem, s.max_free.at(b, i - 1))
                    if cross:
                        j, q, c0 = u // 4, u // 2 % 2, (0, NC - 376)[u % 2]
                        mm = pe.matmul(ps_max[0:TP, i % 2, 0:376], qstack(g, j, STACK, q * TP, (q + 1) * TP),
                                       kstack(g, j, STACK, c0, c0 + 376), start=True, stop=True)
                    else:
                        for q in range(TT):
                            mm = pe.matmul(ps_max[0:TP, i % 2, q * N:(q + 1) * N],
                                           qstack(g, u, STACK, q * TP, (q + 1) * TP),
                                           kstack(g, u, STACK, 0, N), start=True, stop=True)
                    mm.then_inc(s.max_full.sem, 1)

                def shifts(g, half):
                    pe.wait_ge(s.m_ready.sem, s.m_ready.at(b, 2 * g + half + 1))
                    pe.wait_ge(s.shift_free.sem, s.shift_free.at(b, 2 * g + half))
                    for j in (2 * half, 2 * half + 1):
                        for q in range(TT):
                            c0 = (j % 2) * N + q * TP
                            mm = pe.matmul(ps_shift[STACK:STACKM, c0:c0 + TP], mhl[:, j, q, :],
                                           t.ident_bf[0:TP, 0:TP], start=True, stop=True)
                    mm.then_inc(s.shift_full.sem, 1)

                for e in a.events():
                    kind = e[0]
                    if kind == "ctx":
                        k, half = e[1] // 2, e[1] % 2
                        if e[1] == 0:
                            pe.wait_ge(s.cn_ready.sem, s.cn_ready.at(b, 6)) if biased else pe.wait_ge(s.ctx_in.sem, s.ctx_in.at(b, 16))
                        to = bank(e)
                        for i in range(3):
                            mm = pe.transpose(to[:, i * 125:(i + 1) * 125], craw[:, 3 * half + i, k * P:(k + 1) * P],
                                              t.ident[0:125, 0:125])
                        mm.then_inc(s.wk_full.sem, 1)
                    elif kind == "x":
                        if e[1] == 0:
                            pe.wait_ge(s.xn_ready.sem, s.xn_ready.at(b, TT))
                        to = bank(e)
                        for k in range(2):
                            for i in range(TT):
                                c0 = k * N + i * TP
                                kk = 2 * e[1] + k
                                mm = pe.transpose(to[:, c0:c0 + TP], xa[:, i, kk * P:(kk + 1) * P],
                                                  t.ident[0:TP, 0:TP])
                        mm.then_inc(s.wk_full.sem, 1)
                    elif kind == "f":
                        _, g, u = e
                        isq = u == a.fu - 1
                        if isq or not cross:
                            pe.wait_ge(s.xm_lo.sem, s.xm_lo.at(b, KT))
                        else:
                            pe.wait_ge(s.wk_free.sem, s.wk_free.at(b, a.index[("ctx", 7)] + 1))
                        wh, wl = W["wq" if isq else "wk"]
                        c0, c1 = (0, N) if isq else a.kcols[u]
                        sh, sl = (xh, xl) if isq else (kvh, kvl)
                        to = bank(e)
                        for k in range(KT):
                            fs_ = slice(g * P, (g + 1) * P)
                            mm = three_passes(pe, to[:, 0:c1 - c0], wh[:, k, fs_], wl[:, k, fs_],
                                              sh[:, k, c0:c1], sl[:, k, c0:c1], k == 0, k == KT - 1)
                        mm.then_inc(s.wk_full.sem, 1)
                    elif kind == "v":
                        i = e[1]
                        pe.wait_ge(s.wk_free.sem, s.wk_free.at(b, a.index[("ctx", 7)] + 1)) if cross else pe.wait_ge(s.xm_lo.sem, s.xm_lo.at(b, KT))
                        wh, wl = W["wv"]
                        to = bank(e)
                        for k in range(KT):
                            c = slice(i * a.kp, (i + 1) * a.kp)
                            mm = three_passes(pe, to[0:a.kp, :], kvh[:, k, c], kvl[:, k, c],
                                              wh[:, k, :], wl[:, k, :], k == 0, k == KT - 1)
                        mm.then_inc(s.wk_full.sem, 1)
                    elif kind == "y":
                        i = e[1]
                        pe.wait_ge(s.a_lo.sem, s.a_lo.at(b, NG))
                        wh, wl = W["wo"]
                        to = bank(e)
                        for k in range(KT):
                            c = slice(i * TP, (i + 1) * TP)
                            mm = three_passes(pe, to[0:TP, :], ah[:, k, c], al[:, k, c],
                                              wh[:, k, :], wl[:, k, :], k == 0, k == KT - 1)
                        mm.then_inc(s.wk_full.sem, 1)
                    elif kind == "s":
                        scores(*e[1:])
                    elif kind == "a":
                        if e[1] == 0 and e[2] == 0:
                            pe.wait_ge(s.wk_free.sem, s.wk_free.at(b, a.index[("v", a.tiles - 1)] + 1))
                        values(e[1], e[2])
                    elif kind == "m":
                        maxima(e[1], e[2])
                    elif kind == "t":
                        shifts(e[1], e[2])
                    elif kind == "o":
                        sums(e[1])

            with pe.Fori(0, B) as b:
                batch(b)

        @block.vector
        def _(dve):
            stack = kst[STACK:STACKM].rearrange("p a h n -> p (a h n)") if cross else \
                st2[STACK:STACKM, :, 0].rearrange("p a h g n -> p a (h g n)")
            dve.memset(f32(stack), -1.0).then_inc(s.const.sem, 2)
            weights_vector(dve, s, chunks, stage)
            dve.wait_ge(s.c_in.sem, s.c_in.at(0, 96))

            def batch(b):
                if cross and biased:
                    dve.wait_ge(s.ctx_in.sem, s.ctx_in.at(b, 16))
                    ln_vector_stats(dve, s, b, craw, cst, cmv, 6, t.pad, s.cstats, s.cvar)
                    ln_vector_apply(dve, s, b, craw, cmv, crs, 6, s.crstd, s.cn_ready)
                dve.wait_ge(s.x_in.sem, s.x_in.at(b, 16))
                ln_vector_stats(dve, s, b, xa, stt[0:TP], mv[0:TP], TT, t.pad, s.stats, s.ln_var)
                ln_vector_apply(dve, s, b, xa, mv[0:TP], rs[0:TP, :, 0:TT], TT, s.rstd, s.xn_ready)
                for e in a.events():
                    kind = e[0]
                    if kind in ("ctx", "x", "f", "v", "y"):
                        i = a.index[e]
                        dve.wait_ge(s.wk_full.sem, s.wk_full.at(b, i + 1))
                        fr = wk[:, i % 2, :]
                    if kind == "ctx":
                        k, half = e[1] // 2, e[1] % 2
                        c = slice(375 * half, 375 * half + 375)
                        dve.wait_ge(s.cx_hi.sem, s.cx_hi.at(b, e[1] + 1))
                        dve.tensor_tensor(cl[:, k, c], fr[:, 0:375], f32(ch[:, k, c]), ALU.subtract).then_inc(s.wk_free.sem, 1)
                    elif kind == "x":
                        for kk in range(2):
                            k = 2 * e[1] + kk
                            dve.wait_ge(s.xm_lo.sem, s.xm_lo.at(b, k - 1))
                            dve.tensor_scalar(xm[:, k % 2, :], fr[:, kk * N:(kk + 1) * N],
                                                   t.mod[:, ln, 0, k, bass.ds(b, 1)], t.mod[:, ln, 1, k, bass.ds(b, 1)],
                                                   ALU.mult, ALU.add).then_inc((s.xm_ready, s.wk_free)[kk].sem, 1)
                    elif kind == "f":
                        _, g, u = e
                        n = a.fn[e[1:]]
                        isq = u == a.fu - 1
                        w = f_width(u)
                        c0 = 0 if isq else a.kcols[u][0]
                        dve.wait_ge(s.f_lo.sem, s.f_lo.at(b, n - 1))
                        if a.rope:
                            dve.tensor_tensor(fa[:, n % 2, 0:w], fr[:, 0:w], cos[:, c0:c0 + w], ALU.mult).then_inc(s.f_cos.sem, 1)
                            dve.stream_shuffle(fs[:, n % 2, 0:w], fr[:, 0:w], SWAP).then_inc(s.wk_free.sem, 1)
                        else:
                            bias = (bq if isq else bk)[:, g:g + 1]
                            dve.tensor_scalar(fa[:, n % 2, 0:w], fr[:, 0:w], bias, None, ALU.add).then_inc(s.wk_free.sem, 1)
                    elif kind == "v":
                        i = e[1]
                        if i == 0:
                            dve.wait_ge(s.av_done.sem, s.av_done.at(b, 0))
                        if biased:
                            op = dve.tensor_tensor(vt[:, i, :], fr[0:a.kp, :], bv[0:a.kp, :], ALU.add)
                        else:
                            op = dve.tensor_copy(vt[:, i, :], fr[0:a.kp, :])
                        op.then_inc(s.wk_free.sem, 1)
                    elif kind == "m":
                        _, g, u = e
                        i = g * a.mu + u
                        dve.wait_ge(s.max_full.sem, s.max_full.at(b, i + 1))
                        half, nth = 2 * u // a.mu, 2 * g + 2 * u // a.mu
                        last = (u + 1) % (a.mu // 2) == 0
                        if cross:
                            dve.tensor_reduce(mx2[:, u // 4, u // 2 % 2, u % 2:u % 2 + 1], ps_max[0:TP, i % 2, 0:376], AX.X,
                                              ALU.max).then_inc(s.max_free.sem, 1)
                        else:
                            dve.tensor_reduce(mx[:, u, :], ps_max[0:TP, i % 2, 0:2 * N].rearrange("p (a n) -> p a n", a=2),
                                              AX.X, ALU.max).then_inc(s.max_free.sem, 1)
                        if last:
                            hs = slice(2 * half, 2 * half + 2)
                            dve.wait_ge(s.max_free.sem, s.max_free.at(b, i + 1))
                            if cross:
                                dve.tensor_tensor(mx[:, hs, :], mx2[:, hs, :, 0], mx2[:, hs, :, 1], ALU.max).then_inc(s.m_rows.sem, 1)
                                dve.wait_ge(s.m_rows.sem, s.m_rows.at(b, nth + 1))
                            dve.wait_ge(s.shift_full.sem, s.shift_full.at(b, nth - 1))
                            dve.tensor_copy(mhl[:, hs, :, 0], mx[:, hs, :]).then_inc(s.m_top.sem, 1)
                            dve.wait_ge(s.m_top.sem, s.m_top.at(b, nth + 1))
                            dve.tensor_tensor(mhl[:, hs, :, 1], mx[:, hs, :], mhl[:, hs, :, 0], ALU.subtract).then_inc(s.m_ready.sem, 1)
                    elif kind == "e" and e[2] in (0, a.pairs - 1):
                        sum_pair(dve, b, e[1], e[2])
                    elif kind == "o":
                        g = e[1]
                        dve.wait_ge(s.sum_done.sem, s.sum_done.at(b, g + 1))
                        dve.wait_ge(s.a_lo.sem, s.a_lo.at(b, g))
                        dve.reciprocal(rec[:], ps_o[:, N:2 * N]).then_inc(s.a_rec.sem, 1)
                        dve.wait_ge(s.a_rec.sem, s.a_rec.at(b, g + 1))
                        dve.tensor_tensor(af[:], ps_o[:, 0:N], rec[:], ALU.mult).then_inc(s.a_flat.sem, 1)
                    elif kind == "y":
                        i = e[1]
                        if i == 0:
                            dve.wait_ge(s.res_in.sem, s.res_in.at(b, 16))
                            if gated:
                                dve.wait_ge(s.gate_in.sem, s.gate_in.at(b, 16))
                        y = fr[0:TP, :]
                        if biased:
                            dve.wait_ge(s.wk_free.sem, s.wk_free.at(b, a.index[e]))
                            dve.tensor_tensor(ym[:], y, bo[0:TP, :], ALU.add).then_inc(s.y_mid.sem, 1)
                            dve.wait_ge(s.y_mid.sem, s.y_mid.at(b, i + 1))
                            y = ym[:]
                            if gated:
                                dve.tensor_tensor(ym[:], ym[:], gate[:], ALU.mult).then_inc(s.y_gate.sem, 1)
                                dve.wait_ge(s.y_gate.sem, s.y_gate.at(b, i + 1))
                        dve.tensor_tensor(res[:, i, :], res[:, i, :], y, ALU.add).then_inc(s.wk_free.sem, 1)

            with dve.Fori(0, B) as b:
                batch(b)

        @block.scalar
        def _(act):
            weights_scalar(act, s, chunks, stage)

            def batch(b):
                for e in a.events():
                    kind = e[0]
                    if kind == "ctx":
                        k, half = e[1] // 2, e[1] % 2
                        i = a.index[e]
                        c = slice(375 * half, 375 * half + 375)
                        act.wait_ge(s.wk_full.sem, s.wk_full.at(b, i + 1))
                        if e[1] == 0:
                            act.wait_ge(s.wk_full.sem, s.wk_full.at(b, a.index[("f", NG - 1, a.fu - 1)] + 1 - len(a.work)))
                        act.activation(ch[:, k, c], wk[:, i % 2, 0:375], ACT.Copy).then_inc(s.cx_hi.sem, 1)
                    elif kind == "x":
                        for kk in range(2):
                            k = 2 * e[1] + kk
                            if kk == 0:
                                act.wait_ge(s.xm_ready.sem, s.xm_ready.at(b, e[1] + 1))
                            else:
                                act.wait_ge(s.wk_free.sem, s.wk_free.at(b, a.index[e] + 1))
                            act.activation(xh[:, k, :], xm[:, k % 2, :], ACT.Copy).then_inc(s.xm_hi.sem, 1)
                    elif kind == "h":
                        _, g, u = e
                        n = a.fn[e[1:]]
                        if cross:
                            if u != 1:
                                prev = g - 1 if g else 3
                                filled = ((s.k_in0, s.k_in1), None, (s.q_in0, s.q_in1))[u][prev % 2]
                                act.wait_ge(filled.sem, filled.at(b, 16 * dmas * (prev // 2 + 1) - (0 if g else 16 * dmas * a.fills)))
                        elif g % 2 == 0 and u == 0:
                            act.wait_ge((s.k_in0, s.k_in1)[g // 2].sem, (s.k_in0, s.k_in1)[g // 2].at(b, 0))
                        act.wait_ge(s.f_flat.sem, s.f_flat.at(b, n + 1)) if a.rope else act.wait_ge(s.wk_free.sem, s.wk_free.at(b, a.index[("f", g, u)] + 1))
                        act.activation(f_dst(g, u, 0), fa[:, n % 2, 0:f_width(u)], ACT.Copy).then_inc(s.f_hi.sem, 1)
                    elif kind == "t":
                        _, g, half = e
                        act.wait_ge(s.shift_full.sem, s.shift_full.at(b, 2 * g + half + 1))
                        q = qst[STACK:STACKM, g % 2, 2 * half:2 * half + 2, :] if cross else \
                            st2[STACK:STACKM, g // 2, 1, 2 * half:2 * half + 2, g % 2, :]
                        act.activation(q, ps_shift[STACK:STACKM, 0:2 * N].rearrange("p (a n) -> p a n", a=2),
                                       ACT.Copy).then_inc(s.shift_free.sem, 1)
                    elif kind == "s":
                        _, g, c, j = e
                        cs = g * a.pairs + c
                        i = cs * HG + j
                        act.wait_ge(s.s_full.sem, s.s_full.at(b, i + 1))
                        if j == 0:
                            act.wait_ge(s.av_done.sem, s.av_done.at(b, cs - 1))
                            act.wait_ge(s.e_sum.sem, s.e_sum.at(b, e_count(cs - 1)))
                        act.activation(pt[:, cs % 2, j, :, :],
                                       ps_s[0:a.kp, i % 2, 0:2 * N].rearrange("p (a n) -> p a n", a=2),
                                       ACT.Exp, scale=SCALE).then_inc(s.s_free.sem, 1)
                    elif kind == "d":
                        g = e[1]
                        act.wait_ge(s.a_flat.sem, s.a_flat.at(b, g + 1))
                        act.activation(ah[:, g, :], af[:], ACT.Copy).then_inc(s.a_hi.sem, 1)

            with act.Fori(0, B) as b:
                batch(b)

        @block.gpsimd
        def _(pool):
            def batch(b):
                if cross and biased:
                    ln_pool_rstd(pool, s, b, cmv, crs, t.eps[0:125, 1, 0:6], t.neghalf[0:125, 0:6], 6, s.cvar, s.crstd)
                ln_pool_rstd(pool, s, b, mv[0:TP, 0:TT], rs[0:TP, :, 0:TT], t.eps[0:TP, layer, 0:TT],
                             t.neghalf[0:TP, 0:TT], TT, s.ln_var, s.rstd)
                for e in a.events():
                    kind = e[0]
                    if kind == "x":
                        for kk in range(2):
                            k = 2 * e[1] + kk
                            pool.wait_ge(s.xm_hi.sem, s.xm_hi.at(b, k + 1))
                            pool.tensor_tensor(xl[:, k, :], xm[:, k % 2, :], f32(xh[:, k, :]), ALU.subtract).then_inc(s.xm_lo.sem, 1)
                    elif kind == "f":
                        _, g, u = e
                        n = a.fn[e[1:]]
                        isq = u == a.fu - 1
                        w = f_width(u)
                        c0 = 0 if isq else a.kcols[u][0]
                        if a.rope:
                            pool.wait_ge(s.wk_free.sem, s.wk_free.at(b, a.index[e] + 1))
                            pool.tensor_tensor(fs[:, n % 2, 0:w], fs[:, n % 2, 0:w], sin[:, c0:c0 + w], ALU.mult).then_inc(s.f_sin.sem, 1)
                            pool.wait_ge(s.f_sin.sem, s.f_sin.at(b, n + 1))
                            pool.tensor_tensor(fa[:, n % 2, 0:w], fa[:, n % 2, 0:w], fs[:, n % 2, 0:w], ALU.add).then_inc(s.f_flat.sem, 1)
                    elif kind == "h":
                        _, g, u = e
                        n = a.fn[e[1:]]
                        pool.wait_ge(s.f_hi.sem, s.f_hi.at(b, n + 1))
                        pool.tensor_tensor(f_dst(g, u, 1), fa[:, n % 2, 0:f_width(u)], f32(f_dst(g, u, 0)), ALU.subtract).then_inc(s.f_lo.sem, 1)
                    elif kind == "e" and e[2] not in (0, a.pairs - 1):
                        sum_pair(pool, b, e[1], e[2])
                    elif kind == "d":
                        g = e[1]
                        pool.wait_ge(s.a_hi.sem, s.a_hi.at(b, g + 1))
                        pool.tensor_tensor(al[:, g, :], af[:], f32(ah[:, g, :]), ALU.subtract).then_inc(s.a_lo.sem, 1)

            with pool.Fori(0, B) as b:
                batch(b)
    s.close(ONCE, B)



def feed_forward(nc, s, t, io, layer, x_src, x_dst):
    ln = 3 * layer + 2
    PB = 2
    T4 = PB * TT
    M = PB * N
    FC = FF // P
    gated = layer == 1
    LAG = 2
    HS = 3
    with ExitStack() as ctx:
        def sb(name, shape, dt=F32):
            return ctx.enter_context(nc.sbuf_tensor(f"f{layer}_{name}", shape, dt))

        w1 = (sb("w1_hi", [P, KT, FF], F32R), sb("w1_lo", [P, KT, FF], F32R))
        w2 = (sb("w2_hi", [P, FC, D], F32R), sb("w2_lo", [P, FC, D], F32R))
        chunks = weight_chunks(io[f"f{layer}_w1"], *w1) + weight_chunks(io[f"f{layer}_w2"], *w2)
        stage = sb("stage", [P, 2, CHUNK])
        xa, res = sb("xa", [TP, T4, D]), sb("res", [TP, T4, D])
        stt, mv, rs = sb("st", [TP, T4, 6]), sb("mv", [TP, T4, 2]), sb("rs", [TP, 2, T4])
        xm = sb("xm", [P, 2, M])
        xh, xl = sb("xh", [P, KT, M], F32R), sb("xl", [P, KT, M], F32R)
        hf = sb("hf", [P, 2, M])
        hh, hl = sb("hh", [P, HS, M], F32R), sb("hl", [P, HS, M], F32R)
        b1 = sb("b1_col", [P, FC])
        b2 = sb("b2_all", [TP, D])
        ym = sb("ym", [TP, D])
        gate = sb("gate", [TP, PB, D]) if gated else None
        ps_u = ctx.enter_context(nc.psum_tensor(f"f{layer}_u", [P, 3, 512], F32))
        ps_t = ctx.enter_context(nc.psum_tensor(f"f{layer}_t", [P, 512], F32))
        ps_y = ctx.enter_context(nc.psum_tensor(f"f{layer}_y", [P, T4, 512], F32))

        R = B // PB
        s.plan(**weights_plan(chunks), c_in=32, x_in=16, res_in=16, gate_in=16 * PB * gated, x_out=16,
             stats=T4, ln_var=T4, rstd=2, xn_ready=T4, tr_full=KT, xm_ready=KT, tr_free=KT, xm_hi=KT, xm_lo=KT,
             up_full=FC, g_flat=FC, g_hi=FC, g_lo=FC, down_done=FC - 1, y_full=T4, y_mid=T4, y_gate=T4 * gated, y_ready=T4)
        xv = x_src.rearrange("(r b) (t p) d -> r p (b t) d", p=TP, b=PB)
        yv = x_dst.rearrange("(r b) (t p) d -> r p (b t) d", p=TP, b=PB)
        block = ctx.enter_context(nc.Block())

        @block.sync
        def _(sp):
            sp.dma_start(b1[:], io[f"f{layer}_b1"]).then_inc(s.c_in.sem, 16)
            sp.dma_start(b2[:], io[f"f{layer}_b2"].partition_broadcast(TP)).then_inc(s.c_in.sem, 16)
            weights_sync(sp, s, chunks, stage)
            with sp.Fori(0, R) as r:
                sp.wait_ge(s.tr_full.sem, s.tr_full.at(r, 0))
                sp.dma_start(xa[:], xv[r]).then_inc(s.x_in.sem, 16)
                if gated:
                    sp.wait_ge(s.y_gate.sem, s.y_gate.at(r, 0))
                    for i in range(PB):
                        sp.dma_start(gate[:, i, :], io["gates"][1, PB * r + i].partition_broadcast(TP)).then_inc(s.gate_in.sem, 16)
                sp.wait_ge(s.x_out.sem, s.x_out.at(r, 0))
                sp.dma_start(res[:], xv[r]).then_inc(s.res_in.sem, 16)
                sp.wait_ge(s.y_ready.sem, s.y_ready.at(r, T4))
                sp.dma_start(yv[r], res[:]).then_inc(s.x_out.sem, 16)
            sp.wait_ge(s.x_out.sem, s.x_out.at(R, 0))

        @block.tensor
        def _(pe):
            pe.wait_ge(s.w_lo.sem, s.w_lo.at(0, len(chunks)))
            with pe.Fori(0, R) as r:
                pe.wait_ge(s.xn_ready.sem, s.xn_ready.at(r, T4))
                for k in range(KT):
                    pe.wait_ge(s.tr_free.sem, s.tr_free.at(r, k))
                    for i in range(T4):
                        mm = pe.transpose(ps_t[:, i * TP:(i + 1) * TP], xa[:, i, k * P:(k + 1) * P], t.ident[0:TP, 0:TP])
                    mm.then_inc(s.tr_full.sem, 1)
                pe.wait_ge(s.xm_lo.sem, s.xm_lo.at(r, KT))

                def up(f):
                    pe.wait_ge(s.g_flat.sem, s.g_flat.at(r, f - 2))
                    for k in range(KT):
                        c = slice(f * P, (f + 1) * P)
                        mm = three_passes(pe, ps_u[:, f % 3, 0:M], w1[0][:, k, c], w1[1][:, k, c],
                                          xh[:, k, :], xl[:, k, :], k == 0, k == KT - 1)
                    mm.then_inc(s.up_full.sem, 1)

                def down(f):
                    pe.wait_ge(s.g_lo.sem, s.g_lo.at(r, f + 1))
                    if f == 0:
                        pe.wait_ge(s.y_ready.sem, s.y_ready.at(r, 0))
                    for i in range(T4):
                        c = slice(i * TP, (i + 1) * TP)
                        mm = three_passes(pe, ps_y[0:TP, i, :], hh[:, f % HS, c], hl[:, f % HS, c],
                                          w2[0][:, f, :], w2[1][:, f, :], f == 0, f == FC - 1)
                        if f == FC - 1:
                            mm.then_inc(s.y_full.sem, 1)
                    if f < FC - 1:
                        mm.then_inc(s.down_done.sem, 1)

                for f in range(FC + LAG):
                    if f < FC:
                        up(f)
                    if f >= LAG:
                        down(f - LAG)

        @block.vector
        def _(dve):
            weights_vector(dve, s, chunks, stage)
            dve.wait_ge(s.c_in.sem, s.c_in.at(0, 32))
            with dve.Fori(0, R) as r:
                dve.wait_ge(s.x_in.sem, s.x_in.at(r, 16))
                ln_vector_stats(dve, s, r, xa, stt, mv, T4, t.pad, s.stats, s.ln_var)
                ln_vector_apply(dve, s, r, xa, mv, rs, T4, s.rstd, s.xn_ready)
                for k in range(KT):
                    dve.wait_ge(s.tr_full.sem, s.tr_full.at(r, k + 1))
                    dve.wait_ge(s.xm_lo.sem, s.xm_lo.at(r, k - 1))
                    for i in range(PB):
                        c = slice(i * N, (i + 1) * N)
                        dve.tensor_scalar(xm[:, k % 2, c], ps_t[:, c], t.mod[:, ln, 0, k, bass.ds(r * PB + i, 1)],
                                          t.mod[:, ln, 1, k, bass.ds(r * PB + i, 1)], ALU.mult, ALU.add).then_inc((s.xm_ready, s.tr_free)[i].sem, 1)
                for f in range(FC):
                    dve.wait_ge(s.g_hi.sem, s.g_hi.at(r, f + 1))
                    dve.tensor_tensor(hl[:, f % HS, :], hf[:, f % 2, :], f32(hh[:, f % HS, :]), ALU.subtract).then_inc(s.g_lo.sem, 1)
                dve.wait_ge(s.res_in.sem, s.res_in.at(r, 16))
                if gated:
                    dve.wait_ge(s.gate_in.sem, s.gate_in.at(r, 16 * PB))
                for i in range(T4):
                    dve.wait_ge(s.y_full.sem, s.y_full.at(r, i + 1))
                    dve.wait_ge(s.y_ready.sem, s.y_ready.at(r, i))
                    dve.tensor_tensor(ym[:], ps_y[0:TP, i, :], b2[:], ALU.add).then_inc(s.y_mid.sem, 1)
                    dve.wait_ge(s.y_mid.sem, s.y_mid.at(r, i + 1))
                    if gated:
                        dve.tensor_tensor(ym[:], ym[:], gate[:, i // TT, :], ALU.mult).then_inc(s.y_gate.sem, 1)
                        dve.wait_ge(s.y_gate.sem, s.y_gate.at(r, i + 1))
                    dve.tensor_tensor(res[:, i, :], res[:, i, :], ym[:], ALU.add).then_inc(s.y_ready.sem, 1)

        @block.scalar
        def _(act):
            weights_scalar(act, s, chunks, stage)
            act.wait_ge(s.c_in.sem, s.c_in.at(0, 32))
            with act.Fori(0, R) as r:
                for k in range(KT):
                    act.wait_ge(s.tr_free.sem, s.tr_free.at(r, k + 1))
                    act.activation(xh[:, k, :], xm[:, k % 2, :], ACT.Copy).then_inc(s.xm_hi.sem, 1)
                for f in range(FC):
                    act.wait_ge(s.up_full.sem, s.up_full.at(r, f + 1))
                    act.wait_ge(s.g_lo.sem, s.g_lo.at(r, f - 1))
                    act.activation(hf[:, f % 2, :], ps_u[:, f % 3, 0:M], (ACT.Gelu, ACT.Gelu_apprx_tanh)[layer],
                                   bias=b1[:, f:f + 1]).then_inc(s.g_flat.sem, 1)
                    act.wait_ge(s.g_flat.sem, s.g_flat.at(r, f + 1))
                    if f < HS:
                        act.wait_ge(s.y_full.sem, s.y_full.at(r, 0))
                    else:
                        act.wait_ge(s.down_done.sem, s.down_done.at(r, f - HS + 1))
                    act.activation(hh[:, f % HS, :], hf[:, f % 2, :], ACT.Copy).then_inc(s.g_hi.sem, 1)

        @block.gpsimd
        def _(pool):
            with pool.Fori(0, R) as r:
                ln_pool_rstd(pool, s, r, mv, rs, t.eps[0:TP, layer, 0:T4], t.neghalf[0:TP, 0:T4], T4, s.ln_var, s.rstd)
                for k in range(KT):
                    pool.wait_ge(s.xm_hi.sem, s.xm_hi.at(r, k + 1))
                    pool.tensor_tensor(xl[:, k, :], xm[:, k % 2, :], f32(xh[:, k, :]), ALU.subtract).then_inc(s.xm_lo.sem, 1)
    s.close(ONCE, R)


class Tables:

    def __init__(self, nc, ctx):
        def sb(name, shape, dt=F32):
            return ctx.enter_context(nc.sbuf_tensor(name, shape, dt))
        self.ident = sb("ident", [P, P])
        self.ident_bf = sb("ident_bf", [P, P], BF16)
        self.ones = sb("ones", [P, HD])
        self.neghalf = sb("neghalf", [P, 8])
        self.eps = sb("eps", [P, 2, 8])
        self.pad = sb("pad", [P, 2])
        self.mod = sb("mod", [P, 6, 2, KT, B])


def build(nc, io):
    with ExitStack() as ctx:
        s = Signals(nc, ctx)
        t = Tables(nc, ctx)
        with nc.Block() as block:
            @block.sync
            def _(sp):
                for x in s.all.values():
                    sp.sem_inc(x.sem, CREDIT)
        modulation(nc, s, t, io)
        x = io["x"]
        for layer in range(2):
            attention_phase(nc, s, t, io, False, layer, x, io["x1"])
            attention_phase(nc, s, t, io, True, layer, io["x1"], io["x2"])
            x = io["x3"] if layer == 0 else io["out"]
            feed_forward(nc, s, t, io, layer, io["x2"], x)


def rope_tables():
    half = HD // 2
    inv = (np.float32(1.0) / np.float32(10000.0) ** (np.arange(half, dtype=np.float32) / np.float32(half))).astype(np.float32)
    ang = (np.arange(NC, dtype=np.float32)[:, None] * inv[None, :]).astype(np.float32)
    c, s = np.cos(ang).T.astype(np.float32), np.sin(ang).T.astype(np.float32)
    return np.tile(np.concatenate([c, c]), (HG, 1)), np.tile(np.concatenate([-s, s]), (HG, 1))


def kernel(**inputs):
    import concourse.bacc as bacc
    from concourse.bass_utils import run_bass_kernel_spmd

    g = {k: np.asarray(v) for k, v in inputs.items()}
    l0 = {k[9:]: v for k, v in g.items() if k.startswith("L0_xcond_")}
    l1 = {k[9:]: v for k, v in g.items() if k.startswith("L1_xcond_")}
    cos, sin = rope_tables()
    arrays = dict(
        x=g["x"], ctx=g["ctx_1024"], condT=g["cond_1024"].T, cos=cos, sin=sin,
        ln1_w=l0["ln1_w"].T, ln2_w=l0["ln2_w"].T, ln3_w=l0["ln3_w"].T, W_mod=l1["W_mod"],
        ln1_b=l0["ln1_b"], ln2_b=l0["ln2_b"], ln3_b=l0["ln3_b"], b_mod=l1["b_mod"],
        s0_qkv=l0["qkv_w"].T, s0_wo=l0["sa_out_w"].T,
        c0_wq=l0["q_w"].T, c0_wk=l0["k_w"].T, c0_wv=l0["v_w"].T, c0_wo=l0["ca_out_w"].T,
        f0_w1=l0["ffn_w1"].T, f0_b1=l0["ffn_b1"], f0_w2=l0["ffn_w2"].T, f0_b2=l0["ffn_b2"],
        s1_qkv=l1["W_qkv"], s1_wo=l1["W_proj"],
        s_bq=l1["b_qkv"][0:D], s_bk=l1["b_qkv"][D:2 * D], s_bv=l1["b_qkv"][2 * D:3 * D], s_bo=l1["b_proj"],
        c1_wq=l1["W_qc"], c1_wk=l1["W_kvc"][:, 0:D], c1_wv=l1["W_kvc"][:, D:2 * D], c1_wo=l1["W_cproj"],
        c_bq=l1["b_qc"], c_bk=l1["b_kvc"][0:D], c_bv=l1["b_kvc"][D:2 * D], c_bo=l1["b_cproj"],
        f1_w1=l1["W_mlp1"], f1_b1=l1["b_mlp1"], f1_w2=l1["W_mlp2"], f1_b2=l1["b_mlp2"],
    )
    for k in ("f0_b1", "f1_b1", "s_bq", "s_bk", "c_bq", "c_bk"):
        arrays[k] = arrays[k].reshape(-1, P).T
    arrays = {k: np.ascontiguousarray(v) for k, v in arrays.items()}
    nc = bacc.Bacc("TRN2", target_bir_lowering=False, num_devices=1)
    io = {k: nc.dram_tensor(k, v.shape, F32, kind="ExternalInput").ap() for k, v in arrays.items()}
    io["out"] = nc.dram_tensor("out", (B, N, D), F32, kind="ExternalOutput").ap()
    for k in ("x1", "x2", "x3"):
        io[k] = nc.dram_tensor(k, (B, N, D), F32, kind="Internal").ap()
    io["gates"] = nc.dram_tensor("gates", (2, B, D), F32, kind="Internal").ap()
    build(nc, io)
    r = run_bass_kernel_spmd(nc, [arrays], core_ids=[0])
    return r.results[0]["out"]
```

```python
from contextlib import ExitStack

import numpy as np

import concourse.bass as bass
from concourse import mybir

F32 = mybir.dt.float32
F32R = mybir.dt.float32r
BF16 = mybir.dt.bfloat16
ALU = mybir.AluOpType
ACT = mybir.ActivationFunctionType
AX = mybir.AxisListType

B, N, D = 8, 224, 512
NC = 750
H, HD = 16, 32
FF = 2048
P = 128
KT = D // P
TT, TP = 2, 112
HG = P // HD
NG = H // HG
SCALE = HD ** -0.5
STACK = 3 * HD
STACKM = STACK + 2
CHUNK = 1024
SWAP = [(i + HD // 2) % HD for i in range(HD)]
CREDIT = 16


class Tally:

    def __init__(self, sem):
        self.sem, self.base, self.per = sem, CREDIT, 0

    def at(self, rnd, n):
        rnd, ahead = rnd if isinstance(rnd, tuple) else (rnd, 0)
        return rnd * self.per + (self.base + ahead * self.per + n)


class Signals:

    def __init__(self, nc, ctx):
        def new(name):
            self.all[name] = Tally(ctx.enter_context(nc.semaphore(name)))
            return self.all[name]

        self.all = {}
        self.const = new("const")
        self.c_in = new("c_in")
        self.c_silu = new("c_silu")
        self.m_raw0 = new("m_raw0")
        self.m_raw1 = new("m_raw1")
        self.tr_full = new("tr_full")
        self.tr_free = new("tr_free")
        self.mod_rows = new("mod_rows")
        self.gates_out = new("gates_out")
        self.w_raw0 = new("w_raw0")
        self.w_raw1 = new("w_raw1")
        self.w_hi = new("w_hi")
        self.w_lo = new("w_lo")
        self.x_in = new("x_in")
        self.res_in = new("res_in")
        self.ctx_in = new("ctx_in")
        self.gate_in = new("gate_in")
        self.fill0 = new("fill0")
        self.fill1 = new("fill1")
        self.x_out = new("x_out")
        self.two_waits = new("two_waits")
        self.stats = new("stats")
        self.ln_var = new("ln_var")
        self.rstd = new("rstd")
        self.xn_ready = new("xn_ready")
        self.cstats = new("cstats")
        self.cvar = new("cvar")
        self.crstd = new("crstd")
        self.cn_ready = new("cn_ready")
        self.ctx_full, self.ctx_free = new("ctx_full"), new("ctx_free")
        self.x_full, self.x_free = new("x_full"), new("x_free")
        self.f_full, self.f_free = new("f_full"), new("f_free")
        self.v_full, self.v_free = new("v_full"), new("v_free")
        self.y_full, self.y_free = new("y_full"), new("y_free")
        self.xm_ready = new("xm_ready")
        self.xm_hi = new("xm_hi")
        self.xm_lo = new("xm_lo")
        self.cx_hi = new("cx_hi")
        self.f_cos = new("f_cos")
        self.f_sin = new("f_sin")
        self.f_flat = new("f_flat")
        self.f_hi = new("f_hi")
        self.f_lo = new("f_lo")
        self.max_full = new("max_full")
        self.max_free = new("max_free")
        self.m_rows = new("m_rows")
        self.m_top = new("m_top")
        self.m_ready = new("m_ready")
        self.shift_full = new("shift_full")
        self.shift_free = new("shift_free")
        self.s_full = new("s_full")
        self.s_free = new("s_free")
        self.av_done = new("av_done")
        self.e_sum = new("e_sum")
        self.sum_done = new("sum_done")
        self.a_rec = new("a_rec")
        self.a_flat = new("a_flat")
        self.a_hi = new("a_hi")
        self.a_lo = new("a_lo")
        self.up_full = new("up_full")
        self.g_flat = new("g_flat")
        self.g_hi = new("g_hi")
        self.g_lo = new("g_lo")
        self.down_done = new("down_done")
        self.y_mid = new("y_mid")
        self.y_gate = new("y_gate")
        self.y_ready = new("y_ready")

    def plan(self, **per):
        for tally in self.all.values():
            tally.per = 0
        for name, n in per.items():
            self.all[name].per = n

    def close(self, once, rounds):
        for name, tally in self.all.items():
            tally.base += tally.per * (1 if name in once else rounds)
            tally.per = 0


ONCE = ("w_raw0", "w_raw1", "w_hi", "w_lo", "c_in", "const")


def f32(ap):
    return ap.bitcast(F32)


def three_passes(pe, out, w_hi, w_lo, x_hi, x_lo, first, last):
    pe.matmul(out, w_hi, x_hi, start=first, stop=False)
    pe.matmul(out, w_hi, x_lo, start=False, stop=False)
    return pe.matmul(out, w_lo, x_hi, start=False, stop=last)



def weight_chunks(w, hi, lo):
    rows, cols = w.shape
    wv = w.rearrange("(k p) n -> p k n", p=P)
    step = next(c for c in (CHUNK, 768, 512) if cols % c == 0)
    return [(wv[:, k, c:c + step], hi[:, k, c:c + step], lo[:, k, c:c + step])
            for k in range(rows // P) for c in range(0, cols, step)]


def weights_sync(sp, s, chunks, stage):
    for i, (raw, _, _) in enumerate(chunks):
        if i >= 2:
            sp.wait_ge(s.w_lo.sem, s.w_lo.at(0, i - 1))
        sp.dma_start(stage[:, i % 2, 0:raw.shape[1]], raw).then_inc((s.w_raw0, s.w_raw1)[i % 2].sem, 16)


def weights_scalar(act, s, chunks, stage):
    for i, (raw, hi, _) in enumerate(chunks):
        act.wait_ge((s.w_raw0, s.w_raw1)[i % 2].sem, (s.w_raw0, s.w_raw1)[i % 2].at(0, 16 * (i // 2 + 1)))
        act.activation(hi, stage[:, i % 2, 0:raw.shape[1]], ACT.Copy).then_inc(s.w_hi.sem, 1)


def weights_vector(dve, s, chunks, stage):
    for i, (raw, hi, lo) in enumerate(chunks):
        dve.wait_ge(s.w_hi.sem, s.w_hi.at(0, i + 1))
        dve.tensor_tensor(lo, stage[:, i % 2, 0:raw.shape[1]], f32(hi), ALU.subtract).then_inc(s.w_lo.sem, 1)


def weights_plan(chunks):
    n = len(chunks)
    return dict(w_raw0=16 * ((n + 1) // 2), w_raw1=16 * (n // 2), w_hi=n, w_lo=n)



def modulation(nc, s, t, io):
    chunks = []
    for w in (io["ln1_w"], io["ln2_w"], io["ln3_w"], io["W_mod"]):
        wv = w.rearrange("(k p) n -> p k n", p=P)
        chunks += [wv[:, :, c:c + D] for c in range(0, w.shape[1], D)]
    NV = len(chunks)
    with ExitStack() as ctx:
        def sb(name, shape, dt=F32):
            return ctx.enter_context(nc.sbuf_tensor(name, shape, dt))
        raw = sb("mod_raw", [P, 2, KT, D])
        cond = sb("cond", [P, 2, KT, B])
        rows = sb("mod_rows_sb", [B, NV, D])
        bias = sb("mod_bias", [B, NV, D])
        ps_rows = ctx.enter_context(nc.psum_tensor("ps_rows", [B, 2, D], F32))
        ps_vec = ctx.enter_context(nc.psum_tensor("ps_vec", [P, NV, KT, B], F32))
        s.plan(m_raw0=16 * NV // 2, m_raw1=16 * NV // 2, c_in=32 + 16 * 4, tr_full=NV, tr_free=NV, mod_rows=1,
             const=CONSTS, c_silu=1, gates_out=32)
        block = ctx.enter_context(nc.Block())

        @block.sync
        def _(sp):
            sp.dma_start(cond[:, 0], io["condT"].rearrange("(k p) b -> p k b", p=P)).then_inc(s.c_in.sem, 16)
            sp.dma_start(cond[:, 1], io["condT"].rearrange("(k p) b -> p k b", p=P)).then_inc(s.c_in.sem, 16)
            at = 0
            for name in ("ln1_b", "ln2_b", "ln3_b", "b_mod"):
                n = io[name].shape[0] // D
                sp.dma_start(bias[:, at:at + n, :].rearrange("p a d -> p (a d)"),
                             io[name].partition_broadcast(B)).then_inc(s.c_in.sem, 16)
                at += n
            for i, w in enumerate(chunks):
                if i >= 2:
                    sp.wait_ge(s.tr_full.sem, s.tr_full.at(0, i - 1))
                sp.dma_start(raw[:, i % 2], w).then_inc((s.m_raw0, s.m_raw1)[i % 2].sem, 16)
            sp.wait_ge(s.tr_free.sem, s.tr_free.at(0, NV))
            for g, v in enumerate((8, 11)):
                sp.dma_start(io["gates"][g], rows[:, v, :]).then_inc(s.gates_out.sem, 8 * 2)
            sp.wait_ge(s.gates_out.sem, s.gates_out.at(0, 32))

        @block.scalar
        def _(act):
            act.wait_ge(s.c_in.sem, s.c_in.at(0, 96))
            act.activation(cond[:, 1], cond[:, 1], ACT.Silu).then_inc(s.c_silu.sem, 1)

        @block.tensor
        def _(pe):
            pe.wait_ge(s.c_in.sem, s.c_in.at(0, 96))
            pe.wait_ge(s.c_silu.sem, s.c_silu.at(0, 1))
            for i in range(NV):
                pe.wait_ge((s.m_raw0, s.m_raw1)[i % 2].sem, (s.m_raw0, s.m_raw1)[i % 2].at(0, 16 * (i // 2 + 1)))
                if i >= 2:
                    pe.wait_ge(s.tr_free.sem, s.tr_free.at(0, i - 1))
                for k in range(KT):
                    mm = pe.matmul(ps_rows[:, i % 2, :], cond[:, int(i >= 6), k, :], raw[:, i % 2, k, :],
                                   start=(k == 0), stop=(k == KT - 1))
                mm.then_inc(s.tr_full.sem, 1)
            pe.wait_ge(s.tr_free.sem, s.tr_free.at(0, NV))
            pe.wait_ge(s.const.sem, s.const.at(0, CONSTS))
            for v in range(NV):
                for k in range(KT):
                    mm = pe.transpose(ps_vec[:, v, k, :], rows[:, v, k * P:(k + 1) * P], t.ident[0:B, 0:B])
            mm.then_inc(s.mod_rows.sem, 1)

        @block.vector
        def _(dve):
            dve.wait_ge(s.c_in.sem, s.c_in.at(0, 96))
            for i in range(NV):
                dve.wait_ge(s.tr_full.sem, s.tr_full.at(0, i + 1))
                dve.tensor_tensor(rows[:, i, :], ps_rows[:, i % 2, :], bias[:, i, :], ALU.add).then_inc(s.tr_free.sem, 1)
            dve.wait_ge(s.mod_rows.sem, s.mod_rows.at(0, 1))
            for ln, sc, sh in ((0, 0, 1), (1, 2, 3), (2, 4, 5), (3, 7, 6), (5, 10, 9)):
                dve.tensor_scalar(t.mod[:, ln, 0], ps_vec[:, sc], 1.0, None, ALU.add)
                dve.tensor_copy(t.mod[:, ln, 1], ps_vec[:, sh])
            dve.memset(t.mod[:, 4, 0], 1.0)
            dve.memset(t.mod[:, 4, 1], 0.0)
            dve.drain()

        @block.gpsimd
        def _(pool):
            constants(pool, s, t)
    s.close((), 1)


CONSTS = 8


def constants(pool, s, t):
    pool.memset(t.ident[:], 0.0).then_inc(s.const.sem, 1)
    pool.wait_ge(s.const.sem, s.const.at(0, 1))
    pool.affine_select(out=t.ident[:], in_=t.ident[:], compare_op=ALU.not_equal, fill=1.0, base=0,
                       pattern=[[-1, P]], channel_multiplier=1).then_inc(s.const.sem, 1)
    pool.memset(t.ones[:], 1.0).then_inc(s.const.sem, 1)
    pool.memset(t.neghalf[:], -0.5).then_inc(s.const.sem, 1)
    pool.memset(t.eps[:, 0], 1e-5).then_inc(s.const.sem, 1)
    pool.memset(t.eps[:, 1], 1e-6).then_inc(s.const.sem, 1)
    pool.wait_ge(s.const.sem, s.const.at(0, 6))
    pool.tensor_copy(t.ident_bf[:], t.ident[:]).then_inc(s.const.sem, 1)
    pool.wait_ge(s.const.sem, s.const.at(0, 7))
    pool.memset(t.pad[:], 0.0).then_inc(s.const.sem, 1)



def ln_vector_stats(dve, s, rnd, x, st, mv, tiles, pad, stats, var):
    for i in range(tiles):
        dve.bn_stats(st[:, i, :], x[:, i, :]).then_inc(stats.sem, 1)
    dve.wait_ge(stats.sem, stats.at(rnd, tiles))
    dve.tensor_copy(pad[:, 0:1], pad[:, 1:2])
    for i in range(tiles):
        dve.bn_aggr(mv[:, i, :], st[:, i, :]).then_inc(var.sem, 1)


def ln_pool_rstd(pool, s, rnd, mv, rs, eps, nh, tiles, var, rstd):
    pool.wait_ge(var.sem, var.at(rnd, tiles))
    pool.wait_ge(rstd.sem, rstd.at(rnd, 0))
    pool.tensor_tensor(rs[:, 0, :], mv[:, :, 1], eps, ALU.add).then_inc(rstd.sem, 1)
    pool.wait_ge(rstd.sem, rstd.at(rnd, 1))
    pool.tensor_tensor(rs[:, 1, :], rs[:, 0, :], nh, ALU.pow).then_inc(rstd.sem, 1)


def ln_vector_apply(dve, s, rnd, x, mv, rs, tiles, rstd, ready):
    dve.wait_ge(rstd.sem, rstd.at(rnd, 2))
    for i in range(tiles):
        dve.tensor_scalar(x[:, i, :], x[:, i, :], mv[:, i, 0:1], rs[:, 1, i:i + 1],
                          ALU.subtract, ALU.mult).then_inc(ready.sem, 1)



class Attention:

    def __init__(self, cross, layer):
        self.cross, self.layer = cross, layer
        self.keys = NC if cross else N
        self.kp = 125 if cross else TP
        self.tiles = self.keys // self.kp
        self.pairs = self.tiles // 2
        self.kcols = [(0, 376), (376, 750)] if cross else [(0, N)]
        self.fu = len(self.kcols) + 1
        self.mu = HG * (4 if cross else 1)
        self.gs = 1 if cross else 2
        self.fills = NG // self.gs // 2
        self.rope = layer == 0
        self.per_kind = dict(ctx=8 * cross, x=2, f=NG * self.fu, v=self.tiles, y=TT)

        body = [w for g in range(NG) for w in self.step(g)] + [(0, ("y", i)) for i in range(TT)]
        self.prologue = self.ring(self.prepare(), [None, None])
        self.rest = self.tail
        before = [(db - 1, e) for db, e in [w for w in body if w[1][0] in self.per_kind][-2:]]
        self.body = self.ring(body, before)
        self.last = self.ring([w for w in body if w[0] == 0], before)

    def nth(self, e):
        return e[1] * self.fu + e[2] if e[0] == "f" else e[1]

    def ring(self, events, before):
        used, out = list(before), []
        for db, e in events:
            if e[0] in self.per_kind:
                if e[0] not in ("f", "v") or e[-1] == 0:
                    used.append((db, e))
                out.append((db, e, len(used) % 2, used[-3]))
            else:
                out.append((db, e, None, None))
        self.tail = used[-2:]
        assert len(used) % 2 == 0
        return out

    def f(self, g, u):
        return [("f", g, u, k) for k in range(KT)]

    def v(self, *tiles):
        return [("v", i, k) for i in tiles for k in range(KT)]

    def prepare(self):
        m = [("m", 0, u) for u in range(self.mu)]
        half = self.mu // 2
        out = [("cln",)] * self.cross + [("ctx", i) for i in range(8 if self.cross else 0)]
        out += [("ln",)] + [("x", i) for i in range(2)]

        def group(g):
            fs = [self.f(g, u) for u in range(self.fu)]
            hs = [[("h", g, u)] for u in range(self.fu)]
            if self.cross:
                return fs[0] + fs[1] + hs[0] + hs[1] + fs[2] + hs[2]
            return fs[0] + fs[1] + hs[0] + hs[1]
        if self.cross:
            out += group(0) + self.v(0, 1, 2) + group(1) + self.v(3, 4, 5) + self.f(2, 0) + self.f(2, 1)
        else:
            out += group(0) + group(1) + self.v(0, 1) + group(2) + group(3)
        return [(0, e) for e in out + m[:half] + [("t", 0, 0)] + m[half:] + [("t", 0, 1)] * self.cross]

    def step(self, g):
        def mark(events, ahead=0):
            return [(ahead, e) for e in events]

        def weave(main, fill):
            out, n = [], 0
            for i, e in enumerate(main):
                out.append(e)
                while n < len(fill) * (i + 1) // len(main):
                    out.append(fill[n])
                    n += 1
            return out

        mg, md = (g + 1) % NG, (g + 1) // NG
        m = mark([("m", mg, u) for u in range(self.mu)], md)
        t0 = mark([("t", mg, 0)], md)
        t1 = mark([("t", g, 1)])
        s = [mark([("s", g, c, j) for j in range(HG)]) for c in range(self.pairs)]
        e = mark([("e", g, c) for c in range(self.pairs)])
        v = mark([("a", g, c) for c in range(self.pairs)])
        o, d = mark([("o", g)]), mark([("d", g)])
        if not self.cross:
            x = mark([("x", 0), ("x", 1)], 1)
            fh = [mark(self.f(i, 0) + self.f(i, 1), 1) for i in range(NG)]
            h = [mark([("h", i, 0), ("h", i, 1)], 1) for i in range(NG)]
            main = s[0][:2] + t1 + s[0][2:3] + m[:1] + s[0][3:] + m[1:2]
            tail = m[2:] + t0 + e + v + o + d
            if g == 0:
                return main + m[2:] + mark([("ln",)], 1) + t0 + e + v + x + weave(o + d, fh[0][:4]) + fh[0][4:] + h[0]
            if g == 1:
                return weave(main, fh[1]) + h[1] + tail
            if g == 2:
                return weave(main, fh[2]) + h[2] + tail
            return weave(main, fh[3]) + h[3] + m[2:] + t0 + e + v + o + mark(self.v(0), 1) + d + mark(self.v(1), 1)
        kg, kd = (g + 3) % NG, (g + 3) // NG
        fg, fd = (g + 2) % NG, (g + 2) // NG
        fk = mark(self.f(kg, 0) + self.f(kg, 1), kd)
        fq = mark(self.f(fg, 2), fd)
        h = [mark([("h", fg, u)], fd) for u in range(3)]
        late = mark([("o", g - 1)]) if g else []
        later = mark([("d", g - 1)]) if g else []
        ctx = mark([("ctx", i) for i in range(8)], 1)
        x = mark([("ln",), ("x", 0), ("x", 1)], 1)
        t1 = mark([("t", mg, 1)], md)
        out = s[0][:2] + late + s[0][2:] + h[0] + h[1] + weave(s[1], m[:2]) + fq[:1] + e[:1] + later + weave(m[2:4], fq[1:])
        out += v[:1] + h[2]
        if g == 1:
            out += weave(s[2], ctx[:4]) + e[1:2] + v[1:2] + weave(m[4:8], ctx[4:]) + v[2:] + x + t0
            return out + weave(m[8:], fk[:5]) + e[2:] + fk[5:] + t1
        out += weave(s[2], m[4:8]) + e[1:2] + v[1:2] + fk[:1] + t0
        if g == 3:
            vs = mark(self.v(*range(6)), 1)
            out += weave(m[8:13], fk[1:]) + v[2:] + weave(m[13:], vs[:4]) + e[2:] + vs[4:6] + t1
            return out + vs[6:12] + o + vs[12:20] + d + vs[20:]
        return out + weave(m[8:12], fk[1:4]) + v[2:] + weave(m[12:], fk[4:6]) + e[2:] + fk[6:] + t1 + mark([("cln",)] * (g == 0), 1)


def attention_phase(nc, s, t, io, cross, layer, x_src, x_dst):
    a = Attention(cross, layer)
    ln = 3 * layer + int(cross)
    biased = layer == 1
    pre = "c" if cross else "s"
    with ExitStack() as ctx:
        def sb(name, shape, dt=F32):
            return ctx.enter_context(nc.sbuf_tensor(f"{pre}{layer}_{name}", shape, dt))

        def psum(name, shape):
            return ctx.enter_context(nc.psum_tensor(f"{pre}{layer}_ps_{name}", shape, F32))

        names = dict(k="wk", q="wq", v="wv", o="wo")
        W = {}
        if cross:
            srcs = {n: io[f"{'c' if cross else 's'}{layer}_{n}"] for n in ("wk", "wv", "wq", "wo")}
            for n in srcs:
                W[n] = (sb(n + "_hi", [P, KT, D], F32R), sb(n + "_lo", [P, KT, D], F32R))
            chunks = [c for n in ("wk", "wv", "wq", "wo") for c in weight_chunks(srcs[n], *W[n])]
        else:
            wq = (sb("qkv_hi", [P, KT, 3 * D], F32R), sb("qkv_lo", [P, KT, 3 * D], F32R))
            W["wq"], W["wk"], W["wv"] = [tuple(h[:, :, i * D:(i + 1) * D] for h in wq) for i in range(3)]
            W["wo"] = (sb("wo_hi", [P, KT, D], F32R), sb("wo_lo", [P, KT, D], F32R))
            chunks = weight_chunks(io[f"s{layer}_qkv"], *wq) + weight_chunks(io[f"s{layer}_wo"], *W["wo"])
        craw_all = sb("craw", [P, 6, D]) if cross else None
        stage = craw_all[:, 0:4].rearrange("p (s a) n -> p s (a n)", s=2) if cross else sb("stage", [P, 2, CHUNK])

        xa = sb("xa", [TP, TT, D])
        res = sb("res", [TP, TT, D])
        stt, mv, rs = sb("st", [P, 8, 6]), sb("mv", [P, 8, 2]), sb("rs", [P, 2, 8])
        xm = sb("xm", [P, 2, N])
        xh, xl = sb("xh", [P, KT, N], F32R), sb("xl", [P, KT, N], F32R)
        if cross:
            craw = craw_all[0:125]
            cst, cmv, crs = sb("cst", [125, 6, 6]), sb("cmv", [125, 6, 2]), sb("crs", [125, 2, 6])
            ch, cl = sb("ch", [P, KT, NC], F32R), sb("cl", [P, KT, NC], F32R)
            src = sb("src", [P, 2, NC + N], F32R)
            stk = sb("stk", [P, 2, HG, NC + N], F32R)
        else:
            src = sb("src", [P, 2, 4, 2, N], F32R)
            st2 = sb("st2", [P, 2, 2, HG, 2, N], F32R)
        kvh, kvl = (ch, cl) if cross else (xh, xl)
        wid = 376 if cross else N
        fa, fs = sb("fa", [P, 2, wid]), sb("fs", [P, 2, wid]) if a.rope else None
        if a.rope:
            cos, sin = sb("cos", [P, a.keys]), sb("sin", [P, a.keys])
        vt = sb("vt", [a.kp, a.tiles, D])
        mx, mhl = sb("mx", [TP, HG, TT]), sb("mhl", [TP, HG, TT, 2], BF16)
        mx2 = sb("mx2", [TP, HG, TT, 2]) if cross else None
        pt = sb("pt", [a.kp, 2, HG, 2, N])
        es = sb("es", [a.kp, HG, N])
        rec, af = sb("rec", [P, N]), sb("af", [P, N])
        ah, al = sb("ah", [P, NG, N], F32R), sb("al", [P, NG, N], F32R)
        if biased:
            ym = sb("ym", [TP, D])
            bq, bk = sb("bq", [P, KT]), sb("bk", [P, KT])
            bv, bo = sb("bv", [P, D]), sb("bo", [P, D])
            gate = sb("gate", [TP, D]) if not cross else None

        wk = psum("wk", [P, 2, 512])
        ps_max = psum("max", [P, 2, 512])
        ps_s = psum("s", [P, 2, 512])
        ps_o = psum("o", [P, 512])
        ps_shift = psum("shift", [P, 512])

        def kstack(g, j, rows, c0, c1):
            if cross:
                return stk[0:rows, g % 2, j, c0:c1]
            return st2[0:rows, g // 2, 0, j, g % 2, c0:c1]

        def qstack(g, j, rows, c0, c1):
            if cross:
                return stk[0:rows, g % 2, j, NC + c0:NC + c1]
            return st2[0:rows, g // 2, 1, j, g % 2, c0:c1]

        def e_count(cs):
            g, c = divmod(cs, a.pairs)
            per = 2 * a.pairs - 1
            return g * per + (2 * c - 1 if c > 0 else 0)

        def sum_pair(eng, b, g, c):
            cs = g * a.pairs + c
            eng.wait_ge(s.s_free.sem, s.s_free.at(b, (cs + 1) * HG))
            tile = [pt[:, cs % 2, :, k, :] for k in range(2)]
            if c == 0:
                eng.wait_ge(s.sum_done.sem, s.sum_done.at(b, g))
                eng.tensor_tensor(es[:], tile[0], tile[1], ALU.add).then_inc(s.e_sum.sem, 1)
            else:
                for k in range(2):
                    eng.wait_ge(s.e_sum.sem, s.e_sum.at(b, e_count(cs) + k))
                    eng.tensor_tensor(es[:], es[:], tile[k], ALU.add).then_inc(s.e_sum.sem, 1)

        def f_width(u):
            return a.kcols[u][1] - a.kcols[u][0] if u < len(a.kcols) else N

        def f_dst(g, u, half):
            isq = u == a.fu - 1
            if not cross:
                return src[:, g // 2, 2 * isq + half, g % 2, :]
            return src[:, half, NC:] if isq else src[:, 1 - half, a.kcols[u][0]:a.kcols[u][1]]

        slots = 2
        dmas = 16 if cross else 12
        nchunks = len(chunks)
        nf = NG * a.fu
        gated = biased and not cross
        cn = biased and cross
        s.plan(**weights_plan(chunks), x_in=16, res_in=16, ctx_in=16 * cross, gate_in=16 * gated,
             fill0=16 * dmas * a.fills, fill1=16 * dmas * a.fills, x_out=16,
             ctx_full=a.per_kind["ctx"], ctx_free=a.per_kind["ctx"], x_full=2, x_free=2,
             f_full=nf, f_free=nf, v_full=a.tiles, v_free=a.tiles, y_full=TT, y_free=TT, max_full=NG * a.mu, max_free=NG * a.mu,
             s_full=NG * HG * a.pairs, s_free=NG * HG * a.pairs, shift_full=NG * 2, shift_free=NG * 2,
             av_done=NG * a.pairs, sum_done=NG, stats=TT, ln_var=TT, rstd=2, xn_ready=TT,
             cstats=6 * cn, cvar=6 * cn, crstd=2 * cn, cn_ready=6 * cn,
             xm_ready=KT // 2, xm_hi=KT, xm_lo=KT, cx_hi=8 * cross,
             f_cos=nf * a.rope, f_sin=nf * a.rope, f_flat=nf * a.rope, f_hi=nf, f_lo=nf,
             m_top=2 * NG, m_ready=2 * NG, m_rows=2 * NG * cross, e_sum=NG * (2 * a.pairs - 1),
             a_rec=NG, a_flat=NG, a_hi=NG, a_lo=NG, y_mid=TT * biased, y_gate=TT * gated,
             c_in=16 * 6, const=2)
        full = dict(ctx=s.ctx_full, x=s.x_full, f=s.f_full, v=s.v_full, y=s.y_full)
        free = dict(ctx=s.ctx_free, x=s.x_free, f=s.f_free, v=s.v_free, y=s.y_free)
        block = ctx.enter_context(nc.Block())
        xv = x_src.rearrange("b (t p) d -> b p t d", p=TP)
        yv = x_dst.rearrange("b (t p) d -> b p t d", p=TP)

        @block.sync
        def _(sp):
            n = 0
            if a.rope:
                sp.dma_start(cos[:], io["cos"][:, 0:a.keys]).then_inc(s.c_in.sem, 16)
                sp.dma_start(sin[:], io["sin"][:, 0:a.keys]).then_inc(s.c_in.sem, 16)
                n += 2
            if biased:
                for dst, name in ((bq, "bq"), (bk, "bk")):
                    sp.dma_start(dst[:], io[f"{pre}_{name}"]).then_inc(s.c_in.sem, 16)
                for dst, name in ((bv, "bv"), (bo, "bo")):
                    sp.dma_start(dst[:], io[f"{pre}_{name}"].partition_broadcast(P)).then_inc(s.c_in.sem, 16)
                n += 4
            while n < 6:
                sp.dma_start(stt[:, 0, 0:2], io["cos"][:, 0:2]).then_inc(s.c_in.sem, 16)
                n += 1
                sp.wait_ge(s.c_in.sem, s.c_in.at(0, 16 * n))
            weights_sync(sp, s, chunks, stage)
            sp.wait_ge(s.w_lo.sem, s.w_lo.at(0, nchunks))

            def load(r, at):
                sp.wait_ge(s.x_full.sem, s.x_full.at(r, 0))
                sp.dma_start(xa[:], xv[at]).then_inc(s.x_in.sem, 16)
                if cross:
                    sp.wait_ge(s.ctx_full.sem, s.ctx_full.at(r, 0))
                    sp.dma_start(craw[:], io["ctx"][at].rearrange("(t p) d -> p t d", p=125)).then_inc(s.ctx_in.sem, 16)

            def refill(r, i):
                if cross:
                    done = s.s_full.at(r, (i - 1) * HG * a.pairs)
                    sp.wait_ge(s.f_lo.sem, s.f_lo.at(r, a.nth(("f", i, 1)) + 1))
                    sp.sem_inc(s.two_waits.sem, 1)
                    sp.wait_ge(s.s_full.sem, done)
                    sem = (s.fill0, s.fill1)[i % 2].sem
                    rows = [slice(HD * j, HD * (j + 1)) for j in range(HG)]
                    for j in range(HG):
                        sp.dma_start(f32(stk[0:HD, i % 2, j, 0:NC]), f32(src[rows[j], 1, 0:NC])).then_inc(sem, 16)
                    sp.wait_ge(s.f_lo.sem, s.f_lo.at(r, a.nth(("f", i, 2)) + 1))
                    for j in range(HG):
                        sp.dma_start(f32(stk[HD:2 * HD, i % 2, j, :]), f32(src[rows[j], 1, :])).then_inc(sem, 16)
                        sp.dma_start(f32(stk[2 * HD:STACK, i % 2, j, :]), f32(src[rows[j], 0, :])).then_inc(sem, 16)
                        sp.dma_start(f32(stk[0:HD, i % 2, j, NC:]), f32(src[rows[j], 0, NC:])).then_inc(sem, 16)
                else:
                    sp.wait_ge(s.f_lo.sem, s.f_lo.at(r, a.nth(("f", 2 * i + 1, 1)) + 1))
                    sp.sem_inc(s.two_waits.sem, 1)
                    sp.wait_ge(s.s_full.sem, s.s_full.at(r, (2 * i - 2) * HG * a.pairs))
                    sem = (s.fill0, s.fill1)[i].sem
                    for j in range(HG):
                        own = slice(HD * j, HD * (j + 1))
                        for row, kind in ((0, slice(0, 4, 2)), (1, slice(0, 4, 3)), (2, slice(1, 3, 1))):
                            to = slice(HD * row, HD * (row + 1))
                            sp.dma_start(f32(st2[to, i, :, j].rearrange("p a g n -> p a (g n)")),
                                         f32(src[own, i, kind].rearrange("p a g n -> p a (g n)"))).then_inc(sem, 16)

            def batch(b, more):
                if more:
                    load((b, 1), b + 1)
                if gated:
                    sp.wait_ge(s.y_gate.sem, s.y_gate.at(b, 0))
                    sp.dma_start(gate[:], io["gates"][0, b].partition_broadcast(TP)).then_inc(s.gate_in.sem, 16)
                sp.wait_ge(s.x_out.sem, s.x_out.at(b, 0))
                sp.dma_start(res[:], xv[b]).then_inc(s.res_in.sem, 16)
                if cross:
                    refill(b, 2)
                    refill(b, 3)
                if more:
                    refill((b, 1), 0)
                    refill((b, 1), 1)
                sp.wait_ge(s.y_free.sem, s.y_free.at(b, TT))
                sp.dma_start(yv[b], res[:]).then_inc(s.x_out.sem, 16)

            load(0, 0)
            refill(0, 0)
            refill(0, 1)
            with sp.Fori(0, B - 1) as b:
                batch(b, True)
            batch(B - 1, False)
            sp.wait_ge(s.x_out.sem, s.x_out.at(B, 0))

        @block.tensor
        def _(pe):
            pe.wait_ge(s.w_lo.sem, s.w_lo.at(0, nchunks))
            pe.wait_ge(s.const.sem, s.const.at(0, 2))

            def batch(b, events):
                def scores(r, g, c, j):
                    i = (g * a.pairs + c) * HG + j
                    if c == 0 and j in (0, 2):
                        pe.wait_ge(s.shift_free.sem, s.shift_free.at(r, 2 * g + j // 2 + 1))
                    pe.wait_ge(s.s_free.sem, s.s_free.at(r, i - 1))
                    for k in range(2):
                        kt = 2 * c + k
                        mm = pe.matmul(ps_s[0:a.kp, i % 2, k * N:(k + 1) * N],
                                       kstack(g, j, STACKM, kt * a.kp, (kt + 1) * a.kp),
                                       qstack(g, j, STACKM, 0, N), start=True, stop=True)
                    mm.then_inc(s.s_full.sem, 1)

                def values(r, g, c):
                    i = g * a.pairs + c
                    if c == 0:
                        pe.wait_ge(s.a_flat.sem, s.a_flat.at(r, g))
                    pe.wait_ge(s.s_free.sem, s.s_free.at(r, (i + 1) * HG))
                    for k in range(2):
                        for j in range(HG):
                            kt = 2 * c + k
                            h = g * HG + j
                            mm = pe.matmul(ps_o[HD * j:HD * (j + 1), 0:N], vt[:, kt, HD * h:HD * (h + 1)],
                                           pt[:, i % 2, j, k, :], start=(kt == 0), stop=(kt == a.tiles - 1))
                    mm.then_inc(s.av_done.sem, 1)

                def sums(r, g):
                    pe.wait_ge(s.e_sum.sem, s.e_sum.at(r, (g + 1) * (2 * a.pairs - 1)))
                    for j in range(HG):
                        mm = pe.matmul(ps_o[HD * j:HD * (j + 1), N:2 * N], t.ones[0:a.kp, 0:HD], es[:, j, :],
                                       start=True, stop=True)
                    mm.then_inc(s.sum_done.sem, 1)

                def maxima(r, g, u):
                    i = g * a.mu + u
                    slot, fill = (g % 2, g // 2 + 1) if cross else (g // 2, 1)
                    if u == 0:
                        pe.wait_ge((s.fill0, s.fill1)[slot].sem, (s.fill0, s.fill1)[slot].at(r, 16 * dmas * fill))
                    pe.wait_ge(s.max_free.sem, s.max_free.at(r, i - 1))
                    if cross:
                        j, q, c0 = u // 4, u // 2 % 2, (0, NC - 376)[u % 2]
                        mm = pe.matmul(ps_max[0:TP, i % 2, 0:376], qstack(g, j, STACK, q * TP, (q + 1) * TP),
                                       kstack(g, j, STACK, c0, c0 + 376), start=True, stop=True)
                    else:
                        for q in range(TT):
                            mm = pe.matmul(ps_max[0:TP, i % 2, q * N:(q + 1) * N],
                                           qstack(g, u, STACK, q * TP, (q + 1) * TP),
                                           kstack(g, u, STACK, 0, N), start=True, stop=True)
                    mm.then_inc(s.max_full.sem, 1)

                def shifts(r, g, half):
                    pe.wait_ge(s.m_ready.sem, s.m_ready.at(r, 2 * g + half + 1))
                    pe.wait_ge(s.shift_free.sem, s.shift_free.at(r, 2 * g + half))
                    for j in (2 * half, 2 * half + 1):
                        for q in range(TT):
                            c0 = (j % 2) * N + q * TP
                            mm = pe.matmul(ps_shift[STACK:STACKM, c0:c0 + TP], mhl[:, j, q, :],
                                           t.ident_bf[0:TP, 0:TP], start=True, stop=True)
                    mm.then_inc(s.shift_full.sem, 1)

                for db, e, bank, user in events:
                    kind, r = e[0], (b, db)
                    if user is not None and (kind not in ("f", "v") or e[-1] == 0):
                        db0, e0 = user
                        pe.wait_ge(free[e0[0]].sem, free[e0[0]].at((b, db0), a.nth(e0) + 1))
                    to = wk[:, bank, :] if bank is not None else None
                    if kind == "ctx":
                        k, half = e[1] // 2, e[1] % 2
                        if e[1] == 0:
                            pe.wait_ge(s.cn_ready.sem, s.cn_ready.at(r, 6)) if biased else pe.wait_ge(s.ctx_in.sem, s.ctx_in.at(r, 16))
                        for i in range(3):
                            mm = pe.transpose(to[:, i * 125:(i + 1) * 125], craw[:, 3 * half + i, k * P:(k + 1) * P],
                                              t.ident[0:125, 0:125])
                        mm.then_inc(s.ctx_full.sem, 1)
                    elif kind == "x":
                        if e[1] == 0:
                            pe.wait_ge(s.xn_ready.sem, s.xn_ready.at(r, TT))
                        for k in range(2):
                            for i in range(TT):
                                c0 = k * N + i * TP
                                kk = 2 * e[1] + k
                                mm = pe.transpose(to[:, c0:c0 + TP], xa[:, i, kk * P:(kk + 1) * P],
                                                  t.ident[0:TP, 0:TP])
                        mm.then_inc(s.x_full.sem, 1)
                    elif kind == "f":
                        _, g, u, k = e
                        isq = u == a.fu - 1
                        if k == 0 and (isq or not cross):
                            pe.wait_ge(s.xm_lo.sem, s.xm_lo.at(r, KT))
                        elif k == 0:
                            pe.wait_ge(s.ctx_free.sem, s.ctx_free.at(r, 8))
                        wh, wl = W["wq" if isq else "wk"]
                        c0, c1 = (0, N) if isq else a.kcols[u]
                        sh, sl = (xh, xl) if isq else (kvh, kvl)
                        c = slice(g * P, (g + 1) * P)
                        mm = three_passes(pe, to[:, 0:c1 - c0], wh[:, k, c], wl[:, k, c],
                                          sh[:, k, c0:c1], sl[:, k, c0:c1], k == 0, k == KT - 1)
                        if k == KT - 1:
                            mm.then_inc(s.f_full.sem, 1)
                    elif kind == "v":
                        _, i, k = e
                        if k == 0:
                            pe.wait_ge(s.ctx_free.sem, s.ctx_free.at(r, 8)) if cross else pe.wait_ge(s.xm_lo.sem, s.xm_lo.at(r, KT))
                        wh, wl = W["wv"]
                        c = slice(i * a.kp, (i + 1) * a.kp)
                        mm = three_passes(pe, to[0:a.kp, :], kvh[:, k, c], kvl[:, k, c],
                                          wh[:, k, :], wl[:, k, :], k == 0, k == KT - 1)
                        if k == KT - 1:
                            mm.then_inc(s.v_full.sem, 1)
                    elif kind == "y":
                        i = e[1]
                        pe.wait_ge(s.a_lo.sem, s.a_lo.at(r, NG))
                        wh, wl = W["wo"]
                        for k in range(KT):
                            c = slice(i * TP, (i + 1) * TP)
                            mm = three_passes(pe, to[0:TP, :], ah[:, k, c], al[:, k, c],
                                              wh[:, k, :], wl[:, k, :], k == 0, k == KT - 1)
                        mm.then_inc(s.y_full.sem, 1)
                    elif kind == "s":
                        scores(r, *e[1:])
                    elif kind == "a":
                        if e[1] == 0:
                            pe.wait_ge(s.v_free.sem, s.v_free.at(r, 2 * e[2] + 2))
                        values(r, e[1], e[2])
                    elif kind == "m":
                        maxima(r, e[1], e[2])
                    elif kind == "t":
                        shifts(r, e[1], e[2])
                    elif kind == "o":
                        sums(r, e[1])

            batch(0, a.prologue)
            for db, e in a.rest:
                pe.wait_ge(free[e[0]].sem, free[e[0]].at(0, a.nth(e) + 1))
            with pe.Fori(0, B - 1) as b:
                batch(b, a.body)
            batch(B - 1, a.last)

        @block.vector
        def _(dve):
            stack = stk[STACK:STACKM].rearrange("p a h n -> p (a h n)") if cross else \
                st2[STACK:STACKM, :, 0].rearrange("p a h g n -> p a (h g n)")
            dve.memset(f32(stack), -1.0).then_inc(s.const.sem, 2)
            weights_vector(dve, s, chunks, stage)
            dve.wait_ge(s.c_in.sem, s.c_in.at(0, 96))

            def batch(b, events):
                for db, e, bank, user in events:
                    kind, r = e[0], (b, db)
                    if bank is not None and (kind not in ("f", "v") or e[-1] == KT - 1):
                        dve.wait_ge(full[kind].sem, full[kind].at(r, a.nth(e) + 1))
                        fr = wk[:, bank, :]
                    if kind == "cln" and biased:
                        dve.wait_ge(s.ctx_in.sem, s.ctx_in.at(r, 16))
                        ln_vector_stats(dve, s, r, craw, cst, cmv, 6, t.pad, s.cstats, s.cvar)
                        ln_vector_apply(dve, s, r, craw, cmv, crs, 6, s.crstd, s.cn_ready)
                    elif kind == "ln":
                        dve.wait_ge(s.x_in.sem, s.x_in.at(r, 16))
                        ln_vector_stats(dve, s, r, xa, stt[0:TP], mv[0:TP], TT, t.pad, s.stats, s.ln_var)
                        ln_vector_apply(dve, s, r, xa, mv[0:TP], rs[0:TP, :, 0:TT], TT, s.rstd, s.xn_ready)
                    elif kind == "ctx":
                        k, half = e[1] // 2, e[1] % 2
                        c = slice(375 * half, 375 * half + 375)
                        dve.wait_ge(s.cx_hi.sem, s.cx_hi.at(r, e[1] + 1))
                        dve.tensor_tensor(cl[:, k, c], fr[:, 0:375], f32(ch[:, k, c]), ALU.subtract).then_inc(s.ctx_free.sem, 1)
                    elif kind == "x":
                        for kk in range(2):
                            k = 2 * e[1] + kk
                            dve.wait_ge(s.xm_lo.sem, s.xm_lo.at(r, k - 1))
                            dve.tensor_scalar(xm[:, k % 2, :], fr[:, kk * N:(kk + 1) * N],
                                                   t.mod[:, ln, 0, k, bass.ds(b + db, 1)], t.mod[:, ln, 1, k, bass.ds(b + db, 1)],
                                                   ALU.mult, ALU.add).then_inc((s.xm_ready, s.x_free)[kk].sem, 1)
                    elif kind == "f" and e[-1] == KT - 1:
                        _, g, u, _ = e
                        n = a.nth(e)
                        isq = u == a.fu - 1
                        w = f_width(u)
                        c0 = 0 if isq else a.kcols[u][0]
                        dve.wait_ge(s.f_lo.sem, s.f_lo.at(r, n - 1))
                        if a.rope:
                            dve.tensor_tensor(fa[:, n % 2, 0:w], fr[:, 0:w], cos[:, c0:c0 + w], ALU.mult).then_inc(s.f_cos.sem, 1)
                            dve.stream_shuffle(fs[:, n % 2, 0:w], fr[:, 0:w], SWAP).then_inc(s.f_free.sem, 1)
                        else:
                            bias = (bq if isq else bk)[:, g:g + 1]
                            dve.tensor_scalar(fa[:, n % 2, 0:w], fr[:, 0:w], bias, None, ALU.add).then_inc(s.f_free.sem, 1)
                    elif kind == "v" and e[-1] == KT - 1:
                        i = e[1]
                        dve.wait_ge(s.av_done.sem, s.av_done.at(r, i // 2 + 1 - a.pairs))
                        if biased:
                            op = dve.tensor_tensor(vt[:, i, :], fr[0:a.kp, :], bv[0:a.kp, :], ALU.add)
                        else:
                            op = dve.tensor_copy(vt[:, i, :], fr[0:a.kp, :])
                        op.then_inc(s.v_free.sem, 1)
                    elif kind == "m":
                        _, g, u = e
                        i = g * a.mu + u
                        dve.wait_ge(s.max_full.sem, s.max_full.at(r, i + 1))
                        half, nth = 2 * u // a.mu, 2 * g + 2 * u // a.mu
                        last = (u + 1) % (a.mu // 2) == 0
                        if cross:
                            dve.tensor_reduce(mx2[:, u // 4, u // 2 % 2, u % 2:u % 2 + 1], ps_max[0:TP, i % 2, 0:376], AX.X,
                                              ALU.max).then_inc(s.max_free.sem, 1)
                        else:
                            dve.tensor_reduce(mx[:, u, :], ps_max[0:TP, i % 2, 0:2 * N].rearrange("p (a n) -> p a n", a=2),
                                              AX.X, ALU.max).then_inc(s.max_free.sem, 1)
                        if last:
                            hs = slice(2 * half, 2 * half + 2)
                            dve.wait_ge(s.max_free.sem, s.max_free.at(r, i + 1))
                            if cross:
                                dve.tensor_tensor(mx[:, hs, :], mx2[:, hs, :, 0], mx2[:, hs, :, 1], ALU.max).then_inc(s.m_rows.sem, 1)
                                dve.wait_ge(s.m_rows.sem, s.m_rows.at(r, nth + 1))
                            dve.wait_ge(s.shift_full.sem, s.shift_full.at(r, nth - 1))
                            dve.tensor_copy(mhl[:, hs, :, 0], mx[:, hs, :]).then_inc(s.m_top.sem, 1)
                            dve.wait_ge(s.m_top.sem, s.m_top.at(r, nth + 1))
                            dve.tensor_tensor(mhl[:, hs, :, 1], mx[:, hs, :], mhl[:, hs, :, 0], ALU.subtract).then_inc(s.m_ready.sem, 1)
                    elif kind == "e" and e[2] == a.pairs - 1:
                        sum_pair(dve, r, e[1], e[2])
                    elif kind == "o":
                        g = e[1]
                        dve.wait_ge(s.sum_done.sem, s.sum_done.at(r, g + 1))
                        dve.wait_ge(s.a_lo.sem, s.a_lo.at(r, g))
                        dve.reciprocal(rec[:], ps_o[:, N:2 * N]).then_inc(s.a_rec.sem, 1)
                        dve.wait_ge(s.a_rec.sem, s.a_rec.at(r, g + 1))
                        dve.tensor_tensor(af[:], ps_o[:, 0:N], rec[:], ALU.mult).then_inc(s.a_flat.sem, 1)
                    elif kind == "y":
                        i = e[1]
                        if i == 0:
                            dve.wait_ge(s.res_in.sem, s.res_in.at(r, 16))
                            if gated:
                                dve.wait_ge(s.gate_in.sem, s.gate_in.at(r, 16))
                        y = fr[0:TP, :]
                        if biased:
                            dve.wait_ge(s.y_free.sem, s.y_free.at(r, i))
                            dve.tensor_tensor(ym[:], y, bo[0:TP, :], ALU.add).then_inc(s.y_mid.sem, 1)
                            dve.wait_ge(s.y_mid.sem, s.y_mid.at(r, i + 1))
                            y = ym[:]
                            if gated:
                                dve.tensor_tensor(ym[:], ym[:], gate[:], ALU.mult).then_inc(s.y_gate.sem, 1)
                                dve.wait_ge(s.y_gate.sem, s.y_gate.at(r, i + 1))
                        dve.tensor_tensor(res[:, i, :], res[:, i, :], y, ALU.add).then_inc(s.y_free.sem, 1)

            batch(0, a.prologue)
            with dve.Fori(0, B - 1) as b:
                batch(b, a.body)
            batch(B - 1, a.last)

        @block.scalar
        def _(act):
            weights_scalar(act, s, chunks, stage)

            def batch(b, events):
                for db, e, bank, user in events:
                    kind, r = e[0], (b, db)
                    if kind == "ctx":
                        k, half = e[1] // 2, e[1] % 2
                        c = slice(375 * half, 375 * half + 375)
                        act.wait_ge(s.ctx_full.sem, s.ctx_full.at(r, e[1] + 1))
                        if e[1] == 0:
                            act.wait_ge(s.f_full.sem, s.f_full.at(r, 0))
                            act.wait_ge(s.v_full.sem, s.v_full.at(r, 0))
                        act.activation(ch[:, k, c], wk[:, bank, 0:375], ACT.Copy).then_inc(s.cx_hi.sem, 1)
                    elif kind == "x":
                        for kk in range(2):
                            k = 2 * e[1] + kk
                            if kk == 0:
                                act.wait_ge(s.xm_ready.sem, s.xm_ready.at(r, e[1] + 1))
                            else:
                                act.wait_ge(s.x_free.sem, s.x_free.at(r, e[1] + 1))
                            act.activation(xh[:, k, :], xm[:, k % 2, :], ACT.Copy).then_inc(s.xm_hi.sem, 1)
                    elif kind == "h":
                        _, g, u = e
                        n = a.nth(("f", g, u))
                        if cross:
                            if u == 0:
                                prev = g - 1 if g else 3
                                filled = (s.fill0, s.fill1)[prev % 2]
                                act.wait_ge(filled.sem, filled.at(r, 16 * dmas * (prev // 2 + 1) - (0 if g else 16 * dmas * a.fills)))
                        elif g % 2 == 0 and u == 0:
                            act.wait_ge((s.fill0, s.fill1)[g // 2].sem, (s.fill0, s.fill1)[g // 2].at(r, 0))
                        act.wait_ge(s.f_flat.sem, s.f_flat.at(r, n + 1)) if a.rope else act.wait_ge(s.f_free.sem, s.f_free.at(r, n + 1))
                        act.activation(f_dst(g, u, 0), fa[:, n % 2, 0:f_width(u)], ACT.Copy).then_inc(s.f_hi.sem, 1)
                    elif kind == "t":
                        _, g, half = e
                        act.wait_ge(s.shift_full.sem, s.shift_full.at(r, 2 * g + half + 1))
                        q = stk[STACK:STACKM, g % 2, 2 * half:2 * half + 2, NC:] if cross else \
                            st2[STACK:STACKM, g // 2, 1, 2 * half:2 * half + 2, g % 2, :]
                        act.activation(q, ps_shift[STACK:STACKM, 0:2 * N].rearrange("p (a n) -> p a n", a=2),
                                       ACT.Copy).then_inc(s.shift_free.sem, 1)
                    elif kind == "s":
                        _, g, c, j = e
                        cs = g * a.pairs + c
                        i = cs * HG + j
                        act.wait_ge(s.s_full.sem, s.s_full.at(r, i + 1))
                        if j == 0:
                            act.wait_ge(s.av_done.sem, s.av_done.at(r, cs - 1))
                            act.wait_ge(s.e_sum.sem, s.e_sum.at(r, e_count(cs - 1)))
                        act.activation(pt[:, cs % 2, j, :, :],
                                       ps_s[0:a.kp, i % 2, 0:2 * N].rearrange("p (a n) -> p a n", a=2),
                                       ACT.Exp, scale=SCALE).then_inc(s.s_free.sem, 1)
                    elif kind == "d":
                        g = e[1]
                        act.wait_ge(s.a_flat.sem, s.a_flat.at(r, g + 1))
                        act.activation(ah[:, g, :], af[:], ACT.Copy).then_inc(s.a_hi.sem, 1)

            batch(0, a.prologue)
            with act.Fori(0, B - 1) as b:
                batch(b, a.body)
            batch(B - 1, a.last)

        @block.gpsimd
        def _(pool):
            def batch(b, events):
                for db, e, bank, user in events:
                    kind, r = e[0], (b, db)
                    if kind == "cln" and biased:
                        ln_pool_rstd(pool, s, r, cmv, crs, t.eps[0:125, 1, 0:6], t.neghalf[0:125, 0:6], 6, s.cvar, s.crstd)
                    elif kind == "ln":
                        ln_pool_rstd(pool, s, r, mv[0:TP, 0:TT], rs[0:TP, :, 0:TT], t.eps[0:TP, layer, 0:TT],
                                     t.neghalf[0:TP, 0:TT], TT, s.ln_var, s.rstd)
                    elif kind == "x":
                        for kk in range(2):
                            k = 2 * e[1] + kk
                            pool.wait_ge(s.xm_hi.sem, s.xm_hi.at(r, k + 1))
                            pool.tensor_tensor(xl[:, k, :], xm[:, k % 2, :], f32(xh[:, k, :]), ALU.subtract).then_inc(s.xm_lo.sem, 1)
                    elif kind == "f" and a.rope and e[-1] == KT - 1:
                        _, g, u, _ = e
                        n = a.nth(e)
                        w = f_width(u)
                        c0 = 0 if u == a.fu - 1 else a.kcols[u][0]
                        pool.wait_ge(s.f_free.sem, s.f_free.at(r, n + 1))
                        pool.tensor_tensor(fs[:, n % 2, 0:w], fs[:, n % 2, 0:w], sin[:, c0:c0 + w], ALU.mult).then_inc(s.f_sin.sem, 1)
                        pool.wait_ge(s.f_sin.sem, s.f_sin.at(r, n + 1))
                        pool.tensor_tensor(fa[:, n % 2, 0:w], fa[:, n % 2, 0:w], fs[:, n % 2, 0:w], ALU.add).then_inc(s.f_flat.sem, 1)
                    elif kind == "h":
                        _, g, u = e
                        n = a.nth(("f", g, u))
                        pool.wait_ge(s.f_hi.sem, s.f_hi.at(r, n + 1))
                        pool.tensor_tensor(f_dst(g, u, 1), fa[:, n % 2, 0:f_width(u)], f32(f_dst(g, u, 0)), ALU.subtract).then_inc(s.f_lo.sem, 1)
                    elif kind == "e" and e[2] != a.pairs - 1:
                        sum_pair(pool, r, e[1], e[2])
                    elif kind == "d":
                        g = e[1]
                        pool.wait_ge(s.a_hi.sem, s.a_hi.at(r, g + 1))
                        pool.tensor_tensor(al[:, g, :], af[:], f32(ah[:, g, :]), ALU.subtract).then_inc(s.a_lo.sem, 1)

            batch(0, a.prologue)
            with pool.Fori(0, B - 1) as b:
                batch(b, a.body)
            batch(B - 1, a.last)
    s.close(ONCE, B)



def feed_forward(nc, s, t, io, layer, x_src, x_dst):
    ln = 3 * layer + 2
    PB = 2
    T4 = PB * TT
    M = PB * N
    FC = FF // P
    gated = layer == 1
    LAG = 2
    HS = 3
    with ExitStack() as ctx:
        def sb(name, shape, dt=F32):
            return ctx.enter_context(nc.sbuf_tensor(f"f{layer}_{name}", shape, dt))

        w1 = (sb("w1_hi", [P, KT, FF], F32R), sb("w1_lo", [P, KT, FF], F32R))
        w2 = (sb("w2_hi", [P, FC, D], F32R), sb("w2_lo", [P, FC, D], F32R))
        chunks = weight_chunks(io[f"f{layer}_w1"], *w1) + weight_chunks(io[f"f{layer}_w2"], *w2)
        stage = sb("stage", [P, 2, CHUNK])
        xa, res = sb("xa", [TP, T4, D]), sb("res", [TP, T4, D])
        stt, mv, rs = sb("st", [TP, T4, 6]), sb("mv", [TP, T4, 2]), sb("rs", [TP, 2, T4])
        xm = sb("xm", [P, 2, M])
        xh, xl = sb("xh", [P, KT, M], F32R), sb("xl", [P, KT, M], F32R)
        hf = sb("hf", [P, 2, M])
        hh, hl = sb("hh", [P, HS, M], F32R), sb("hl", [P, HS, M], F32R)
        b1 = sb("b1_col", [P, FC])
        b2 = sb("b2_all", [TP, D])
        ym = sb("ym", [TP, D])
        gate = sb("gate", [TP, PB, D]) if gated else None
        ps_u = ctx.enter_context(nc.psum_tensor(f"f{layer}_u", [P, 3, 512], F32))
        ps_t = ctx.enter_context(nc.psum_tensor(f"f{layer}_t", [P, 512], F32))
        ps_y = ctx.enter_context(nc.psum_tensor(f"f{layer}_y", [P, T4, 512], F32))

        R = B // PB
        s.plan(**weights_plan(chunks), c_in=32, x_in=16, res_in=16, gate_in=16 * PB * gated, x_out=16,
             stats=T4, ln_var=T4, rstd=2, xn_ready=T4, tr_full=KT, xm_ready=KT, tr_free=KT, xm_hi=KT, xm_lo=KT,
             up_full=FC, g_flat=FC, g_hi=FC, g_lo=FC, down_done=FC - 1, y_full=T4, y_mid=T4, y_gate=T4 * gated, y_ready=T4)
        xv = x_src.rearrange("(r b) (t p) d -> r p (b t) d", p=TP, b=PB)
        yv = x_dst.rearrange("(r b) (t p) d -> r p (b t) d", p=TP, b=PB)
        block = ctx.enter_context(nc.Block())

        @block.sync
        def _(sp):
            sp.dma_start(b1[:], io[f"f{layer}_b1"]).then_inc(s.c_in.sem, 16)
            sp.dma_start(b2[:], io[f"f{layer}_b2"].partition_broadcast(TP)).then_inc(s.c_in.sem, 16)
            weights_sync(sp, s, chunks, stage)
            with sp.Fori(0, R) as r:
                sp.wait_ge(s.tr_full.sem, s.tr_full.at(r, 0))
                sp.dma_start(xa[:], xv[r]).then_inc(s.x_in.sem, 16)
                if gated:
                    sp.wait_ge(s.y_gate.sem, s.y_gate.at(r, 0))
                    for i in range(PB):
                        sp.dma_start(gate[:, i, :], io["gates"][1, PB * r + i].partition_broadcast(TP)).then_inc(s.gate_in.sem, 16)
                sp.wait_ge(s.x_out.sem, s.x_out.at(r, 0))
                sp.dma_start(res[:], xv[r]).then_inc(s.res_in.sem, 16)
                sp.wait_ge(s.y_ready.sem, s.y_ready.at(r, T4))
                sp.dma_start(yv[r], res[:]).then_inc(s.x_out.sem, 16)
            sp.wait_ge(s.x_out.sem, s.x_out.at(R, 0))

        @block.tensor
        def _(pe):
            pe.wait_ge(s.w_lo.sem, s.w_lo.at(0, len(chunks)))
            with pe.Fori(0, R) as r:
                pe.wait_ge(s.xn_ready.sem, s.xn_ready.at(r, T4))
                for k in range(KT):
                    pe.wait_ge(s.tr_free.sem, s.tr_free.at(r, k))
                    for i in range(T4):
                        mm = pe.transpose(ps_t[:, i * TP:(i + 1) * TP], xa[:, i, k * P:(k + 1) * P], t.ident[0:TP, 0:TP])
                    mm.then_inc(s.tr_full.sem, 1)
                pe.wait_ge(s.xm_lo.sem, s.xm_lo.at(r, KT))

                def up(f):
                    pe.wait_ge(s.g_flat.sem, s.g_flat.at(r, f - 2))
                    for k in range(KT):
                        c = slice(f * P, (f + 1) * P)
                        mm = three_passes(pe, ps_u[:, f % 3, 0:M], w1[0][:, k, c], w1[1][:, k, c],
                                          xh[:, k, :], xl[:, k, :], k == 0, k == KT - 1)
                    mm.then_inc(s.up_full.sem, 1)

                def down(f):
                    pe.wait_ge(s.g_lo.sem, s.g_lo.at(r, f + 1))
                    if f == 0:
                        pe.wait_ge(s.y_ready.sem, s.y_ready.at(r, 0))
                    for i in range(T4):
                        c = slice(i * TP, (i + 1) * TP)
                        mm = three_passes(pe, ps_y[0:TP, i, :], hh[:, f % HS, c], hl[:, f % HS, c],
                                          w2[0][:, f, :], w2[1][:, f, :], f == 0, f == FC - 1)
                        if f == FC - 1:
                            mm.then_inc(s.y_full.sem, 1)
                    if f < FC - 1:
                        mm.then_inc(s.down_done.sem, 1)

                for f in range(FC + LAG):
                    if f < FC:
                        up(f)
                    if f >= LAG:
                        down(f - LAG)

        @block.vector
        def _(dve):
            weights_vector(dve, s, chunks, stage)
            dve.wait_ge(s.c_in.sem, s.c_in.at(0, 32))
            with dve.Fori(0, R) as r:
                dve.wait_ge(s.x_in.sem, s.x_in.at(r, 16))
                ln_vector_stats(dve, s, r, xa, stt, mv, T4, t.pad, s.stats, s.ln_var)
                ln_vector_apply(dve, s, r, xa, mv, rs, T4, s.rstd, s.xn_ready)
                for k in range(KT):
                    dve.wait_ge(s.tr_full.sem, s.tr_full.at(r, k + 1))
                    dve.wait_ge(s.xm_lo.sem, s.xm_lo.at(r, k - 1))
                    for i in range(PB):
                        c = slice(i * N, (i + 1) * N)
                        dve.tensor_scalar(xm[:, k % 2, c], ps_t[:, c], t.mod[:, ln, 0, k, bass.ds(r * PB + i, 1)],
                                          t.mod[:, ln, 1, k, bass.ds(r * PB + i, 1)], ALU.mult, ALU.add).then_inc((s.xm_ready, s.tr_free)[i].sem, 1)
                for f in range(FC):
                    dve.wait_ge(s.g_hi.sem, s.g_hi.at(r, f + 1))
                    dve.tensor_tensor(hl[:, f % HS, :], hf[:, f % 2, :], f32(hh[:, f % HS, :]), ALU.subtract).then_inc(s.g_lo.sem, 1)
                dve.wait_ge(s.res_in.sem, s.res_in.at(r, 16))
                if gated:
                    dve.wait_ge(s.gate_in.sem, s.gate_in.at(r, 16 * PB))
                for i in range(T4):
                    dve.wait_ge(s.y_full.sem, s.y_full.at(r, i + 1))
                    dve.wait_ge(s.y_ready.sem, s.y_ready.at(r, i))
                    dve.tensor_tensor(ym[:], ps_y[0:TP, i, :], b2[:], ALU.add).then_inc(s.y_mid.sem, 1)
                    dve.wait_ge(s.y_mid.sem, s.y_mid.at(r, i + 1))
                    if gated:
                        dve.tensor_tensor(ym[:], ym[:], gate[:, i // TT, :], ALU.mult).then_inc(s.y_gate.sem, 1)
                        dve.wait_ge(s.y_gate.sem, s.y_gate.at(r, i + 1))
                    dve.tensor_tensor(res[:, i, :], res[:, i, :], ym[:], ALU.add).then_inc(s.y_ready.sem, 1)

        @block.scalar
        def _(act):
            weights_scalar(act, s, chunks, stage)
            act.wait_ge(s.c_in.sem, s.c_in.at(0, 32))
            with act.Fori(0, R) as r:
                for k in range(KT):
                    act.wait_ge(s.tr_free.sem, s.tr_free.at(r, k + 1))
                    act.activation(xh[:, k, :], xm[:, k % 2, :], ACT.Copy).then_inc(s.xm_hi.sem, 1)
                for f in range(FC):
                    act.wait_ge(s.up_full.sem, s.up_full.at(r, f + 1))
                    act.wait_ge(s.g_lo.sem, s.g_lo.at(r, f - 1))
                    act.activation(hf[:, f % 2, :], ps_u[:, f % 3, 0:M], (ACT.Gelu, ACT.Gelu_apprx_tanh)[layer],
                                   bias=b1[:, f:f + 1]).then_inc(s.g_flat.sem, 1)
                    act.wait_ge(s.g_flat.sem, s.g_flat.at(r, f + 1))
                    if f < HS:
                        act.wait_ge(s.y_full.sem, s.y_full.at(r, 0))
                    else:
                        act.wait_ge(s.down_done.sem, s.down_done.at(r, f - HS + 1))
                    act.activation(hh[:, f % HS, :], hf[:, f % 2, :], ACT.Copy).then_inc(s.g_hi.sem, 1)

        @block.gpsimd
        def _(pool):
            with pool.Fori(0, R) as r:
                ln_pool_rstd(pool, s, r, mv, rs, t.eps[0:TP, layer, 0:T4], t.neghalf[0:TP, 0:T4], T4, s.ln_var, s.rstd)
                for k in range(KT):
                    pool.wait_ge(s.xm_hi.sem, s.xm_hi.at(r, k + 1))
                    pool.tensor_tensor(xl[:, k, :], xm[:, k % 2, :], f32(xh[:, k, :]), ALU.subtract).then_inc(s.xm_lo.sem, 1)
    s.close(ONCE, R)


class Tables:

    def __init__(self, nc, ctx):
        def sb(name, shape, dt=F32):
            return ctx.enter_context(nc.sbuf_tensor(name, shape, dt))
        self.ident = sb("ident", [P, P])
        self.ident_bf = sb("ident_bf", [P, P], BF16)
        self.ones = sb("ones", [P, HD])
        self.neghalf = sb("neghalf", [P, 8])
        self.eps = sb("eps", [P, 2, 8])
        self.pad = sb("pad", [P, 2])
        self.mod = sb("mod", [P, 6, 2, KT, B])


def build(nc, io):
    with ExitStack() as ctx:
        s = Signals(nc, ctx)
        t = Tables(nc, ctx)
        with nc.Block() as block:
            @block.sync
            def _(sp):
                for x in s.all.values():
                    sp.sem_inc(x.sem, CREDIT)
        modulation(nc, s, t, io)
        x = io["x"]
        for layer in range(2):
            attention_phase(nc, s, t, io, False, layer, x, io["x1"])
            attention_phase(nc, s, t, io, True, layer, io["x1"], io["x2"])
            x = io["x3"] if layer == 0 else io["out"]
            feed_forward(nc, s, t, io, layer, io["x2"], x)


def rope_tables():
    half = HD // 2
    inv = (np.float32(1.0) / np.float32(10000.0) ** (np.arange(half, dtype=np.float32) / np.float32(half))).astype(np.float32)
    ang = (np.arange(NC, dtype=np.float32)[:, None] * inv[None, :]).astype(np.float32)
    c, s = np.cos(ang).T.astype(np.float32), np.sin(ang).T.astype(np.float32)
    return np.tile(np.concatenate([c, c]), (HG, 1)), np.tile(np.concatenate([-s, s]), (HG, 1))


def kernel(**inputs):
    import concourse.bacc as bacc
    from concourse.bass_utils import run_bass_kernel_spmd

    g = {k: np.asarray(v) for k, v in inputs.items()}
    l0 = {k[9:]: v for k, v in g.items() if k.startswith("L0_xcond_")}
    l1 = {k[9:]: v for k, v in g.items() if k.startswith("L1_xcond_")}
    cos, sin = rope_tables()
    arrays = dict(
        x=g["x"], ctx=g["ctx_1024"], condT=g["cond_1024"].T, cos=cos, sin=sin,
        ln1_w=l0["ln1_w"].T, ln2_w=l0["ln2_w"].T, ln3_w=l0["ln3_w"].T, W_mod=l1["W_mod"],
        ln1_b=l0["ln1_b"], ln2_b=l0["ln2_b"], ln3_b=l0["ln3_b"], b_mod=l1["b_mod"],
        s0_qkv=l0["qkv_w"].T, s0_wo=l0["sa_out_w"].T,
        c0_wq=l0["q_w"].T, c0_wk=l0["k_w"].T, c0_wv=l0["v_w"].T, c0_wo=l0["ca_out_w"].T,
        f0_w1=l0["ffn_w1"].T, f0_b1=l0["ffn_b1"], f0_w2=l0["ffn_w2"].T, f0_b2=l0["ffn_b2"],
        s1_qkv=l1["W_qkv"], s1_wo=l1["W_proj"],
        s_bq=l1["b_qkv"][0:D], s_bk=l1["b_qkv"][D:2 * D], s_bv=l1["b_qkv"][2 * D:3 * D], s_bo=l1["b_proj"],
        c1_wq=l1["W_qc"], c1_wk=l1["W_kvc"][:, 0:D], c1_wv=l1["W_kvc"][:, D:2 * D], c1_wo=l1["W_cproj"],
        c_bq=l1["b_qc"], c_bk=l1["b_kvc"][0:D], c_bv=l1["b_kvc"][D:2 * D], c_bo=l1["b_cproj"],
        f1_w1=l1["W_mlp1"], f1_b1=l1["b_mlp1"], f1_w2=l1["W_mlp2"], f1_b2=l1["b_mlp2"],
    )
    for k in ("f0_b1", "f1_b1", "s_bq", "s_bk", "c_bq", "c_bk"):
        arrays[k] = arrays[k].reshape(-1, P).T
    arrays = {k: np.ascontiguousarray(v) for k, v in arrays.items()}
    nc = bacc.Bacc("TRN2", target_bir_lowering=False, num_devices=1)
    io = {k: nc.dram_tensor(k, v.shape, F32, kind="ExternalInput").ap() for k, v in arrays.items()}
    io["out"] = nc.dram_tensor("out", (B, N, D), F32, kind="ExternalOutput").ap()
    for k in ("x1", "x2", "x3"):
        io[k] = nc.dram_tensor(k, (B, N, D), F32, kind="Internal").ap()
    io["gates"] = nc.dram_tensor("gates", (2, B, D), F32, kind="Internal").ap()
    build(nc, io)
    r = run_bass_kernel_spmd(nc, [arrays], core_ids=[0])
    return r.results[0]["out"]
```

```python
from contextlib import ExitStack

import numpy as np

import concourse.bass as bass
from concourse import mybir

F32 = mybir.dt.float32
F32R = mybir.dt.float32r
BF16 = mybir.dt.bfloat16
ALU = mybir.AluOpType
ACT = mybir.ActivationFunctionType
AX = mybir.AxisListType

B, N, D = 8, 224, 512
NC = 750
H, HD = 16, 32
FF = 2048
P = 128
KT = D // P
TT, TP = 2, 112
HG = P // HD
NG = H // HG
SCALE = HD ** -0.5
STACK = 3 * HD
STACKM = STACK + 2
CHUNK = 1024
SLOTS = 6
SWAP = [(i + HD // 2) % HD for i in range(HD)]
CREDIT = 16


class Tally:

    def __init__(self, sem):
        self.sem, self.base, self.per = sem, CREDIT, 0

    def at(self, rnd, n):
        rnd, ahead = rnd if isinstance(rnd, tuple) else (rnd, 0)
        return rnd * self.per + (self.base + ahead * self.per + n)


class Signals:

    def __init__(self, nc, ctx):
        def new(name):
            self.all[name] = Tally(ctx.enter_context(nc.semaphore(name)))
            return self.all[name]

        self.all = {}
        self.const = new("const")
        self.c_in = new("c_in")
        self.c_silu = new("c_silu")
        self.m_raw0 = new("m_raw0")
        self.m_raw1 = new("m_raw1")
        self.tr_full = new("tr_full")
        self.tr_free = new("tr_free")
        self.mod_rows = new("mod_rows")
        self.gates_out = new("gates_out")
        self.w_raw = [new(f"w_raw{i}") for i in range(SLOTS)]
        self.w_hi = new("w_hi")
        self.w_lo = new("w_lo")
        self.x_in = new("x_in")
        self.res_in = new("res_in")
        self.ctx_in = new("ctx_in")
        self.gate_in = new("gate_in")
        self.fill0 = new("fill0")
        self.fill1 = new("fill1")
        self.x_out = new("x_out")
        self.two_waits = new("two_waits")
        self.stats = new("stats")
        self.ln_var = new("ln_var")
        self.rstd = new("rstd")
        self.xn_ready = new("xn_ready")
        self.cstats = new("cstats")
        self.cvar = new("cvar")
        self.crstd = new("crstd")
        self.cn_ready = new("cn_ready")
        self.ctx_full, self.ctx_free = new("ctx_full"), new("ctx_free")
        self.x_full, self.x_free = new("x_full"), new("x_free")
        self.f_full, self.f_free = new("f_full"), new("f_free")
        self.v_full, self.v_free = new("v_full"), new("v_free")
        self.y_full, self.y_free = new("y_full"), new("y_free")
        self.xm_ready = new("xm_ready")
        self.xm_hi = new("xm_hi")
        self.xm_lo = new("xm_lo")
        self.cx_hi = new("cx_hi")
        self.f_cos = new("f_cos")
        self.f_sin = new("f_sin")
        self.f_flat = new("f_flat")
        self.f_hi = new("f_hi")
        self.f_lo = new("f_lo")
        self.max_full = new("max_full")
        self.max_free = new("max_free")
        self.m_rows = new("m_rows")
        self.m_top = new("m_top")
        self.m_ready = new("m_ready")
        self.shift_full = new("shift_full")
        self.shift_free = new("shift_free")
        self.s_full = new("s_full")
        self.s_free = new("s_free")
        self.av_done = new("av_done")
        self.e_sum = new("e_sum")
        self.sum_done = new("sum_done")
        self.a_rec = new("a_rec")
        self.a_flat = new("a_flat")
        self.a_hi = new("a_hi")
        self.a_lo = new("a_lo")
        self.up_full = new("up_full")
        self.g_flat = new("g_flat")
        self.g_hi = new("g_hi")
        self.g_lo = new("g_lo")
        self.down_done = new("down_done")
        self.y_mid = new("y_mid")
        self.y_gate = new("y_gate")
        self.y_ready = new("y_ready")

    def plan(self, **per):
        for tally in self.all.values():
            tally.per = 0
        for name, n in per.items():
            self.all[name].per = n

    def close(self, once, rounds):
        for name, tally in self.all.items():
            tally.base += tally.per * (1 if name in once else rounds)
            tally.per = 0


ONCE = tuple(f"w_raw{i}" for i in range(SLOTS)) + ("w_hi", "w_lo", "c_in", "const")


def f32(ap):
    return ap.bitcast(F32)


def three_passes(pe, out, w_hi, w_lo, x_hi, x_lo, first, last):
    pe.matmul(out, w_hi, x_hi, start=first, stop=False)
    pe.matmul(out, w_hi, x_lo, start=False, stop=False)
    return pe.matmul(out, w_lo, x_hi, start=False, stop=last)



def weight_chunks(w, cols, hi, lo):
    raw = w.rearrange("(k p) n -> p k n", p=P)[:, :, cols]
    rows, wide = raw.shape[1], raw.shape[2]
    n = min(CHUNK, wide)
    step = CHUNK // n
    return [tuple(x[:, k:k + step, c:c + n] for x in (raw, hi, lo)) for k in range(0, rows, step) for c in range(0, wide, n)]


def staged(stage, chunks, i):
    return stage[i % len(stage)].rearrange("p (k n) -> p k n", k=chunks[i][0].shape[1])


def weights_sync(sp, s, chunks, stage):
    n = len(stage)
    for i, (raw, _, _) in enumerate(chunks):
        if i >= n:
            sp.wait_ge(s.w_lo.sem, s.w_lo.at(0, i - n + 1))
        sp.dma_start(staged(stage, chunks, i), raw).then_inc(s.w_raw[i % n].sem, 16)


def weight_scalar(act, s, chunks, stage, i):
    n = len(stage)
    act.wait_ge(s.w_raw[i % n].sem, s.w_raw[i % n].at(0, 16 * (i // n + 1)))
    act.activation(chunks[i][1], staged(stage, chunks, i), ACT.Copy).then_inc(s.w_hi.sem, 1)


def weight_vector(dve, s, chunks, stage, i):
    _, hi, lo = chunks[i]
    dve.wait_ge(s.w_hi.sem, s.w_hi.at(0, i + 1))
    dve.tensor_tensor(lo, staged(stage, chunks, i), f32(hi), ALU.subtract).then_inc(s.w_lo.sem, 1)


def weights_plan(chunks, stage):
    c, n = len(chunks), len(stage)
    return dict(w_hi=c, w_lo=c, **{f"w_raw{i}": 16 * len(range(i, c, n)) for i in range(n)})



def modulation(nc, s, t, io):
    chunks = []
    for w in (io["ln1_w"], io["ln2_w"], io["ln3_w"], io["W_mod"]):
        wv = w.rearrange("(k p) n -> p k n", p=P)
        chunks += [wv[:, :, c:c + D] for c in range(0, w.shape[1], D)]
    NV = len(chunks)
    with ExitStack() as ctx:
        def sb(name, shape, dt=F32):
            return ctx.enter_context(nc.sbuf_tensor(name, shape, dt))
        raw = sb("mod_raw", [P, 2, KT, D])
        cond = sb("cond", [P, 2, KT, B])
        rows = sb("mod_rows_sb", [B, NV, D])
        bias = sb("mod_bias", [B, NV, D])
        ps_rows = ctx.enter_context(nc.psum_tensor("ps_rows", [B, 2, D], F32))
        ps_vec = ctx.enter_context(nc.psum_tensor("ps_vec", [P, NV, KT, B], F32))
        s.plan(m_raw0=16 * NV // 2, m_raw1=16 * NV // 2, c_in=32 + 16 * 4, tr_full=NV, tr_free=NV, mod_rows=1,
             const=CONSTS, c_silu=1, gates_out=32)
        block = ctx.enter_context(nc.Block())

        @block.sync
        def _(sp):
            sp.dma_start(cond[:, 0], io["condT"].rearrange("(k p) b -> p k b", p=P)).then_inc(s.c_in.sem, 16)
            sp.dma_start(cond[:, 1], io["condT"].rearrange("(k p) b -> p k b", p=P)).then_inc(s.c_in.sem, 16)
            at = 0
            for name in ("ln1_b", "ln2_b", "ln3_b", "b_mod"):
                n = io[name].shape[0] // D
                sp.dma_start(bias[:, at:at + n, :].rearrange("p a d -> p (a d)"),
                             io[name].partition_broadcast(B)).then_inc(s.c_in.sem, 16)
                at += n
            for i, w in enumerate(chunks):
                if i >= 2:
                    sp.wait_ge(s.tr_full.sem, s.tr_full.at(0, i - 1))
                sp.dma_start(raw[:, i % 2], w).then_inc((s.m_raw0, s.m_raw1)[i % 2].sem, 16)
            sp.wait_ge(s.tr_free.sem, s.tr_free.at(0, NV))
            for g, v in enumerate((8, 11)):
                sp.dma_start(io["gates"][g], rows[:, v, :]).then_inc(s.gates_out.sem, 8 * 2)
            sp.wait_ge(s.gates_out.sem, s.gates_out.at(0, 32))

        @block.scalar
        def _(act):
            act.wait_ge(s.c_in.sem, s.c_in.at(0, 96))
            act.activation(cond[:, 1], cond[:, 1], ACT.Silu).then_inc(s.c_silu.sem, 1)

        @block.tensor
        def _(pe):
            pe.wait_ge(s.c_in.sem, s.c_in.at(0, 96))
            pe.wait_ge(s.c_silu.sem, s.c_silu.at(0, 1))
            for i in range(NV):
                pe.wait_ge((s.m_raw0, s.m_raw1)[i % 2].sem, (s.m_raw0, s.m_raw1)[i % 2].at(0, 16 * (i // 2 + 1)))
                if i >= 2:
                    pe.wait_ge(s.tr_free.sem, s.tr_free.at(0, i - 1))
                for k in range(KT):
                    mm = pe.matmul(ps_rows[:, i % 2, :], cond[:, int(i >= 6), k, :], raw[:, i % 2, k, :],
                                   start=(k == 0), stop=(k == KT - 1))
                mm.then_inc(s.tr_full.sem, 1)
            pe.wait_ge(s.tr_free.sem, s.tr_free.at(0, NV))
            pe.wait_ge(s.const.sem, s.const.at(0, CONSTS))
            for v in range(NV):
                for k in range(KT):
                    mm = pe.transpose(ps_vec[:, v, k, :], rows[:, v, k * P:(k + 1) * P], t.ident[0:B, 0:B])
            mm.then_inc(s.mod_rows.sem, 1)

        @block.vector
        def _(dve):
            dve.wait_ge(s.c_in.sem, s.c_in.at(0, 96))
            for i in range(NV):
                dve.wait_ge(s.tr_full.sem, s.tr_full.at(0, i + 1))
                dve.tensor_tensor(rows[:, i, :], ps_rows[:, i % 2, :], bias[:, i, :], ALU.add).then_inc(s.tr_free.sem, 1)
            dve.wait_ge(s.mod_rows.sem, s.mod_rows.at(0, 1))
            for ln, sc, sh in ((0, 0, 1), (1, 2, 3), (2, 4, 5), (3, 7, 6), (5, 10, 9)):
                dve.tensor_scalar(t.mod[:, ln, 0], ps_vec[:, sc], 1.0, None, ALU.add)
                dve.tensor_copy(t.mod[:, ln, 1], ps_vec[:, sh])
            dve.memset(t.mod[:, 4, 0], 1.0)
            dve.memset(t.mod[:, 4, 1], 0.0)
            dve.drain()

        @block.gpsimd
        def _(pool):
            constants(pool, s, t)
    s.close((), 1)


CONSTS = 8


def constants(pool, s, t):
    pool.memset(t.ident[:], 0.0).then_inc(s.const.sem, 1)
    pool.wait_ge(s.const.sem, s.const.at(0, 1))
    pool.affine_select(out=t.ident[:], in_=t.ident[:], compare_op=ALU.not_equal, fill=1.0, base=0,
                       pattern=[[-1, P]], channel_multiplier=1).then_inc(s.const.sem, 1)
    pool.memset(t.ones[:], 1.0).then_inc(s.const.sem, 1)
    pool.memset(t.neghalf[:], -0.5).then_inc(s.const.sem, 1)
    pool.memset(t.eps[:, 0], 1e-5).then_inc(s.const.sem, 1)
    pool.memset(t.eps[:, 1], 1e-6).then_inc(s.const.sem, 1)
    pool.wait_ge(s.const.sem, s.const.at(0, 6))
    pool.tensor_copy(t.ident_bf[:], t.ident[:]).then_inc(s.const.sem, 1)
    pool.wait_ge(s.const.sem, s.const.at(0, 7))
    pool.memset(t.pad[:], 0.0).then_inc(s.const.sem, 1)



def ln_vector_stats(dve, s, rnd, x, st, mv, tiles, pad, stats, var):
    for i in range(tiles):
        dve.bn_stats(st[:, i, :], x[:, i, :]).then_inc(stats.sem, 1)
    dve.wait_ge(stats.sem, stats.at(rnd, tiles))
    dve.tensor_copy(pad[:, 0:1], pad[:, 1:2])
    for i in range(tiles):
        dve.bn_aggr(mv[:, i, :], st[:, i, :]).then_inc(var.sem, 1)


def ln_pool_rstd(pool, s, rnd, mv, rs, eps, nh, tiles, var, rstd):
    pool.wait_ge(var.sem, var.at(rnd, tiles))
    pool.wait_ge(rstd.sem, rstd.at(rnd, 0))
    pool.tensor_tensor(rs[:, 0, :], mv[:, :, 1], eps, ALU.add).then_inc(rstd.sem, 1)
    pool.wait_ge(rstd.sem, rstd.at(rnd, 1))
    pool.tensor_tensor(rs[:, 1, :], rs[:, 0, :], nh, ALU.pow).then_inc(rstd.sem, 1)


def ln_vector_apply(dve, s, rnd, x, mv, rs, tiles, rstd, ready):
    dve.wait_ge(rstd.sem, rstd.at(rnd, 2))
    for i in range(tiles):
        dve.tensor_scalar(x[:, i, :], x[:, i, :], mv[:, i, 0:1], rs[:, 1, i:i + 1],
                          ALU.subtract, ALU.mult).then_inc(ready.sem, 1)



def weave(main, fill):
    out, n = [], 0
    for i, e in enumerate(main):
        out.append(e)
        while n < len(fill) * (i + 1) // len(main):
            out.append(fill[n])
            n += 1
    return out


class Attention:

    def __init__(self, cross, layer):
        self.cross, self.layer = cross, layer
        self.keys = NC if cross else N
        self.kp = 125 if cross else TP
        self.tiles = self.keys // self.kp
        self.pairs = self.tiles // 2
        self.kcols = [(0, 376), (376, 750)] if cross else [(0, N)]
        self.fu = len(self.kcols) + 1
        self.mu = HG * (4 if cross else 1)
        self.gs = 1 if cross else 2
        self.fills = NG // self.gs // 2
        self.rope = layer == 0
        self.per_kind = dict(ctx=8 * cross, x=2, f=NG * self.fu, v=self.tiles, y=TT)

        body = [(1, ("load",))] + [w for g in range(NG) for w in self.step(g)] + [(0, ("y", i)) for i in range(TT)]
        self.prologue = self.ring(self.prepare(), [None, None])
        self.rest = self.tail
        before = [(db - 1, e) for db, e in [w for w in body if w[1][0] in self.per_kind][-2:]]
        self.body = self.ring(body, before)
        self.last = self.ring([w for w in body if w[0] == 0], before)

    def nth(self, e):
        return e[1] * self.fu + e[2] if e[0] == "f" else e[1]

    def ring(self, events, before):
        used, out = list(before), []
        for db, e in events:
            if e[0] in self.per_kind:
                if e[0] not in ("f", "v") or e[-1] == 0:
                    used.append((db, e))
                out.append((db, e, len(used) % 2, used[-3]))
            else:
                out.append((db, e, None, None))
        self.tail = used[-2:]
        assert len(used) % 2 == 0
        return out

    def f(self, g, u):
        return [("f", g, u, k) for k in range(KT)]

    def v(self, *tiles):
        return [("v", i, k) for i in tiles for k in range(KT)]

    def prepare(self):
        m = [("m", 0, u) for u in range(self.mu)]
        half = self.mu // 2
        out = [("cln",)] * self.cross + [("ctx", i) for i in range(8 if self.cross else 0)]
        out += [("ln",)] + [("x", i) for i in range(2)]

        def group(g):
            fs = [self.f(g, u) for u in range(self.fu)]
            hs = [[("h", g, u)] for u in range(self.fu)]
            if self.cross:
                return fs[0] + fs[1] + hs[0] + hs[1] + fs[2] + hs[2]
            return fs[0] + fs[1] + hs[0] + hs[1]
        w = [("w", i) for i in range(8)]
        if self.cross:
            out = out[:5] + w[:1] + out[5:9] + w[1:2] + out[9:11] + w[2:3] + out[11:] + w[3:4]
        else:
            out = out[:1] + w[:1] + out[1:2] + w[1:2] + out[2:] + w[2:4]
        if self.cross:
            out += group(0) + w[4:6] + self.v(0, 1, 2) + group(1)
            out += weave(m[:half], self.v(3, 4)) + w[6:] + [("t", 0, 0)] + weave(m[half:], self.v(5) + self.f(2, 0) + self.f(2, 1))
            return [(0, e) for e in out + [("t", 0, 1)]]
        else:
            out += group(0) + w[4:6] + group(1) + self.v(0, 1) + group(2) + group(3)
        return [(0, e) for e in out + m[:half] + w[6:] + [("t", 0, 0)] + m[half:] + [("t", 0, 1)]]

    def step(self, g):
        def mark(events, ahead=0):
            return [(ahead, e) for e in events]

        mg, md = (g + 1) % NG, (g + 1) // NG
        m = mark([("m", mg, u) for u in range(self.mu)], md)
        t0 = mark([("t", mg, 0)], md)
        t1 = mark([("t", mg, 1)], md)
        s = [mark([("s", g, c, j) for j in range(HG)]) for c in range(self.pairs)]
        e = mark([("e", g, c) for c in range(self.pairs)])
        v = mark([("a", g, c) for c in range(self.pairs)])
        o, d = mark([("o", g)]), mark([("d", g)])
        if not self.cross:
            ln, x = mark([("ln",)], 1), mark([("x", 0), ("x", 1)], 1)
            fh = [mark(self.f(i, 0) + self.f(i, 1), 1) for i in range(NG)]
            h = [mark([("h", i, 0), ("h", i, 1)], 1) for i in range(NG)]
            late = mark([("o", g - 1)]) if g else []
            later = mark([("d", g - 1)]) if g else []
            a, b = s[0][:2] + late + m[:1] + s[0][2:], m[1:2] + later + t0 + m[2:] + v
            if g == 0:
                return ln + s[0][:2] + m[:1] + s[0][2:] + m[1:2] + x[:1] + t0 + m[2:] + x[1:] + v + t1
            if g == 1:
                return weave(a, fh[0]) + h[0] + weave(b, fh[1]) + h[1] + t1
            if g == 2:
                return weave(a, fh[2][:4]) + weave(b[:-1], fh[2][4:]) + h[2] + b[-1:] + t1
            vs = mark(self.v(0, 1), 1)
            return weave(a, fh[3][:4]) + weave(b[:-1], fh[3][4:]) + h[3] + b[-1:] + vs[:2] + t1 + o + vs[2:6] + d + vs[6:]
        kg, kd = (g + 3) % NG, (g + 3) // NG
        fg, fd = (g + 2) % NG, (g + 2) // NG
        fk = mark(self.f(kg, 0) + self.f(kg, 1), kd)
        fq = mark(self.f(fg, 2), fd)
        h = [mark([("h", fg, u)], fd) for u in range(3)]
        late = mark([("o", g - 1)]) if g else []
        later = mark([("d", g - 1)]) if g else []
        ctx = mark([("ctx", i) for i in range(8)], 1)
        ln, x = mark([("ln",)], 1), mark([("x", 0), ("x", 1)], 1)
        out = s[0][:2] + fq[:1] + s[0][2:3] + late + s[0][3:] + fq[1:2] + s[1][:2] + e[:1] + fq[2:3] + s[1][2:] + h[0] + v[:1] + m[:1] + h[1]
        head = s[2][:2] + fq[3:] + s[2][2:] + later
        if g == 1:
            out += ln + head + m[1:2] + h[2] + e[1:2] + weave(m[2:4], ctx[:4]) + v[1:2] + x[:1] + weave(m[4:8], ctx[4:]) + x[1:] + v[2:] + t0
            return out + weave(m[8:], fk[:5]) + fk[5:] + t1
        out += head + m[1:2] + h[2] + e[1:2] + m[2:3] + v[1:2] + m[3:5] + v[2:] + m[5:6] + weave(m[6:8], fk[:2]) + t0
        if g == 3:
            vs = mark(self.v(*range(6)), 1)
            out += weave(m[8:12], fk[2:]) + weave(m[12:], vs[:4]) + vs[4:5] + o + vs[5:6] + t1
            return out + vs[6:14] + d + vs[14:]
        return out + weave(m[8:], fk[2:6]) + fk[6:] + t1 + mark([("cln",)] * (g == 0), 1)


def attention_phase(nc, s, t, io, cross, layer, x_src, x_dst):
    a = Attention(cross, layer)
    ln = 3 * layer + int(cross)
    biased = layer == 1
    pre = "c" if cross else "s"
    with ExitStack() as ctx:
        def sb(name, shape, dt=F32):
            return ctx.enter_context(nc.sbuf_tensor(f"{pre}{layer}_{name}", shape, dt))

        def psum(name, shape):
            return ctx.enter_context(nc.psum_tensor(f"{pre}{layer}_ps_{name}", shape, F32))

        order = ("wk", "wq", "wv", "wo")
        W = {n: (sb(n + "_hi", [P, KT, D], F32R), sb(n + "_lo", [P, KT, D], F32R)) for n in order}
        chunks = []
        for n in order:
            if cross or n == "wo":
                src, at = io[f"{pre}{layer}_{n}"], 0
            else:
                src, at = io[f"s{layer}_qkv"], D * ("wq", "wk", "wv").index(n)
            chunks += weight_chunks(src, slice(at, at + D), *W[n])
        craw_all = sb("craw", [P, 6, D]) if cross else None

        xa = sb("xa", [TP, TT, D])
        res = sb("res", [TP, TT, D])
        stt, mv, rs = sb("st", [P, 8, 6]), sb("mv", [P, 8, 2]), sb("rs", [P, 2, 8])
        xm = sb("xm", [P, 2, N])
        xh, xl = sb("xh", [P, KT, N], F32R), sb("xl", [P, KT, N], F32R)
        if cross:
            craw = craw_all[0:125]
            cst, cmv, crs = sb("cst", [125, 6, 6]), sb("cmv", [125, 6, 2]), sb("crs", [125, 2, 6])
            ch, cl = sb("ch", [P, KT, NC], F32R), sb("cl", [P, KT, NC], F32R)
            src = sb("src", [P, 2, NC + N], F32R)
            stk = sb("stk", [P, 2, HG, NC + N], F32R)
        else:
            src = sb("src", [P, 2, 4, 2, N], F32R)
            st2 = sb("st2", [P, 2, 2, HG, 2, N], F32R)
        kvh, kvl = (ch, cl) if cross else (xh, xl)
        wid = 376 if cross else N
        fa, fs = sb("fa", [P, 2, wid]), sb("fs", [P, 2, wid]) if a.rope else None
        if a.rope:
            cos, sin = sb("cos", [P, a.keys]), sb("sin", [P, a.keys])
        vt_all = sb("vt", [P, a.tiles, D])
        vt = vt_all[0:a.kp]
        mx, mhl = sb("mx", [TP, HG, TT]), sb("mhl", [TP, HG, TT, 2], BF16)
        mx2 = sb("mx2", [TP, HG, TT, 2]) if cross else None
        pt_all = sb("pt", [P, 2 * HG * 2 * N])
        pt = pt_all[0:a.kp].rearrange("p (s h k n) -> p s h k n", s=2, h=HG, k=2)
        es = sb("es", [a.kp, HG, N]) if cross else None
        spare = (vt_all if cross else sb("raw", [P, 6, D])).rearrange("p (c a) d -> p c (a d)", a=2)
        stage = [pt_all[:, i * CHUNK:(i + 1) * CHUNK] for i in range(3)] + [spare[:, i, :] for i in range(3)]
        rec, af = sb("rec", [P, N]), sb("af", [P, N])
        ah, al = sb("ah", [P, NG, N], F32R), sb("al", [P, NG, N], F32R)
        if biased:
            ym = sb("ym", [TP, D])
            bq, bk = sb("bq", [P, KT]), sb("bk", [P, KT])
            bv, bo = sb("bv", [P, D]), sb("bo", [P, D])
            gate = sb("gate", [TP, D]) if not cross else None

        wk = psum("wk", [P, 2, 512])
        ps_max = psum("max", [P, 2, 512])
        ps_s = psum("s", [P, 2, 512])
        ps_o = psum("o", [P, 512])
        ps_shift = psum("shift", [P, 512])

        def kstack(g, j, rows, c0, c1):
            if cross:
                return stk[0:rows, g % 2, j, c0:c1]
            return st2[0:rows, g // 2, 0, j, g % 2, c0:c1]

        def qstack(g, j, rows, c0, c1):
            if cross:
                return stk[0:rows, g % 2, j, NC + c0:NC + c1]
            return st2[0:rows, g // 2, 1, j, g % 2, c0:c1]

        e_per = max(2 * a.pairs - 3, 0)

        def e_count(cs):
            g, c = divmod(cs, a.pairs)
            return g * e_per + (2 * c - 1 if c > 0 else 0)

        def sum_pair(eng, r, g, c):
            cs = g * a.pairs + c
            eng.wait_ge(s.s_free.sem, s.s_free.at(r, (cs + 1) * HG))
            tile = [pt[:, cs % 2, :, k, :] for k in range(2)]
            if c == 0:
                eng.wait_ge(s.sum_done.sem, s.sum_done.at(r, g))
                eng.tensor_tensor(es[:], tile[0], tile[1], ALU.add).then_inc(s.e_sum.sem, 1)
            else:
                for k in range(2):
                    eng.wait_ge(s.e_sum.sem, s.e_sum.at(r, e_count(cs) + k))
                    eng.tensor_tensor(es[:], es[:], tile[k], ALU.add).then_inc(s.e_sum.sem, 1)

        def f_width(u):
            return a.kcols[u][1] - a.kcols[u][0] if u < len(a.kcols) else N

        def f_dst(g, u, half):
            isq = u == a.fu - 1
            if not cross:
                return src[:, g // 2, 2 * isq + half, g % 2, :]
            return src[:, half, NC:] if isq else src[:, 1 - half, a.kcols[u][0]:a.kcols[u][1]]

        dmas = 16 if cross else 12
        nf = NG * a.fu
        gated = biased and not cross
        cn = biased and cross
        ncin = 2 * a.rope + 4 * biased
        s.plan(**weights_plan(chunks, stage), x_in=16, res_in=16, ctx_in=16 * cross, gate_in=16 * gated,
             fill0=16 * dmas * a.fills, fill1=16 * dmas * a.fills, x_out=16,
             ctx_full=a.per_kind["ctx"], ctx_free=a.per_kind["ctx"], x_full=2, x_free=2,
             f_full=nf, f_free=nf, v_full=a.tiles, v_free=a.tiles, y_full=TT, y_free=TT, max_full=NG * a.mu, max_free=NG * a.mu,
             s_full=NG * HG * a.pairs, s_free=NG * HG * a.pairs, shift_full=NG * 2, shift_free=NG * 2,
             av_done=NG * a.pairs, sum_done=NG, stats=TT, ln_var=TT, rstd=2, xn_ready=TT,
             cstats=6 * cn, cvar=6 * cn, crstd=2 * cn, cn_ready=6 * cn,
             xm_ready=KT // 2, xm_hi=KT, xm_lo=KT, cx_hi=8 * cross,
             f_cos=nf * a.rope, f_sin=nf * a.rope, f_flat=nf * a.rope, f_hi=nf, f_lo=nf,
             m_top=2 * NG, m_ready=2 * NG, m_rows=2 * NG * cross, e_sum=NG * e_per,
             a_rec=NG, a_flat=NG, a_hi=NG, a_lo=NG, y_mid=TT * biased, y_gate=TT * gated,
             c_in=16 * ncin, const=2)
        full = dict(ctx=s.ctx_full, x=s.x_full, f=s.f_full, v=s.v_full, y=s.y_full)
        free = dict(ctx=s.ctx_free, x=s.x_free, f=s.f_free, v=s.v_free, y=s.y_free)
        block = ctx.enter_context(nc.Block())
        xv = x_src.rearrange("b (t p) d -> b p t d", p=TP)
        yv = x_dst.rearrange("b (t p) d -> b p t d", p=TP)

        @block.sync
        def _(sp):
            def load(r, at, first):
                if first:
                    sp.dma_start(xa[:], xv[at]).then_inc(s.x_in.sem, 16)
                if cross:
                    sp.wait_ge(s.ctx_full.sem, s.ctx_full.at(r, 0))
                    sp.dma_start(craw[:], io["ctx"][at].rearrange("(t p) d -> p t d", p=125)).then_inc(s.ctx_in.sem, 16)

            def refill(r, i):
                if cross:
                    done = s.s_full.at(r, (i - 1) * HG * a.pairs)
                    sp.wait_ge(s.f_lo.sem, s.f_lo.at(r, a.nth(("f", i, 1)) + 1))
                    sp.sem_inc(s.two_waits.sem, 1)
                    sp.wait_ge(s.s_full.sem, done)
                    sem = (s.fill0, s.fill1)[i % 2].sem
                    rows = [slice(HD * j, HD * (j + 1)) for j in range(HG)]
                    for j in range(HG):
                        sp.dma_start(f32(stk[0:HD, i % 2, j, 0:NC]), f32(src[rows[j], 1, 0:NC])).then_inc(sem, 16)
                    sp.wait_ge(s.f_lo.sem, s.f_lo.at(r, a.nth(("f", i, 2)) + 1))
                    for j in range(HG):
                        sp.dma_start(f32(stk[HD:2 * HD, i % 2, j, :]), f32(src[rows[j], 1, :])).then_inc(sem, 16)
                        sp.dma_start(f32(stk[2 * HD:STACK, i % 2, j, :]), f32(src[rows[j], 0, :])).then_inc(sem, 16)
                        sp.dma_start(f32(stk[0:HD, i % 2, j, NC:]), f32(src[rows[j], 0, NC:])).then_inc(sem, 16)
                else:
                    sp.wait_ge(s.f_lo.sem, s.f_lo.at(r, a.nth(("f", 2 * i + 1, 1)) + 1))
                    sp.sem_inc(s.two_waits.sem, 1)
                    sp.wait_ge(s.s_full.sem, s.s_full.at(r, (2 * i - 2) * HG * a.pairs))
                    sem = (s.fill0, s.fill1)[i].sem
                    for j in range(HG):
                        own = slice(HD * j, HD * (j + 1))
                        for row, kind in ((0, slice(0, 4, 2)), (1, slice(0, 4, 3)), (2, slice(1, 3, 1))):
                            to = slice(HD * row, HD * (row + 1))
                            sp.dma_start(f32(st2[to, i, :, j].rearrange("p a g n -> p a (g n)")),
                                         f32(src[own, i, kind].rearrange("p a g n -> p a (g n)"))).then_inc(sem, 16)

            def batch(b, more):
                if more:
                    load((b, 1), b + 1, False)
                if gated:
                    sp.wait_ge(s.y_gate.sem, s.y_gate.at(b, 0))
                    sp.dma_start(gate[:], io["gates"][0, b].partition_broadcast(TP)).then_inc(s.gate_in.sem, 16)
                sp.wait_ge(s.x_out.sem, s.x_out.at(b, 0))
                sp.dma_start(res[:], xv[b]).then_inc(s.res_in.sem, 16)
                if cross:
                    refill(b, 2)
                    refill(b, 3)
                if more:
                    refill((b, 1), 0)
                    refill((b, 1), 1)
                sp.wait_ge(s.y_free.sem, s.y_free.at(b, TT))
                sp.dma_start(yv[b], res[:]).then_inc(s.x_out.sem, 16)

            load(0, 0, True)
            if a.rope:
                sp.dma_start(cos[:], io["cos"][:, 0:a.keys]).then_inc(s.c_in.sem, 16)
                sp.dma_start(sin[:], io["sin"][:, 0:a.keys]).then_inc(s.c_in.sem, 16)
            if biased:
                for dst, name in ((bq, "bq"), (bk, "bk")):
                    sp.dma_start(dst[:], io[f"{pre}_{name}"]).then_inc(s.c_in.sem, 16)
                for dst, name in ((bv, "bv"), (bo, "bo")):
                    sp.dma_start(dst[:], io[f"{pre}_{name}"].partition_broadcast(P)).then_inc(s.c_in.sem, 16)
            weights_sync(sp, s, chunks, stage)
            refill(0, 0)
            refill(0, 1)
            with sp.Fori(0, B - 1) as b:
                batch(b, True)
            batch(B - 1, False)
            sp.wait_ge(s.x_out.sem, s.x_out.at(B, 0))

        @block.tensor
        def _(pe):
            pe.wait_ge(s.const.sem, s.const.at(0, 2))

            def batch(b, events):
                def scores(r, g, c, j):
                    i = (g * a.pairs + c) * HG + j
                    if c == 0 and j in (0, 2):
                        pe.wait_ge(s.shift_free.sem, s.shift_free.at(r, 2 * g + j // 2 + 1))
                    pe.wait_ge(s.s_free.sem, s.s_free.at(r, i - 1))
                    for k in range(2):
                        kt = 2 * c + k
                        mm = pe.matmul(ps_s[0:a.kp, i % 2, k * N:(k + 1) * N],
                                       kstack(g, j, STACKM, kt * a.kp, (kt + 1) * a.kp),
                                       qstack(g, j, STACKM, 0, N), start=True, stop=True)
                    mm.then_inc(s.s_full.sem, 1)

                def values(r, g, c):
                    i = g * a.pairs + c
                    if c == 0:
                        pe.wait_ge(s.a_flat.sem, s.a_flat.at(r, g))
                    pe.wait_ge(s.s_free.sem, s.s_free.at(r, (i + 1) * HG))
                    for k in range(2):
                        for j in range(HG):
                            kt = 2 * c + k
                            h = g * HG + j
                            mm = pe.matmul(ps_o[HD * j:HD * (j + 1), 0:N], vt[:, kt, HD * h:HD * (h + 1)],
                                           pt[:, i % 2, j, k, :], start=(kt == 0), stop=(kt == a.tiles - 1))
                    mm.then_inc(s.av_done.sem, 1)

                def sums(r, g):
                    cs = (g + 1) * a.pairs - 1
                    pe.wait_ge(s.s_free.sem, s.s_free.at(r, (cs + 1) * HG))
                    if cross:
                        pe.wait_ge(s.e_sum.sem, s.e_sum.at(r, (g + 1) * e_per))
                    for j in range(HG):
                        parts = ([es[:, j, :]] if cross else []) + [pt[:, cs % 2, j, k, :] for k in range(2)]
                        for i, part in enumerate(parts):
                            mm = pe.matmul(ps_o[HD * j:HD * (j + 1), N:2 * N], t.ones[0:a.kp, 0:HD], part,
                                           start=(i == 0), stop=(i == len(parts) - 1))
                    mm.then_inc(s.sum_done.sem, 1)

                def maxima(r, g, u):
                    i = g * a.mu + u
                    slot, fill = (g % 2, g // 2 + 1) if cross else (g // 2, 1)
                    if u == 0:
                        pe.wait_ge((s.fill0, s.fill1)[slot].sem, (s.fill0, s.fill1)[slot].at(r, 16 * dmas * fill))
                    pe.wait_ge(s.max_free.sem, s.max_free.at(r, i - 1))
                    if cross:
                        j, q, c0 = u // 4, u // 2 % 2, (0, NC - 376)[u % 2]
                        mm = pe.matmul(ps_max[0:TP, i % 2, 0:376], qstack(g, j, STACK, q * TP, (q + 1) * TP),
                                       kstack(g, j, STACK, c0, c0 + 376), start=True, stop=True)
                    else:
                        for q in range(TT):
                            mm = pe.matmul(ps_max[0:TP, i % 2, q * N:(q + 1) * N],
                                           qstack(g, u, STACK, q * TP, (q + 1) * TP),
                                           kstack(g, u, STACK, 0, N), start=True, stop=True)
                    mm.then_inc(s.max_full.sem, 1)

                def shifts(r, g, half):
                    pe.wait_ge(s.m_ready.sem, s.m_ready.at(r, 2 * g + half + 1))
                    pe.wait_ge(s.shift_free.sem, s.shift_free.at(r, 2 * g + half))
                    for j in (2 * half, 2 * half + 1):
                        for q in range(TT):
                            c0 = (j % 2) * N + q * TP
                            mm = pe.matmul(ps_shift[STACK:STACKM, c0:c0 + TP], mhl[:, j, q, :],
                                           t.ident_bf[0:TP, 0:TP], start=True, stop=True)
                    mm.then_inc(s.shift_full.sem, 1)

                for db, e, bank, user in events:
                    kind, r = e[0], (b, db)
                    if user is not None and (kind not in ("f", "v") or e[-1] == 0):
                        db0, e0 = user
                        pe.wait_ge(free[e0[0]].sem, free[e0[0]].at((b, db0), a.nth(e0) + 1))
                    to = wk[:, bank, :] if bank is not None else None
                    if events is a.prologue and kind in ("f", "v"):
                        pe.wait_ge(s.w_lo.sem, s.w_lo.at(0, 6 if kind == "v" else 2 if e[2] < a.fu - 1 else 4))
                    if kind == "ctx":
                        k, half = e[1] // 2, e[1] % 2
                        if e[1] == 0:
                            pe.wait_ge(s.cn_ready.sem, s.cn_ready.at(r, 6)) if biased else pe.wait_ge(s.ctx_in.sem, s.ctx_in.at(r, 16))
                        for i in range(3):
                            mm = pe.transpose(to[:, i * 125:(i + 1) * 125], craw[:, 3 * half + i, k * P:(k + 1) * P],
                                              t.ident[0:125, 0:125])
                        mm.then_inc(s.ctx_full.sem, 1)
                    elif kind == "x":
                        if e[1] == 0:
                            pe.wait_ge(s.xn_ready.sem, s.xn_ready.at(r, TT))
                        for k in range(2):
                            for i in range(TT):
                                c0 = k * N + i * TP
                                kk = 2 * e[1] + k
                                mm = pe.transpose(to[:, c0:c0 + TP], xa[:, i, kk * P:(kk + 1) * P],
                                                  t.ident[0:TP, 0:TP])
                        mm.then_inc(s.x_full.sem, 1)
                    elif kind == "f":
                        _, g, u, k = e
                        isq = u == a.fu - 1
                        if k == 0 and (isq or not cross):
                            pe.wait_ge(s.xm_lo.sem, s.xm_lo.at(r, KT))
                        elif k == 0:
                            pe.wait_ge(s.ctx_free.sem, s.ctx_free.at(r, 8))
                        wh, wl = W["wq" if isq else "wk"]
                        c0, c1 = (0, N) if isq else a.kcols[u]
                        sh, sl = (xh, xl) if isq else (kvh, kvl)
                        c = slice(g * P, (g + 1) * P)
                        mm = three_passes(pe, to[:, 0:c1 - c0], wh[:, k, c], wl[:, k, c],
                                          sh[:, k, c0:c1], sl[:, k, c0:c1], k == 0, k == KT - 1)
                        if k == KT - 1:
                            mm.then_inc(s.f_full.sem, 1)
                    elif kind == "v":
                        _, i, k = e
                        if k == 0:
                            pe.wait_ge(s.ctx_free.sem, s.ctx_free.at(r, 8)) if cross else pe.wait_ge(s.xm_lo.sem, s.xm_lo.at(r, KT))
                        wh, wl = W["wv"]
                        c = slice(i * a.kp, (i + 1) * a.kp)
                        mm = three_passes(pe, to[0:a.kp, :], kvh[:, k, c], kvl[:, k, c],
                                          wh[:, k, :], wl[:, k, :], k == 0, k == KT - 1)
                        if k == KT - 1:
                            mm.then_inc(s.v_full.sem, 1)
                    elif kind == "y":
                        i = e[1]
                        pe.wait_ge(s.a_lo.sem, s.a_lo.at(r, NG))
                        wh, wl = W["wo"]
                        for k in range(KT):
                            c = slice(i * TP, (i + 1) * TP)
                            mm = three_passes(pe, to[0:TP, :], ah[:, k, c], al[:, k, c],
                                              wh[:, k, :], wl[:, k, :], k == 0, k == KT - 1)
                        mm.then_inc(s.y_full.sem, 1)
                    elif kind == "s":
                        scores(r, *e[1:])
                    elif kind == "a":
                        if e[1] == 0:
                            pe.wait_ge(s.v_free.sem, s.v_free.at(r, 2 * e[2] + 2))
                        values(r, e[1], e[2])
                    elif kind == "m":
                        maxima(r, e[1], e[2])
                    elif kind == "t":
                        shifts(r, e[1], e[2])
                    elif kind == "o":
                        sums(r, e[1])

            batch(0, a.prologue)
            pe.wait_ge(s.w_lo.sem, s.w_lo.at(0, len(chunks)))
            for db, e in a.rest:
                pe.wait_ge(free[e[0]].sem, free[e[0]].at(0, a.nth(e) + 1))
            with pe.Fori(0, B - 1) as b:
                batch(b, a.body)
            batch(B - 1, a.last)

        @block.vector
        def _(dve):
            def batch(b, events):
                for db, e, bank, user in events:
                    kind, r = e[0], (b, db)
                    if kind in ("ctx", "x", "y") or e[-1] == KT - 1 and (kind == "f" and a.rope or kind == "v" and biased):
                        dve.wait_ge(full[kind].sem, full[kind].at(r, a.nth(e) + 1))
                        fr = wk[:, bank, :]
                    if kind == "w":
                        weight_vector(dve, s, chunks, stage, e[1])
                        if e[1] == 0 and ncin:
                            dve.wait_ge(s.c_in.sem, s.c_in.at(0, 16 * ncin))
                    elif kind == "cln" and biased:
                        dve.wait_ge(s.ctx_in.sem, s.ctx_in.at(r, 16))
                        ln_vector_stats(dve, s, r, craw, cst, cmv, 6, t.pad, s.cstats, s.cvar)
                        ln_vector_apply(dve, s, r, craw, cmv, crs, 6, s.crstd, s.cn_ready)
                    elif kind == "ln":
                        dve.wait_ge(s.x_in.sem, s.x_in.at(r, 16))
                        ln_vector_stats(dve, s, r, xa, stt[0:TP], mv[0:TP], TT, t.pad, s.stats, s.ln_var)
                        ln_vector_apply(dve, s, r, xa, mv[0:TP], rs[0:TP, :, 0:TT], TT, s.rstd, s.xn_ready)
                    elif kind == "ctx":
                        k, half = e[1] // 2, e[1] % 2
                        c = slice(375 * half, 375 * half + 375)
                        dve.wait_ge(s.cx_hi.sem, s.cx_hi.at(r, e[1] + 1))
                        dve.tensor_tensor(cl[:, k, c], fr[:, 0:375], f32(ch[:, k, c]), ALU.subtract).then_inc(s.ctx_free.sem, 1)
                    elif kind == "x":
                        for kk in range(2):
                            k = 2 * e[1] + kk
                            dve.wait_ge(s.xm_lo.sem, s.xm_lo.at(r, k - 1))
                            dve.tensor_scalar(xm[:, k % 2, :], fr[:, kk * N:(kk + 1) * N],
                                                   t.mod[:, ln, 0, k, bass.ds(b + db, 1)], t.mod[:, ln, 1, k, bass.ds(b + db, 1)],
                                                   ALU.mult, ALU.add).then_inc((s.xm_ready, s.x_free)[kk].sem, 1)
                    elif kind == "f" and a.rope and e[-1] == KT - 1:
                        _, g, u, _ = e
                        n = a.nth(e)
                        isq = u == a.fu - 1
                        w = f_width(u)
                        c0 = 0 if isq else a.kcols[u][0]
                        if a.rope:
                            dve.wait_ge(s.f_lo.sem, s.f_lo.at(r, n - 1))
                            dve.tensor_tensor(fa[:, n % 2, 0:w], fr[:, 0:w], cos[:, c0:c0 + w], ALU.mult).then_inc(s.f_cos.sem, 1)
                            dve.stream_shuffle(fs[:, n % 2, 0:w], fr[:, 0:w], SWAP).then_inc(s.f_free.sem, 1)
                    elif kind == "v" and biased and e[-1] == KT - 1:
                        i = e[1]
                        dve.wait_ge(s.av_done.sem, s.av_done.at(r, i // 2 + 1 - a.pairs))
                        dve.tensor_tensor(vt[:, i, :], fr[0:a.kp, :], bv[0:a.kp, :], ALU.add).then_inc(s.v_free.sem, 1)
                    elif kind == "m":
                        _, g, u = e
                        i = g * a.mu + u
                        dve.wait_ge(s.max_full.sem, s.max_full.at(r, i + 1))
                        half, nth = 2 * u // a.mu, 2 * g + 2 * u // a.mu
                        last = (u + 1) % (a.mu // 2) == 0
                        if cross:
                            dve.tensor_reduce(mx2[:, u // 4, u // 2 % 2, u % 2:u % 2 + 1], ps_max[0:TP, i % 2, 0:376], AX.X,
                                              ALU.max).then_inc(s.max_free.sem, 1)
                        else:
                            dve.tensor_reduce(mx[:, u, :], ps_max[0:TP, i % 2, 0:2 * N].rearrange("p (a n) -> p a n", a=2),
                                              AX.X, ALU.max).then_inc(s.max_free.sem, 1)
                        if last:
                            hs = slice(2 * half, 2 * half + 2)
                            dve.wait_ge(s.max_free.sem, s.max_free.at(r, i + 1))
                            if cross:
                                dve.tensor_tensor(mx[:, hs, :], mx2[:, hs, :, 0], mx2[:, hs, :, 1], ALU.max).then_inc(s.m_rows.sem, 1)
                                dve.wait_ge(s.m_rows.sem, s.m_rows.at(r, nth + 1))
                            dve.wait_ge(s.shift_full.sem, s.shift_full.at(r, nth - 1))
                            dve.tensor_copy(mhl[:, hs, :, 0], mx[:, hs, :]).then_inc(s.m_top.sem, 1)
                            dve.wait_ge(s.m_top.sem, s.m_top.at(r, nth + 1))
                            dve.tensor_tensor(mhl[:, hs, :, 1], mx[:, hs, :], mhl[:, hs, :, 0], ALU.subtract).then_inc(s.m_ready.sem, 1)
                    elif kind == "e" and e[2] == 0:
                        sum_pair(dve, r, e[1], e[2])
                    elif kind == "o":
                        g = e[1]
                        dve.wait_ge(s.sum_done.sem, s.sum_done.at(r, g + 1))
                        dve.wait_ge(s.a_lo.sem, s.a_lo.at(r, g))
                        dve.reciprocal(rec[:], ps_o[:, N:2 * N]).then_inc(s.a_rec.sem, 1)
                        dve.wait_ge(s.a_rec.sem, s.a_rec.at(r, g + 1))
                        dve.tensor_tensor(af[:], ps_o[:, 0:N], rec[:], ALU.mult).then_inc(s.a_flat.sem, 1)
                    elif kind == "y":
                        i = e[1]
                        if i == 0:
                            dve.wait_ge(s.res_in.sem, s.res_in.at(r, 16))
                            if gated:
                                dve.wait_ge(s.gate_in.sem, s.gate_in.at(r, 16))
                        y = fr[0:TP, :]
                        if biased:
                            dve.wait_ge(s.y_free.sem, s.y_free.at(r, i))
                            dve.tensor_tensor(ym[:], y, bo[0:TP, :], ALU.add).then_inc(s.y_mid.sem, 1)
                            dve.wait_ge(s.y_mid.sem, s.y_mid.at(r, i + 1))
                            y = ym[:]
                            if gated:
                                dve.tensor_tensor(ym[:], ym[:], gate[:], ALU.mult).then_inc(s.y_gate.sem, 1)
                                dve.wait_ge(s.y_gate.sem, s.y_gate.at(r, i + 1))
                        dve.tensor_tensor(res[:, i, :], res[:, i, :], y, ALU.add).then_inc(s.y_free.sem, 1)

            batch(0, a.prologue)
            with dve.Fori(0, B - 1) as b:
                batch(b, a.body)
            batch(B - 1, a.last)

        @block.scalar
        def _(act):
            def batch(b, events):
                for db, e, bank, user in events:
                    kind, r = e[0], (b, db)
                    if kind == "w":
                        weight_scalar(act, s, chunks, stage, e[1])
                    elif kind == "v" and not biased and e[-1] == KT - 1:
                        i = e[1]
                        act.wait_ge(s.v_full.sem, s.v_full.at(r, i + 1))
                        act.wait_ge(s.av_done.sem, s.av_done.at(r, i // 2 + 1 - a.pairs))
                        act.activation(vt[:, i, :], wk[0:a.kp, bank, :], ACT.Copy).then_inc(s.v_free.sem, 1)
                    elif kind == "f" and not a.rope and e[-1] == KT - 1:
                        _, g, u, _ = e
                        n = a.nth(e)
                        act.wait_ge(s.f_full.sem, s.f_full.at(r, n + 1))
                        act.wait_ge(s.f_lo.sem, s.f_lo.at(r, n - 1))
                        if n == 0:
                            act.wait_ge(s.c_in.sem, s.c_in.at(0, 16 * ncin))
                        act.activation(fa[:, n % 2, 0:f_width(u)], wk[:, bank, 0:f_width(u)], ACT.Identity,
                                       bias=(bq if u == a.fu - 1 else bk)[:, g:g + 1]).then_inc(s.f_free.sem, 1)
                    elif kind == "load":
                        act.wait_ge(s.x_full.sem, s.x_full.at(r, 0))
                        act.dma_start(xa[:], xv[b + db]).then_inc(s.x_in.sem, 16)
                    elif kind == "ctx":
                        k, half = e[1] // 2, e[1] % 2
                        c = slice(375 * half, 375 * half + 375)
                        act.wait_ge(s.ctx_full.sem, s.ctx_full.at(r, e[1] + 1))
                        if e[1] == 0:
                            act.wait_ge(s.f_full.sem, s.f_full.at(r, 0))
                            act.wait_ge(s.v_full.sem, s.v_full.at(r, 0))
                        act.activation(ch[:, k, c], wk[:, bank, 0:375], ACT.Copy).then_inc(s.cx_hi.sem, 1)
                    elif kind == "x":
                        for kk in range(2):
                            k = 2 * e[1] + kk
                            if kk == 0:
                                act.wait_ge(s.xm_ready.sem, s.xm_ready.at(r, e[1] + 1))
                            else:
                                act.wait_ge(s.x_free.sem, s.x_free.at(r, e[1] + 1))
                            act.activation(xh[:, k, :], xm[:, k % 2, :], ACT.Copy).then_inc(s.xm_hi.sem, 1)
                    elif kind == "h":
                        _, g, u = e
                        n = a.nth(("f", g, u))
                        if cross:
                            if u == 0:
                                prev = g - 1 if g else 3
                                filled = (s.fill0, s.fill1)[prev % 2]
                                act.wait_ge(filled.sem, filled.at(r, 16 * dmas * (prev // 2 + 1) - (0 if g else 16 * dmas * a.fills)))
                        elif g % 2 == 0 and u == 0:
                            act.wait_ge((s.fill0, s.fill1)[g // 2].sem, (s.fill0, s.fill1)[g // 2].at(r, 0))
                        act.wait_ge(s.f_flat.sem, s.f_flat.at(r, n + 1)) if a.rope else act.wait_ge(s.f_free.sem, s.f_free.at(r, n + 1))
                        act.activation(f_dst(g, u, 0), fa[:, n % 2, 0:f_width(u)], ACT.Copy).then_inc(s.f_hi.sem, 1)
                    elif kind == "t":
                        _, g, half = e
                        act.wait_ge(s.shift_full.sem, s.shift_full.at(r, 2 * g + half + 1))
                        q = stk[STACK:STACKM, g % 2, 2 * half:2 * half + 2, NC:] if cross else \
                            st2[STACK:STACKM, g // 2, 1, 2 * half:2 * half + 2, g % 2, :]
                        act.activation(q, ps_shift[STACK:STACKM, 0:2 * N].rearrange("p (a n) -> p a n", a=2),
                                       ACT.Copy).then_inc(s.shift_free.sem, 1)
                    elif kind == "s":
                        _, g, c, j = e
                        cs = g * a.pairs + c
                        i = cs * HG + j
                        act.wait_ge(s.s_full.sem, s.s_full.at(r, i + 1))
                        if j == 0:
                            act.wait_ge(s.av_done.sem, s.av_done.at(r, cs - 1))
                            if (cs - 1) % a.pairs == 0:
                                act.wait_ge(s.sum_done.sem, s.sum_done.at(r, (cs - 1) // a.pairs))
                            else:
                                act.wait_ge(s.e_sum.sem, s.e_sum.at(r, e_count(cs - 1)))
                        act.activation(pt[:, cs % 2, j, :, :],
                                       ps_s[0:a.kp, i % 2, 0:2 * N].rearrange("p (a n) -> p a n", a=2),
                                       ACT.Exp, scale=SCALE).then_inc(s.s_free.sem, 1)
                    elif kind == "d":
                        g = e[1]
                        act.wait_ge(s.a_flat.sem, s.a_flat.at(r, g + 1))
                        act.activation(ah[:, g, :], af[:], ACT.Copy).then_inc(s.a_hi.sem, 1)

            batch(0, a.prologue)
            with act.Fori(0, B - 1) as b:
                batch(b, a.body)
            batch(B - 1, a.last)

        @block.gpsimd
        def _(pool):
            stack = stk[STACK:STACKM].rearrange("p a h n -> p (a h n)") if cross else \
                st2[STACK:STACKM, :, 0].rearrange("p a h g n -> p a (h g n)")
            pool.memset(f32(stack), -1.0).then_inc(s.const.sem, 2)
            pool.wait_ge(s.const.sem, s.const.at(0, 2))

            def batch(b, events):
                for db, e, bank, user in events:
                    kind, r = e[0], (b, db)
                    if kind == "cln" and biased:
                        ln_pool_rstd(pool, s, r, cmv, crs, t.eps[0:125, 1, 0:6], t.neghalf[0:125, 0:6], 6, s.cvar, s.crstd)
                    elif kind == "ln":
                        ln_pool_rstd(pool, s, r, mv[0:TP, 0:TT], rs[0:TP, :, 0:TT], t.eps[0:TP, layer, 0:TT],
                                     t.neghalf[0:TP, 0:TT], TT, s.ln_var, s.rstd)
                    elif kind == "x":
                        for kk in range(2):
                            k = 2 * e[1] + kk
                            pool.wait_ge(s.xm_hi.sem, s.xm_hi.at(r, k + 1))
                            pool.tensor_tensor(xl[:, k, :], xm[:, k % 2, :], f32(xh[:, k, :]), ALU.subtract).then_inc(s.xm_lo.sem, 1)
                    elif kind == "f" and a.rope and e[-1] == KT - 1:
                        _, g, u, _ = e
                        n = a.nth(e)
                        w = f_width(u)
                        c0 = 0 if u == a.fu - 1 else a.kcols[u][0]
                        pool.wait_ge(s.f_free.sem, s.f_free.at(r, n + 1))
                        pool.tensor_tensor(fs[:, n % 2, 0:w], fs[:, n % 2, 0:w], sin[:, c0:c0 + w], ALU.mult).then_inc(s.f_sin.sem, 1)
                        pool.wait_ge(s.f_sin.sem, s.f_sin.at(r, n + 1))
                        pool.tensor_tensor(fa[:, n % 2, 0:w], fa[:, n % 2, 0:w], fs[:, n % 2, 0:w], ALU.add).then_inc(s.f_flat.sem, 1)
                    elif kind == "h":
                        _, g, u = e
                        n = a.nth(("f", g, u))
                        pool.wait_ge(s.f_hi.sem, s.f_hi.at(r, n + 1))
                        pool.tensor_tensor(f_dst(g, u, 1), fa[:, n % 2, 0:f_width(u)], f32(f_dst(g, u, 0)), ALU.subtract).then_inc(s.f_lo.sem, 1)
                    elif kind == "e" and e[2] == 1:
                        sum_pair(pool, r, e[1], e[2])
                    elif kind == "d":
                        g = e[1]
                        pool.wait_ge(s.a_hi.sem, s.a_hi.at(r, g + 1))
                        pool.tensor_tensor(al[:, g, :], af[:], f32(ah[:, g, :]), ALU.subtract).then_inc(s.a_lo.sem, 1)

            batch(0, a.prologue)
            with pool.Fori(0, B - 1) as b:
                batch(b, a.body)
            batch(B - 1, a.last)
    s.close(ONCE, B)



def feed_forward(nc, s, t, io, layer, x_src, x_dst):
    ln = 3 * layer + 2
    PB = 2
    T4 = PB * TT
    M = PB * N
    FC = FF // P
    gated = layer == 1
    LAG = 2
    HS = 3
    with ExitStack() as ctx:
        def sb(name, shape, dt=F32):
            return ctx.enter_context(nc.sbuf_tensor(f"f{layer}_{name}", shape, dt))

        w1 = (sb("w1_hi", [P, KT, FF], F32R), sb("w1_lo", [P, KT, FF], F32R))
        w2 = (sb("w2_hi", [P, FC, D], F32R), sb("w2_lo", [P, FC, D], F32R))
        chunks = weight_chunks(io[f"f{layer}_w1"], slice(0, FF), *w1) + weight_chunks(io[f"f{layer}_w2"], slice(0, D), *w2)
        n1 = len(chunks) // 2
        raw = sb("raw", [P, 4, CHUNK])
        stage = [raw[:, i, :] for i in range(4)]
        xa, res = sb("xa", [TP, T4, D]), sb("res", [TP, T4, D])
        stt, mv, rs = sb("st", [TP, T4, 6]), sb("mv", [TP, T4, 2]), sb("rs", [TP, 2, T4])
        xm = sb("xm", [P, 2, M])
        xh, xl = sb("xh", [P, KT, M], F32R), sb("xl", [P, KT, M], F32R)
        hf = sb("hf", [P, 2, M])
        hh, hl = sb("hh", [P, HS, M], F32R), sb("hl", [P, HS, M], F32R)
        b1 = sb("b1_col", [P, FC])
        b2 = sb("b2_all", [TP, D])
        ym = sb("ym", [TP, D])
        gate = sb("gate", [TP, PB, D]) if gated else None
        ps_u = ctx.enter_context(nc.psum_tensor(f"f{layer}_u", [P, 3, 512], F32))
        ps_t = ctx.enter_context(nc.psum_tensor(f"f{layer}_t", [P, 512], F32))
        ps_y = ctx.enter_context(nc.psum_tensor(f"f{layer}_y", [P, T4, 512], F32))

        R = B // PB
        s.plan(**weights_plan(chunks, stage), c_in=32, x_in=16, res_in=16, gate_in=16 * PB * gated, x_out=16,
             stats=T4, ln_var=T4, rstd=2, xn_ready=T4, tr_full=KT, xm_ready=KT, tr_free=KT, xm_hi=KT, xm_lo=KT,
             up_full=FC, g_flat=FC, g_hi=FC, g_lo=FC, down_done=FC - 1, y_full=T4, y_mid=T4, y_gate=T4 * gated, y_ready=T4)
        xv = x_src.rearrange("(r b) (t p) d -> r p (b t) d", p=TP, b=PB)
        yv = x_dst.rearrange("(r b) (t p) d -> r p (b t) d", p=TP, b=PB)
        block = ctx.enter_context(nc.Block())

        @block.sync
        def _(sp):
            def load(r, at):
                sp.wait_ge(s.tr_full.sem, s.tr_full.at(r, 0))
                sp.dma_start(xa[:], xv[at]).then_inc(s.x_in.sem, 16)

            def run(r, more):
                if more:
                    load((r, 1), r + 1)
                if gated:
                    sp.wait_ge(s.y_gate.sem, s.y_gate.at(r, 0))
                    for i in range(PB):
                        sp.dma_start(gate[:, i, :], io["gates"][1, PB * r + i].partition_broadcast(TP)).then_inc(s.gate_in.sem, 16)
                sp.wait_ge(s.x_out.sem, s.x_out.at(r, 0))
                sp.dma_start(res[:], xv[r]).then_inc(s.res_in.sem, 16)
                sp.wait_ge(s.y_ready.sem, s.y_ready.at(r, T4))
                sp.dma_start(yv[r], res[:]).then_inc(s.x_out.sem, 16)

            load(0, 0)
            sp.dma_start(b1[:], io[f"f{layer}_b1"]).then_inc(s.c_in.sem, 16)
            sp.dma_start(b2[:], io[f"f{layer}_b2"].partition_broadcast(TP)).then_inc(s.c_in.sem, 16)
            weights_sync(sp, s, chunks, stage)
            run(0, True)
            with sp.Fori(1, R - 1) as r:
                run(r, True)
            run(R - 1, False)
            sp.wait_ge(s.x_out.sem, s.x_out.at(R, 0))

        def events(first, more):
            ahead = [(0, ("ln",))] + [(0, ("x", k)) for k in range(KT)] + [(0, ("w", i)) for i in range(n1)]
            out = ahead if first else []
            for f in range(FC):
                out.append((0, ("u", f)))
                if first and n1 + f < len(chunks):
                    out.append((0, ("w", n1 + f)))
                if f == 8 and more:
                    out.append((1, ("ln",)))
                if LAG <= f < FC - 1:
                    out.append((0, ("d", f - LAG)))
            x = [(1, ("x", k)) for k in range(KT)] if more else []
            out += x[:1] + [(0, ("d", FC - 3))] + x[1:3] + [(0, ("d", FC - 2))] + x[3:] + [(0, ("d", FC - 1)), (0, ("y",))]
            return out

        @block.tensor
        def _(pe):
            def run(r0, first, more):
                for dr, e in events(first, more):
                    kind, r = e[0], (r0, dr)
                    if kind == "x":
                        k = e[1]
                        if k == 0:
                            pe.wait_ge(s.xn_ready.sem, s.xn_ready.at(r, T4))
                        pe.wait_ge(s.tr_free.sem, s.tr_free.at(r, k))
                        for i in range(T4):
                            mm = pe.transpose(ps_t[:, i * TP:(i + 1) * TP], xa[:, i, k * P:(k + 1) * P], t.ident[0:TP, 0:TP])
                        mm.then_inc(s.tr_full.sem, 1)
                    elif kind == "u":
                        f = e[1]
                        if f == 0:
                            if first:
                                pe.wait_ge(s.w_lo.sem, s.w_lo.at(0, n1))
                            pe.wait_ge(s.xm_lo.sem, s.xm_lo.at(r, KT))
                        pe.wait_ge(s.g_flat.sem, s.g_flat.at(r, f - 2 if f else 0))
                        c = slice(f * P, (f + 1) * P)
                        for k in range(KT):
                            mm = three_passes(pe, ps_u[:, f % 3, 0:M], w1[0][:, k, c], w1[1][:, k, c],
                                              xh[:, k, :], xl[:, k, :], k == 0, k == KT - 1)
                        mm.then_inc(s.up_full.sem, 1)
                    elif kind == "d":
                        f = e[1]
                        if first and f % 2 == 0:
                            pe.wait_ge(s.w_lo.sem, s.w_lo.at(0, n1 + f // 2 + 1))
                        pe.wait_ge(s.g_lo.sem, s.g_lo.at(r, f + 1))
                        if f == 0:
                            pe.wait_ge(s.y_ready.sem, s.y_ready.at(r, 0))
                        for i in range(T4):
                            c = slice(i * TP, (i + 1) * TP)
                            mm = three_passes(pe, ps_y[0:TP, i, :], hh[:, f % HS, c], hl[:, f % HS, c],
                                              w2[0][:, f, :], w2[1][:, f, :], f == 0, f == FC - 1)
                            if f == FC - 1:
                                mm.then_inc(s.y_full.sem, 1)
                        if f < FC - 1:
                            mm.then_inc(s.down_done.sem, 1)

            run(0, True, True)
            with pe.Fori(1, R - 1) as r:
                run(r, False, True)
            run(R - 1, False, False)

        @block.vector
        def _(dve):
            def run(r0, first, more):
                for dr, e in events(first, more):
                    kind, r = e[0], (r0, dr)
                    if kind == "w":
                        weight_vector(dve, s, chunks, stage, e[1])
                    elif kind == "ln":
                        dve.wait_ge(s.x_in.sem, s.x_in.at(r, 16))
                        ln_vector_stats(dve, s, r, xa, stt, mv, T4, t.pad, s.stats, s.ln_var)
                        ln_vector_apply(dve, s, r, xa, mv, rs, T4, s.rstd, s.xn_ready)
                    elif kind == "x":
                        k = e[1]
                        dve.wait_ge(s.tr_full.sem, s.tr_full.at(r, k + 1))
                        dve.wait_ge(s.xm_lo.sem, s.xm_lo.at(r, k - 1))
                        for i in range(PB):
                            c = slice(i * N, (i + 1) * N)
                            at = bass.ds((r0 + dr) * PB + i, 1)
                            dve.tensor_scalar(xm[:, k % 2, c], ps_t[:, c], t.mod[:, ln, 0, k, at], t.mod[:, ln, 1, k, at],
                                              ALU.mult, ALU.add).then_inc((s.xm_ready, s.tr_free)[i].sem, 1)
                    elif kind == "u":
                        f = e[1]
                        dve.wait_ge(s.g_hi.sem, s.g_hi.at(r, f + 1))
                        dve.tensor_tensor(hl[:, f % HS, :], hf[:, f % 2, :], f32(hh[:, f % HS, :]), ALU.subtract).then_inc(s.g_lo.sem, 1)
                    elif kind == "y":
                        if first:
                            dve.wait_ge(s.c_in.sem, s.c_in.at(0, 32))
                        dve.wait_ge(s.res_in.sem, s.res_in.at(r, 16))
                        if gated:
                            dve.wait_ge(s.gate_in.sem, s.gate_in.at(r, 16 * PB))
                        for i in range(T4):
                            dve.wait_ge(s.y_full.sem, s.y_full.at(r, i + 1))
                            dve.wait_ge(s.y_ready.sem, s.y_ready.at(r, i))
                            dve.tensor_tensor(ym[:], ps_y[0:TP, i, :], b2[:], ALU.add).then_inc(s.y_mid.sem, 1)
                            dve.wait_ge(s.y_mid.sem, s.y_mid.at(r, i + 1))
                            if gated:
                                dve.tensor_tensor(ym[:], ym[:], gate[:, i // TT, :], ALU.mult).then_inc(s.y_gate.sem, 1)
                                dve.wait_ge(s.y_gate.sem, s.y_gate.at(r, i + 1))
                            dve.tensor_tensor(res[:, i, :], res[:, i, :], ym[:], ALU.add).then_inc(s.y_ready.sem, 1)

            run(0, True, True)
            with dve.Fori(1, R - 1) as r:
                run(r, False, True)
            run(R - 1, False, False)

        @block.scalar
        def _(act):
            def run(r0, first, more):
                for dr, e in events(first, more):
                    kind, r = e[0], (r0, dr)
                    if kind == "w":
                        weight_scalar(act, s, chunks, stage, e[1])
                    elif kind == "x":
                        k = e[1]
                        act.wait_ge(s.tr_free.sem, s.tr_free.at(r, k + 1))
                        act.activation(xh[:, k, :], xm[:, k % 2, :], ACT.Copy).then_inc(s.xm_hi.sem, 1)
                    elif kind == "u":
                        f = e[1]
                        if first and f == 0:
                            act.wait_ge(s.c_in.sem, s.c_in.at(0, 32))
                        act.wait_ge(s.up_full.sem, s.up_full.at(r, f + 1))
                        act.wait_ge(s.g_lo.sem, s.g_lo.at(r, f - 1))
                        act.activation(hf[:, f % 2, :], ps_u[:, f % 3, 0:M], (ACT.Gelu, ACT.Gelu_apprx_tanh)[layer],
                                       bias=b1[:, f:f + 1]).then_inc(s.g_flat.sem, 1)
                        act.wait_ge(s.g_flat.sem, s.g_flat.at(r, f + 1))
                        if f < HS:
                            act.wait_ge(s.y_full.sem, s.y_full.at(r, 0))
                        else:
                            act.wait_ge(s.down_done.sem, s.down_done.at(r, f - HS + 1))
                        act.activation(hh[:, f % HS, :], hf[:, f % 2, :], ACT.Copy).then_inc(s.g_hi.sem, 1)

            run(0, True, True)
            with act.Fori(1, R - 1) as r:
                run(r, False, True)
            run(R - 1, False, False)

        @block.gpsimd
        def _(pool):
            def run(r0, first, more):
                for dr, e in events(first, more):
                    kind, r = e[0], (r0, dr)
                    if kind == "ln":
                        ln_pool_rstd(pool, s, r, mv, rs, t.eps[0:TP, layer, 0:T4], t.neghalf[0:TP, 0:T4], T4, s.ln_var, s.rstd)
                    elif kind == "x":
                        k = e[1]
                        pool.wait_ge(s.xm_hi.sem, s.xm_hi.at(r, k + 1))
                        pool.tensor_tensor(xl[:, k, :], xm[:, k % 2, :], f32(xh[:, k, :]), ALU.subtract).then_inc(s.xm_lo.sem, 1)

            run(0, True, True)
            with pool.Fori(1, R - 1) as r:
                run(r, False, True)
            run(R - 1, False, False)
    s.close(ONCE, R)


class Tables:

    def __init__(self, nc, ctx):
        def sb(name, shape, dt=F32):
            return ctx.enter_context(nc.sbuf_tensor(name, shape, dt))
        self.ident = sb("ident", [P, P])
        self.ident_bf = sb("ident_bf", [P, P], BF16)
        self.ones = sb("ones", [P, HD])
        self.neghalf = sb("neghalf", [P, 8])
        self.eps = sb("eps", [P, 2, 8])
        self.pad = sb("pad", [P, 2])
        self.mod = sb("mod", [P, 6, 2, KT, B])


def build(nc, io):
    with ExitStack() as ctx:
        s = Signals(nc, ctx)
        t = Tables(nc, ctx)
        with nc.Block() as block:
            @block.sync
            def _(sp):
                for x in s.all.values():
                    sp.sem_inc(x.sem, CREDIT)
        modulation(nc, s, t, io)
        x = io["x"]
        for layer in range(2):
            attention_phase(nc, s, t, io, False, layer, x, io["x1"])
            attention_phase(nc, s, t, io, True, layer, io["x1"], io["x2"])
            x = io["x3"] if layer == 0 else io["out"]
            feed_forward(nc, s, t, io, layer, io["x2"], x)


def rope_tables():
    half = HD // 2
    inv = (np.float32(1.0) / np.float32(10000.0) ** (np.arange(half, dtype=np.float32) / np.float32(half))).astype(np.float32)
    ang = (np.arange(NC, dtype=np.float32)[:, None] * inv[None, :]).astype(np.float32)
    c, s = np.cos(ang).T.astype(np.float32), np.sin(ang).T.astype(np.float32)
    return np.tile(np.concatenate([c, c]), (HG, 1)), np.tile(np.concatenate([-s, s]), (HG, 1))


def kernel(**inputs):
    import concourse.bacc as bacc
    from concourse.bass_utils import run_bass_kernel_spmd

    g = {k: np.asarray(v) for k, v in inputs.items()}
    l0 = {k[9:]: v for k, v in g.items() if k.startswith("L0_xcond_")}
    l1 = {k[9:]: v for k, v in g.items() if k.startswith("L1_xcond_")}
    cos, sin = rope_tables()
    arrays = dict(
        x=g["x"], ctx=g["ctx_1024"], condT=g["cond_1024"].T, cos=cos, sin=sin,
        ln1_w=l0["ln1_w"].T, ln2_w=l0["ln2_w"].T, ln3_w=l0["ln3_w"].T, W_mod=l1["W_mod"],
        ln1_b=l0["ln1_b"], ln2_b=l0["ln2_b"], ln3_b=l0["ln3_b"], b_mod=l1["b_mod"],
        s0_qkv=l0["qkv_w"].T, s0_wo=l0["sa_out_w"].T,
        c0_wq=l0["q_w"].T, c0_wk=l0["k_w"].T, c0_wv=l0["v_w"].T, c0_wo=l0["ca_out_w"].T,
        f0_w1=l0["ffn_w1"].T, f0_b1=l0["ffn_b1"], f0_w2=l0["ffn_w2"].T, f0_b2=l0["ffn_b2"],
        s1_qkv=l1["W_qkv"], s1_wo=l1["W_proj"],
        s_bq=l1["b_qkv"][0:D], s_bk=l1["b_qkv"][D:2 * D], s_bv=l1["b_qkv"][2 * D:3 * D], s_bo=l1["b_proj"],
        c1_wq=l1["W_qc"], c1_wk=l1["W_kvc"][:, 0:D], c1_wv=l1["W_kvc"][:, D:2 * D], c1_wo=l1["W_cproj"],
        c_bq=l1["b_qc"], c_bk=l1["b_kvc"][0:D], c_bv=l1["b_kvc"][D:2 * D], c_bo=l1["b_cproj"],
        f1_w1=l1["W_mlp1"], f1_b1=l1["b_mlp1"], f1_w2=l1["W_mlp2"], f1_b2=l1["b_mlp2"],
    )
    for k in ("f0_b1", "f1_b1", "s_bq", "s_bk", "c_bq", "c_bk"):
        arrays[k] = arrays[k].reshape(-1, P).T
    arrays = {k: np.ascontiguousarray(v) for k, v in arrays.items()}
    nc = bacc.Bacc("TRN2", target_bir_lowering=False, num_devices=1)
    io = {k: nc.dram_tensor(k, v.shape, F32, kind="ExternalInput").ap() for k, v in arrays.items()}
    io["out"] = nc.dram_tensor("out", (B, N, D), F32, kind="ExternalOutput").ap()
    for k in ("x1", "x2", "x3"):
        io[k] = nc.dram_tensor(k, (B, N, D), F32, kind="Internal").ap()
    io["gates"] = nc.dram_tensor("gates", (2, B, D), F32, kind="Internal").ap()
    build(nc, io)
    r = run_bass_kernel_spmd(nc, [arrays], core_ids=[0])
    return r.results[0]["out"]
```
